# Optimizing a Trainium2 kernel written in Bass

```python
import numpy as np
import jax
import jax.numpy as jnp

def _softmax(x, axis=-1):
    return jax.nn.softmax(x, axis=axis)

def _gelu(x):
    return jax.nn.gelu(x, approximate=True)

def _silu(x):
    return jax.nn.silu(x)

def _sigmoid(x):
    return jax.nn.sigmoid(x)

def _layernorm(x, axis=-1, eps=1e-05):
    m = jnp.mean(x, axis=axis, keepdims=True)
    v = jnp.var(x, axis=axis, keepdims=True)
    return (x - m) / jnp.sqrt(v + eps)

def _scatter_add(tgt, idx, src, axis=0):
    return tgt.at[idx].add(src)

def _segment_sum(src, seg, n):
    return jax.ops.segment_sum(src, seg, n)
kernel_name = 'mk_xattn_ffn_d1_seqx_r4_39b0d5'

def setup_inputs(seed: int=0):
    np.random.seed(seed)
    _w = jnp.asarray

    def _rec_inputs():
        import jax
        import jax.numpy as jnp
        _rk = jax.random.key(seed)
        x = -0.0002928 + 1 * jax.random.normal(jax.random.fold_in(_rk, 1), (2, 1024, 256), jnp.float32)
        _lenS = 1024 - jax.random.randint(jax.random.fold_in(_rk, 7), (2,), 0, max(1, 1024 // 4) + 1, jnp.int32)
        _lenS2 = 64 - jax.random.randint(jax.random.fold_in(_rk, 8), (2,), 0, max(1, 64 // 4) + 1, jnp.int32)
        _ctx_1024P = jax.random.normal(jax.random.fold_in(_rk, 11), (2, 16, 256), jnp.float32)
        _ctx_1024c = jax.random.dirichlet(jax.random.fold_in(_rk, 511), 0.3 * jnp.ones((16,), jnp.float32), (2, 64))
        _ctx_1024t = jnp.einsum('bsk,bkd->bsd', _ctx_1024c, _ctx_1024P)
        _ctx_1024t = _ctx_1024t * jax.lax.rsqrt(jnp.mean(jnp.square(_ctx_1024t)) + 1e-12) * 0.953939
        ctx_1024 = -1.39393e-06 + 0.999914 * (_ctx_1024t + 0.3 * jax.random.normal(jax.random.fold_in(_rk, 611), (2, 64, 256), jnp.float32))
        fside_BxS2_0 = jax.random.uniform(jax.random.fold_in(_rk, 12), (2, 64), jnp.float32, 0.0, 9)
        return (x, ctx_1024, fside_BxS2_0)
    x, ctx_1024, fside_BxS2_0 = _rec_inputs()

    def _L0_xattn_setup():
        import jax, jax.numpy as jnp
        import numpy as np
        B, N, E, H = (2, 512, 256, 16)
        HD = E // H
        key = jax.random.key(seed)
        ks = jax.random.split(key, 8)
        query = jax.random.normal(ks[0], (B, N, E), dtype=jnp.float32)
        k_in = jax.random.normal(ks[1], (B, N, E), dtype=jnp.float32)
        v_in = jax.random.normal(ks[2], (B, N, E), dtype=jnp.float32)
        key_abundance = jax.random.randint(ks[3], (B, N), 1, 10).astype(jnp.float32)
        in_proj_weight = jax.random.normal(ks[4], (3 * E, HD * H), dtype=jnp.float32) * (1.0 / np.sqrt(E))
        in_proj_bias = jax.random.normal(ks[5], (3 * HD * H,), dtype=jnp.float32) * 0.02
        out_proj_weight = jax.random.normal(ks[6], (E, HD * H), dtype=jnp.float32) * (1.0 / np.sqrt(E))
        out_proj_bias = jax.random.normal(ks[7], (E,), dtype=jnp.float32) * 0.02
        return {'query': query, 'key': k_in, 'value': v_in, 'key_abundance': key_abundance, 'in_proj_weight': in_proj_weight, 'in_proj_bias': in_proj_bias, 'out_proj_weight': out_proj_weight, 'out_proj_bias': out_proj_bias, 'num_heads': H}
    _L0_xattn_all = _L0_xattn_setup()
    _L0_xattn_in = {k: v for k, v in _L0_xattn_all.items() if k in ('in_proj_weight', 'in_proj_bias', 'out_proj_weight', 'out_proj_bias')}
    del _L0_xattn_all

    def _L0_ffn_setup():
        import jax, jax.numpy as jnp
        import numpy as np
        TOP_K = 2
        NUM_EXPERTS = 8
        DIM = 256
        HIDDEN = 704
        BS, SLEN = (2, 256)

        def _grouped_ffn(x, w1, w2, w3, counts):
            num_experts = w1.shape[0]
            ends = jnp.cumsum(counts)
            starts = ends - counts
            t = jnp.arange(x.shape[0])
            out = jnp.zeros((x.shape[0], w2.shape[-1]), x.dtype)
            for e in range(num_experts):
                m = ((t >= starts[e]) & (t < ends[e])).astype(x.dtype)[:, None]
                xe = x * m
                h = jax.nn.silu(xe @ w1[e]) * (xe @ w3[e])
                out = out + h @ w2[e] * m
            return out
        key = jax.random.key(seed)
        k = jax.random.split(key, 5)
        std = 0.02
        return {'x': jax.random.normal(k[0], (BS, SLEN, DIM), jnp.float32), 'gate_w': jax.random.normal(k[1], (NUM_EXPERTS, DIM), jnp.float32) * std, 'expert_bias': jnp.zeros((NUM_EXPERTS,), jnp.float32), 'w1': jax.random.normal(k[2], (NUM_EXPERTS, DIM, HIDDEN), jnp.float32) * std, 'w2': jax.random.normal(k[3], (NUM_EXPERTS, HIDDEN, DIM), jnp.float32) * std, 'w3': jax.random.normal(k[4], (NUM_EXPERTS, DIM, HIDDEN), jnp.float32) * std}
    _L0_ffn_all = _L0_ffn_setup()
    _L0_ffn_in = {k: v for k, v in _L0_ffn_all.items() if k in ('gate_w', 'expert_bias', 'w1', 'w2', 'w3')}
    del _L0_ffn_all
    return {'x': x, 'ctx_1024': ctx_1024, 'fside_BxS2_0': fside_BxS2_0, 'L0_xattn_in_proj_weight': _L0_xattn_in['in_proj_weight'], 'L0_xattn_in_proj_bias': _L0_xattn_in['in_proj_bias'], 'L0_xattn_out_proj_weight': _L0_xattn_in['out_proj_weight'], 'L0_xattn_out_proj_bias': _L0_xattn_in['out_proj_bias'], 'L0_ffn_gate_w': _L0_ffn_in['gate_w'], 'L0_ffn_expert_bias': _L0_ffn_in['expert_bias'], 'L0_ffn_w1': _L0_ffn_in['w1'], 'L0_ffn_w2': _L0_ffn_in['w2'], 'L0_ffn_w3': _L0_ffn_in['w3']}

def reference(x, ctx_1024, fside_BxS2_0, L0_xattn_in_proj_weight, L0_xattn_in_proj_bias, L0_xattn_out_proj_weight, L0_xattn_out_proj_bias, L0_ffn_gate_w, L0_ffn_expert_bias, L0_ffn_w1, L0_ffn_w2, L0_ffn_w3):
    import jax
    import jax.numpy as jnp

    def _L0_xattn_ref(query, key, value, key_abundance, in_proj_weight, in_proj_bias, out_proj_weight, out_proj_bias, num_heads):
        import jax, jax.numpy as jnp
        import numpy as np
        B, N, E, H = (2, 512, 256, 16)
        HD = E // H
        b, n_q, e = query.shape
        n_k = key.shape[1]
        hd = in_proj_weight.shape[1] // num_heads
        w_q, w_k, w_v = jnp.split(in_proj_weight, 3, axis=0)
        b_q, b_k, b_v = jnp.split(in_proj_bias, 3, axis=0)
        q = query @ w_q.T + b_q
        k = key @ w_k.T + b_k
        v = value @ w_v.T + b_v
        q = q.reshape(b, n_q, num_heads, hd).transpose(0, 2, 1, 3)
        k = k.reshape(b, n_k, num_heads, hd).transpose(0, 2, 1, 3)
        v = v.reshape(b, n_k, num_heads, hd).transpose(0, 2, 1, 3)
        scale = 1.0 / jnp.sqrt(jnp.asarray(hd, dtype=q.dtype))
        scores = jnp.einsum('bhqd,bhkd->bhqk', q, k) * scale
        scores = scores + jnp.log(key_abundance)[:, None, None, :]
        attn = jax.nn.softmax(scores, axis=-1)
        out = jnp.einsum('bhqk,bhkd->bhqd', attn, v)
        out = out.transpose(0, 2, 1, 3).reshape(b, n_q, num_heads * hd)
        return out @ out_proj_weight.T + out_proj_bias

    def _L0_ffn_ref(x, gate_w, expert_bias, w1, w2, w3):
        import jax, jax.numpy as jnp
        import numpy as np
        TOP_K = 2
        NUM_EXPERTS = 8
        DIM = 256
        HIDDEN = 704
        BS, SLEN = (2, 256)

        def _grouped_ffn(x, w1, w2, w3, counts):
            num_experts = w1.shape[0]
            ends = jnp.cumsum(counts)
            starts = ends - counts
            t = jnp.arange(x.shape[0])
            out = jnp.zeros((x.shape[0], w2.shape[-1]), x.dtype)
            for e in range(num_experts):
                m = ((t >= starts[e]) & (t < ends[e])).astype(x.dtype)[:, None]
                xe = x * m
                h = jax.nn.silu(xe @ w1[e]) * (xe @ w3[e])
                out = out + h @ w2[e] * m
            return out
        bs, slen, dim = x.shape
        num_experts = gate_w.shape[0]
        xf = x.reshape(bs * slen, dim)
        scores = jax.nn.softmax((xf @ gate_w.T).astype(jnp.float32), axis=-1)
        _, sel = jax.lax.top_k(scores + expert_bias, TOP_K)
        top_scores = jnp.take_along_axis(scores, sel, axis=1).reshape(-1)
        sel_flat = sel.reshape(-1)
        counts = jnp.zeros((num_experts,), jnp.int32).at[sel_flat].add(1)
        order = jnp.argsort(sel_flat, stable=True)
        top_scores_sorted = top_scores[order]
        token_idx = order // TOP_K
        routed = xf[token_idx] * top_scores_sorted[:, None].astype(xf.dtype)
        routed_out = _grouped_ffn(routed, w1, w2, w3, counts)
        out = jnp.zeros_like(xf).at[token_idx].add(routed_out)
        return out.reshape(bs, slen, dim)
    x = x + _L0_xattn_ref(_layernorm(x, axis=-1), ctx_1024, ctx_1024, fside_BxS2_0, L0_xattn_in_proj_weight, L0_xattn_in_proj_bias, L0_xattn_out_proj_weight, L0_xattn_out_proj_bias, 16)
    x = x + _L0_ffn_ref(_layernorm(x, axis=-1), L0_ffn_gate_w, L0_ffn_expert_bias, L0_ffn_w1, L0_ffn_w2, L0_ffn_w3)
    return x

_drawn_inputs = setup_inputs


def setup_inputs(seed=0):
    import zlib

    import numpy as np

    out = dict(_drawn_inputs(seed))
    spreads = {'L0_ffn_expert_bias': (0.0, 0.8)}
    factors = {'L0_xattn_in_proj_bias': 3.339,
     'L0_xattn_out_proj_bias': 3.192,
     'L0_ffn_gate_w': 8.0,
     'L0_ffn_w1': 8.0,
     'L0_ffn_w2': 8.0,
     'L0_ffn_w3': 8.0}
    for name, (base, spread) in spreads.items():
        noise = np.random.default_rng([zlib.crc32(name.encode()), seed]).standard_normal(out[name].shape)
        drawn = base * np.exp(spread * noise) if base else spread * noise
        out[name] = jnp.asarray(drawn.astype(out[name].dtype))
    for name, factor in factors.items():
        out[name] = (out[name] * factor).astype(out[name].dtype)
    return out
```

```python
from contextlib import ExitStack

import concourse.bass as bass
from concourse import mybir

ALU = mybir.AluOpType
ACT = mybir.ActivationFunctionType
F32 = mybir.dt.float32
F16 = mybir.dt.float16
I32 = mybir.dt.int32
AX = mybir.AxisListType

P = 128
LN_EPS = 1e-5
TINY = 1.2e-38
PARTS = 96


def xattn_moe(nc, x, ctx_in, abundance, w_in, b_in, w_out, b_out, gate_w, expert_bias, w1, w2, w3, out):
    B, N, D = x.shape
    S2 = ctx_in.shape[1]
    HD = 16
    H = D // HD
    E, _, F = w1.shape
    KD = D // P
    KF = (F + P - 1) // P
    FL = F - (KF - 1) * P
    UT = N // P
    T = B * UT
    TOK = B * N
    SL = H * S2
    HS = SL // 2
    TOPK = 2
    J = (TOK * TOPK + E * (P - 1)) // P
    NOUT = HD + 1
    W13 = KD * F
    W2H = KF // 2 * D
    HALF = W13 + W2H
    WE = 2 * HALF
    FH = F // 2
    XR = D + E
    assert B == 2 and KD == 2 and E == 8 and UT == 8 and KF == 6

    with ExitStack() as stack:
        def sb(name, shape, dt=F32):
            return stack.enter_context(nc.sbuf_tensor(name, shape, dt))

        def sem(name):
            return stack.enter_context(nc.semaphore(name))

        table = nc.dram_tensor("table", [TOK, XR], F32, kind="Internal").ap()
        acc = nc.dram_tensor("acc", [TOK + P, D], F32, kind="Internal").ap()
        table_v = table.rearrange("(b u p) d -> b u p d", b=B, p=P)
        acc_v = acc[0:TOK, :].rearrange("(b u p) d -> b u p d", b=B, p=P)

        w_hi = sb("w_hi", [P, E * WE], F16)
        w_lo = sb("w_lo", [P, E * WE], F16)
        ARENA = T * D + B * KD * SL
        arena = sb("arena", [P, ARENA])
        stage = [sb(f"stage{i}", [P, HALF]) for i in range(2)]

        class Region:

            def __init__(self, base, start=0):
                self.base, self.at = base, start

            def __call__(self, cols, dt=F32):
                words = cols if dt != F16 else (cols + 1) // 2
                assert self.at + words <= self.base.shape[-1], (self.at, words)
                a = self.base[:, self.at:self.at + words]
                self.at += words
                return a if dt == F32 else a.bitcast(dt)

        take = Region(arena)
        xs = take(T * D).rearrange("p (t d) -> p t d", t=T)
        a_hi = [take(KD * SL, F16).rearrange("p (k n) -> p k n", k=KD) for _ in range(B)]
        a_lo = [take(KD * SL, F16).rearrange("p (k n) -> p k n", k=KD) for _ in range(B)]
        LATE = T - 2
        take = Region(w_hi[:, (E - 1) * WE:E * WE].bitcast(F32))
        prob = [take(SL) for _ in range(2)]
        take = Region(w_lo[:, (E - 1) * WE:E * WE].bitcast(F32))
        probT = [take(SL) for _ in range(2)]
        xn = [sb(f"xn{i}", [P, D]) for i in range(2)]
        xn2 = [sb(f"xn2{i}", [P, D]) for i in range(2)]

        take = Region(arena)
        oneh_b = take(T * TOPK * P, F16).rearrange("p (n s) -> p n s", s=P)
        oneh_a = take(T * TOPK * J).rearrange("p (n j) -> p n j", j=J)
        val_a = take(T * TOPK * (J + 1), F16).rearrange("p (n j) -> p n j", j=J + 1)
        rank_w = take(T * E * E).rearrange("p (t e f) -> p t e f", t=T, e=E)
        rank_w2 = take(T * E * E).rearrange("p (t e f) -> p t e f", t=T, e=E)
        r_small = [take(T * E).rearrange("p (t e) -> p t e", t=T) for _ in range(7)]
        tile_oh = take(J * E).rearrange("p (j e) -> p j e", j=J)
        tile_cmp = take(J * E).rearrange("p (j e) -> p j e", j=J)
        count_w = take(E * T).rearrange("p (e t) -> p e t", e=E)
        ee_w = take(E * E).rearrange("p (e f) -> p e f", e=E)
        n_tiles, first_tile, last_tile = take(E), take(E), take(E)
        tile_exp, slot_tok, slot_pad, slot_tmp = take(J), take(J), take(J), take(J)
        tile_off, idx_get, idx_put = (take(J).bitcast(I32) for _ in range(3))
        pos_k, pos_b, pos_a = (take(T * TOPK).rearrange("p (t k) -> p t k", k=TOPK) for _ in range(3))
        t_max, t_sum = take(T), take(T)
        pos_i = take(T * TOPK).bitcast(I32).rearrange("p (t k) -> p t k", k=TOPK)

        take = Region(arena)
        hid = [take(F) for _ in range(2)]
        sil = [take(F) for _ in range(2)]
        hT_hi = [take(KF * P, F16) for _ in range(2)]
        hT_lo = [take(KF * P, F16) for _ in range(2)]
        y_sb = [take(D) for _ in range(2)]
        gx = [take(XR) for _ in range(2)]
        gT_hi = [take(KD * P, F16) for _ in range(2)]
        gT_lo = [take(KD * P, F16) for _ in range(2)]
        assert take.at <= 5984
        score_w = sb("score_w", [P, E])
        slot_score = [sb(f"slot_score{i}", [P, 1]) for i in range(2)]
        get_now = [sb(f"get_now{i}", [P, 1], I32) for i in range(2)]
        put_now = [sb(f"put_now{i}", [P, 1], I32) for i in range(2)]

        ident = sb("ident", [P, P])
        ones16 = sb("ones16", [P, P], F16)
        before_half = sb("before_half", [P, P], F16)
        iota_p = sb("iota_p", [P, P])
        tok_id = sb("tok_id", [P, T])
        row_id = sb("row_id", [P, 1])
        lower = sb("lower", [P, E, E])
        tile_edge = sb("tile_edge", [P, E, T])

        gateT = sb("gateT", [P, KD, E])
        woT = sb("woT", [P, KD, D])
        v_blk = sb("v_blk", [P, B, 8, 2 * NOUT])
        beta = sb("beta", [PARTS, B, SL], F16)
        bo_parts = sb("bo_parts", [PARTS, D], F16)
        ebias = sb("ebias", [P, E])

        take = Region(w_hi[:, 3 * WE:(E - 1) * WE].bitcast(F32))
        prep = take(6 * D).rearrange("p (r d) -> p r d", r=6)
        wo_n = take(2 * D).rearrange("p (r d) -> p r d", r=2)
        ctx_n = take(D)
        wkvT = take(KD * 4 * P).rearrange("p (k n) -> p k n", k=KD)
        k_blk = [take(B * HS).rearrange("p (b n) -> p b n", b=B) for _ in range(2)]
        ctxT = take(KD * P).rearrange("p (k n) -> p k n", k=KD)
        ctxD = take(KD * B * P).rearrange("p (k b n) -> p k b n", k=KD, b=B)
        kT = take(2 * P).rearrange("p (c n) -> p c n", c=2)
        gate_n = take(D)[0:E]
        bias_qk = take(4)
        bq_sel = take(2 * PARTS).rearrange("p (c n) -> p c n", c=2)
        bv_row = take(D)[0:1]
        take = Region(w_lo[:, 3 * WE:(E - 1) * WE].bitcast(F32))
        bo_row = take(D)[0:1]
        ab_row = take(B * S2)[0:1]
        ab_col = take(B)
        ab_mask = take(B)
        beta_res = [take(HS)[0:PARTS] for i in range(2)]
        ones_row = take(P)[0:1]
        parts_sel = take(PARTS)[0:1]
        head_mask = take(8)
        zero_rows = take(D)

        st_all = take(T * 6).rearrange("p (t n) -> p t n", t=T)
        mv_all = sb("mv_all", [P, T, 2])
        rs_all = sb("rs_all", [P, T])
        rsw = sb("rsw", [P, 3 * T])
        st2 = sb("st2", [P, 6])
        mv2 = sb("mv2", [P, 2])
        rs2 = sb("rs2", [P, 1])
        xT_hi = [sb(f"xThi{i}", [P, KD * P], F16) for i in range(2)]
        xT_lo = [sb(f"xTlo{i}", [P, KD * P], F16) for i in range(2)]
        top = sb("top", [P, H])
        o_inv = sb("o_inv", [P, H])
        o_sb = sb("o_sb", [P, D])
        oT = sb("oT", [P, KD * P])
        xn2T = sb("xn2T", [P, KD * P])
        logits = sb("logits", [P, T, E])
        sel16 = sb("sel16", [P, T, E], F16)

        bank = [stack.enter_context(nc.psum_tensor(f"bank{i}", [P, 512], F32)) for i in range(2)]
        sc_ps = [stack.enter_context(nc.psum_tensor(f"sc{i}", [P, 1024], F32)) for i in range(2)]
        pt_ps2 = stack.enter_context(nc.psum_tensor("ptps", [P, 1024], F32))
        bk6, bk7 = bank
        h1_ps = sc_ps[0][:, :].rearrange("p (c n) -> p c n", c=2)[:, :, 0:FH]
        h3_ps = sc_ps[1][:, :].rearrange("p (c n) -> p c n", c=2)[:, :, 0:FH]
        hT_ps = pt_ps2[:, 0:KF * P]

        names = """consts prep_loads x_loads w_loads0 w_loads1 xn2_st0 xn2_st1 x2_st0 x2_st1 score_st zero_st
            ctxT_ps ctxT_sb wkvT_ps wkvT_sb woT_ps woT_sb gT_ps gT_sb kT_ps kT_sb kblk v_ps v_sb a_ps a_hi_s a_lo_s
            beta_ps beta_sb bo_ps bo_sb prep_dve prep_act
            ln1_stats ln1_mv ln1_rstd xn_ready xt_ps xt_hi xt_lo s_ps smax ssub p_exp pt_ps pt_sb
            o_ps o_recip o_norm ot_ps ot_sb attn_ps x2_ready ln2_stats ln2_mv ln2_rstd xn2_ready
            x2t_ps x2t_sb logit_ps logit_sb whi wlo
            route exp_in exp_out scores_in selected prefix_ps oneh_ready slots_ps idx_ready
            get_idx gat0 gat1 put_idx put_done sc_tmp sc_ready gt_ps gt_hi gt_lo h_ps silu_done h_ready ht_ps ht_hi ht_lo
            y_ps y_ready copied carried_dve carried_pool""".split()
        s = {n: sem(n) for n in names}
        w_loads = [s["w_loads0"], s["w_loads1"]]
        xn2_st = [s["xn2_st0"], s["xn2_st1"]]
        x2_st = [s["x2_st0"], s["x2_st1"]]
        gathered = [s["gat0"], s["gat1"]]
        LOADS = 12

        def back(u, par, k):
            return u + (par - k) // 2, (par - k) % 2

        def attention_steps(eng, step):
            for t in range(4):
                step(t // 2, t % 2, t)
            with eng.Fori(2, UT - 1) as u:
                step(u, 0, None)
                step(u, 1, None)
            for t in range(T - 2, T + 3):
                step(t // 2, t % 2, t)

        def here(t, lag):
            return t is None or 0 <= t - lag < T

        def expert_steps(eng, step):
            for j in range(3):
                step(j, j % 2)
            with eng.Fori(1, (J - 3) // 2) as v:
                step(2 * v + 1, 1)
                step(2 * v + 2, 0)
            for j in range(J - 2, J + 1):
                step(j, j % 2)

        def carry(eng):
            eng.sem_inc(s["carried_dve" if eng.engine == nc.vector.engine else "carried_pool"], 1)

        def a_bank(n):
            return sc_ps[n // 2 % 2][:, n % 2 * 512:n % 2 * 512 + HS]

        assert J % 2 == 1
        block = stack.enter_context(nc.Block())

        @block.sync
        def _(sp):
            sp.dma_start(ctx_n, ctx_in.rearrange("b s d -> (b s) d")).then_inc(s["prep_loads"], 16)
            sp.dma_start(prep, w_in.rearrange("(r p) d -> p r d", p=P)).then_inc(s["prep_loads"], 16)
            sp.dma_start(wo_n, w_out.rearrange("(r p) d -> p r d", p=P)).then_inc(s["prep_loads"], 16)
            for b in range(B):
                sp.dma_start(xs[:, b:T:2, :], x[b].rearrange("(u p) d -> p u d", p=P)).then_inc(s["x_loads"], 16)

            sp.wait_ge(s["consts"], N_CONST_EARLY)
            sp.dma_start(acc[TOK:TOK + P, :], zero_rows).then_inc(s["zero_st"], 16)

            def step(u, par, t):
                if here(t, 0):
                    if t is None or t >= 2:
                        sp.wait_ge(s["whi"], 2 * u + par - 1)
                        sp.wait_ge(s["wlo"], 2 * u + par - 1)
                    wa = (w1, w3)[par]
                    dst = stage[par]
                    uu = u if t is not None else bass.ds(u, 1)
                    src13 = wa[uu].rearrange("(k p) f -> p k f", p=P) if t is not None else \
                        wa[uu].rearrange("e (k p) f -> p (e k) f", p=P)
                    sp.dma_start(dst[:, 0:W13].rearrange("p (k f) -> p k f", k=KD), src13).then_inc(w_loads[par], 16)
                    c0 = par * KF // 2 * P
                    w2e = w2[uu] if t is not None else w2[uu].rearrange("e f d -> (e f) d")
                    full = KF // 2 - par
                    sp.dma_start(dst[:, W13:W13 + full * D].rearrange("p (c d) -> p c d", c=full),
                                 w2e[c0:c0 + full * P, :].rearrange("(c p) d -> p c d", p=P)).then_inc(w_loads[par], 16)
                    if par:
                        sp.dma_start(dst[0:FL, W13 + full * D:HALF], w2e[F - FL:F, :]).then_inc(w_loads[par], 16)
                if here(t, 2):
                    bu, bp = back(u, par, 2)
                    bt = 2 * bu + bp
                    if t is None:
                        row = bass.ds(bu, 1)
                        acc_d = acc_v[bp, row].rearrange("u p d -> p (u d)")
                        tab_d = table_v[bp, row, :, 0:D].rearrange("u p d -> p (u d)")
                        x_s = xs[:, bass.ds(bt, 1), :].rearrange("p u d -> p (u d)")
                    else:
                        acc_d, tab_d, x_s = acc_v[bp, bu], table_v[bp, bu, :, 0:D], xs[:, bt, :]
                    sp.wait_ge(s["x2_ready"], bt + 1)
                    sp.dma_start(acc_d, x_s).then_inc(x2_st[bp], 16)
                    sp.wait_ge(s["xn2_ready"], bt + 1)
                    sp.dma_start(tab_d, xn2[bp][:, :]).then_inc(xn2_st[bp], 16)

            attention_steps(sp, step)
            sp.wait_ge(s["scores_in"], 1)
            for b in range(B):
                sp.dma_start(table_v[b, :, :, D:XR].rearrange("u p e -> p u e"),
                             r_small[0][:, b:T:2, :]).then_inc(s["score_st"], 16)
            sp.wait_ge(s["put_done"], 16 * J)
            sp.dma_start(out.rearrange("b n d -> (b n) d"), acc[0:TOK, :]).then_inc(s["copied"], 16)
            sp.wait_ge(s["copied"], 16)

        @block.gpsimd
        def _(pool):
            n_c = [0]

            def const(ins):
                n_c[0] += 1
                ins.then_inc(s["consts"], 1)
                pool.wait_ge(s["consts"], n_c[0])

            const(pool.memset(ident[:, :], 0.0))
            const(pool.affine_select(out=ident[:, :], in_=ident[:, :], compare_op=ALU.not_equal, fill=1.0, base=0,
                                     pattern=[[-1, P]], channel_multiplier=1))
            const(pool.memset(ones_row[:, :], 1.0))
            const(pool.memset(ones16[:, :], 1.0))
            const(pool.memset(before_half[:, :], 0.5))
            const(pool.affine_select(out=before_half[:, :], in_=before_half[:, :], compare_op=ALU.is_gt, fill=0.0, base=0,
                                     pattern=[[1, P]], channel_multiplier=-1))
            const(pool.memset(head_mask[:, :], 1.0))
            const(pool.affine_select(out=head_mask[:, :], in_=head_mask[:, :], compare_op=ALU.is_ge, fill=0.0,
                                     base=0, pattern=[[-HD, 8]], channel_multiplier=1))
            const(pool.affine_select(out=head_mask[:, :], in_=head_mask[:, :], compare_op=ALU.is_ge, fill=0.0,
                                     base=HD - 1, pattern=[[HD, 8]], channel_multiplier=-1))
            const(pool.memset(bq_sel[:, :, :], 0.0))
            const(pool.memset(parts_sel[:, :], 0.0))
            const(pool.memset(parts_sel[:, 0:PARTS:32], 1.0))
            const(pool.memset(v_blk[:, :, :, :], 0.0))
            const(pool.memset(zero_rows[:, :], 0.0))
            const(pool.iota(iota_p[:, :], pattern=[[1, P]], base=0, channel_multiplier=0,
                            allow_small_or_imprecise_dtypes=True))
            const(pool.iota(row_id[:, :], pattern=[[0, 1]], base=0, channel_multiplier=1,
                            allow_small_or_imprecise_dtypes=True))
            for b in range(B):
                const(pool.iota(tok_id[:, b:T:2], pattern=[[P, UT]], base=b * N + 1, channel_multiplier=1,
                                allow_small_or_imprecise_dtypes=True))
            const(pool.memset(lower[:, :, :], 1.0))
            const(pool.affine_select(out=lower[:, :, :], in_=lower[:, :, :], compare_op=ALU.is_gt, fill=0.0, base=0,
                                     pattern=[[1, E], [-1, E]], channel_multiplier=0))
            const(pool.iota(tile_edge[:, :, :], pattern=[[0, E], [P, T]], base=0, channel_multiplier=0,
                            allow_small_or_imprecise_dtypes=True))
            const(pool.memset(stage[1][FL:P, HALF - D:HALF], 0.0))
            assert n_c[0] == N_CONST

            def step(u, par, t):
                if t is None or t < LATE:
                    tt = 2 * u + par
                    pool.wait_ge(s["whi"], tt + 1)
                    dst = slice(tt * HALF, (tt + 1) * HALF) if t is not None else bass.ds(tt * HALF, HALF)
                    pool.tensor_tensor(w_lo[:, dst], stage[par][:, :], w_hi[:, dst], ALU.subtract).then_inc(s["wlo"], 1)

            attention_steps(pool, step)
            pool.wait_ge(s["o_ps"], T)
            for h in range(LATE, T):
                pool.wait_ge(s["whi"], h + 1)
                dst = slice(h * HALF, (h + 1) * HALF)
                pool.tensor_tensor(w_lo[:, dst], stage[h % 2][:, :], w_hi[:, dst], ALU.subtract).then_inc(s["wlo"], 1)
            pool.wait_ge(s["zero_st"], 16)
            for b in range(2):
                pool.wait_ge(x2_st[b], 16 * UT)
                pool.wait_ge(xn2_st[b], 16 * UT)
            pool.wait_ge(s["score_st"], 16 * B)
            pool.wait_ge(s["idx_ready"], 1)

            def gather(j, par, dyn):
                col = bass.ds(j, 1) if dyn else slice(j, j + 1)
                pool.tensor_copy(get_now[par][:, :], idx_get[:, col]).then_inc(s["get_idx"], 1)
                pool.wait_ge(s["get_idx"], j + 1)
                carry(pool)
                pool.indirect_dma_start(out=gx[par], out_offset=None, in_=table[:, :],
                                        in_offset=bass.IndirectOffsetOnAxis(ap=get_now[par][:, 0:1], axis=0))\
                    .then_inc(gathered[par], 16)

            gather(0, 0, False)
            gather(1, 1, False)

            def step(j, par):
                static = isinstance(j, int)
                if not static or j + 2 < J:
                    pool.wait_ge(s["gt_ps"], j + 1)
                    pool.wait_ge(s["sc_tmp"], j + 1)
                    gather(j + 2, par, not static)
                if not static or j >= 1:
                    q = 1 - par
                    col = slice(j - 1, j) if static else bass.ds(j - 1, 1)
                    pool.tensor_copy(put_now[q][:, :], idx_put[:, col]).then_inc(s["put_idx"], 1)
                    pool.wait_ge(s["put_idx"], j)
                    pool.wait_ge(s["y_ready"], j)
                    if not static or j >= 2:
                        pool.wait_ge(s["put_done"], 16 * (j - 1))
                    carry(pool)
                    pool.indirect_dma_start(out=acc[:, :],
                                            out_offset=bass.IndirectOffsetOnAxis(ap=put_now[q][:, 0:1], axis=0),
                                            in_=y_sb[q], in_offset=None, compute_op=ALU.add)\
                        .then_inc(s["put_done"], 16)

            expert_steps(pool, step)

        @block.scalar
        def _(act):
            with nc.allow_non_contiguous_dma(reason="columns of biases"):
                for c in range(4):
                    act.dma_start(bias_qk[:, c:c + 1], b_in[c * P:(c + 1) * P].rearrange("(p a) -> p a", a=1))\
                        .then_inc(s["prep_loads"], 16)
                for b in range(B):
                    for r in range(2):
                        act.dma_start(ab_col[r * S2:(r + 1) * S2, b:b + 1],
                                      abundance[b].rearrange("(p a) -> p a", a=1)).then_inc(s["prep_loads"], 16)
            act.dma_start(gate_n[:, :], gate_w).then_inc(s["prep_loads"], 16)
            act.dma_start(bv_row[:, :], b_in[2 * D:3 * D].rearrange("(a n) -> a n", a=1)).then_inc(s["prep_loads"], 16)
            act.dma_start(bo_row[:, :], b_out.rearrange("(a n) -> a n", a=1)).then_inc(s["prep_loads"], 16)
            act.dma_start(ab_row[:, :], abundance.rearrange("(a b) s -> a (b s)", a=1)).then_inc(s["prep_loads"], 16)
            act.dma_start(ebias[:, :], expert_bias.rearrange("(a n) -> a n", a=1).broadcast_to([P, E]))\
                .then_inc(s["prep_loads"], 16)
            act.wait_ge(s["prep_dve"], AB_DONE)
            act.activation(ab_row[:, :], ab_row[:, :], ACT.Ln).then_inc(s["prep_act"], 1)
            act.wait_ge(s["wkvT_ps"], 1)
            act.activation(wkvT[:, 0, :], sc_ps[0][:, 0:4 * P], ACT.Copy).then_inc(s["wkvT_sb"], 1)
            act.activation(wkvT[:, 1, :], sc_ps[0][:, 512:512 + 4 * P], ACT.Copy).then_inc(s["wkvT_sb"], 1)
            act.wait_ge(s["woT_ps"], 1)
            act.activation(woT[:, :, :], pt_ps2[:, 0:2 * D].rearrange("p (k n) -> p k n", k=2), ACT.Copy)\
                .then_inc(s["woT_sb"], 1)
            for n in range(8):
                b, c, k = n // 4, n // 2 % 2, n % 2
                act.wait_ge(s["a_ps"], n + 1)
                act.activation(a_hi[b][:, k, c * HS:(c + 1) * HS], a_bank(n), ACT.Copy).then_inc(s["a_hi_s"], 1)

            def step(u, par, t):
                tt = 2 * u + par
                if here(t, 0):
                    act.wait_ge(s["xt_ps"], tt + 1)
                    if t is None or t >= 2:
                        act.wait_ge(s["s_ps"], tt - 1)
                    act.activation(xT_hi[par][:, :], bk6[:, 0:KD * P], ACT.Copy).then_inc(s["xt_hi"], 1)
                if here(t, 3):
                    bt = tt - 3
                    act.wait_ge(s["x2t_ps"], bt + 1)
                    act.activation(xn2T[:, :], bk6[:, 0:KD * P], ACT.Copy).then_inc(s["x2t_sb"], 1)
                if here(t, 2):
                    bt = tt - 2
                    act.wait_ge(s["ot_ps"], bt + 1)
                    act.activation(oT[:, :], bk7[:, 0:KD * P], ACT.Copy).then_inc(s["ot_sb"], 1)
                if here(t, 1):
                    bu, bp = back(u, par, 1)
                    bt = tt - 1
                    for c in range(2):
                        act.wait_ge(s["pt_ps"], 2 * bt + c + 1)
                        act.activation(probT[bp][:, c * HS:(c + 1) * HS], pt_ps2[:, c * HS:(c + 1) * HS], ACT.Copy)\
                            .then_inc(s["pt_sb"], 1)
                if t is None or t < LATE:
                    act.wait_ge(w_loads[par], (32 + 16 * par) * (u + 1))
                    if t == 1:
                        act.wait_ge(s["consts"], N_CONST)
                    dst = slice(tt * HALF, (tt + 1) * HALF) if t is not None else bass.ds(tt * HALF, HALF)
                    act.activation(w_hi[:, dst], stage[par][:, :], ACT.Copy).then_inc(s["whi"], 1)
                if here(t, 0):
                    act.wait_ge(s["ssub"], tt + 1)
                    act.activation(prob[par], prob[par], ACT.Exp).then_inc(s["p_exp"], 1)

            attention_steps(act, step)
            act.wait_ge(s["pt_ps"], 2 * T)
            for h in range(LATE, T):
                act.wait_ge(w_loads[h % 2], (32 + 16 * (h % 2)) * (h // 2 + 1))
                act.activation(w_hi[:, h * HALF:(h + 1) * HALF], stage[h % 2][:, :], ACT.Copy).then_inc(s["whi"], 1)
            act.wait_ge(s["exp_in"], 1)
            act.activation(r_small[1], r_small[1], ACT.Exp).then_inc(s["exp_out"], 1)

            def rows_high(j, par):
                act.wait_ge(s["gt_ps"], j + 1)
                if not isinstance(j, int) or j >= 2:
                    act.wait_ge(s["h_ps"], 2 * (j - 1))
                act.activation(gT_hi[par], bk6[:, 0:KD * P], ACT.Copy).then_inc(s["gt_hi"], 1)

            rows_high(0, 0)

            def step(j, par):
                static = isinstance(j, int)
                if not static or j < J:
                    act.wait_ge(s["sc_ready"], j + 1)
                    for c in range(2):
                        act.wait_ge(s["h_ps"], 2 * j + c + 1)
                        act.activation(sil[par].rearrange("p (c n) -> p c n", c=2)[:, c, :], h1_ps[:, c, :], ACT.Silu,
                                       scale=slot_score[par][:, 0:1]).then_inc(s["silu_done"], 1)
                    if not static or j + 1 < J:
                        rows_high(j + 1, 1 - par)
                    act.wait_ge(s["ht_ps"], j + 1)
                    if not static or j >= 2:
                        act.wait_ge(s["y_ps"], j - 1)
                    act.activation(hT_hi[par], hT_ps, ACT.Copy).then_inc(s["ht_hi"], 1)

            expert_steps(act, step)

        @block.vector
        def _(dve):
            def link(ins):
                n_d[0] += 1
                ins.then_inc(s["prep_dve"], 1)
                dve.wait_ge(s["prep_dve"], n_d[0])

            n_d = [0]
            dve.wait_ge(s["prep_loads"], 16 * PREP_DMAS)
            link(dve.tensor_scalar(ab_mask[:, :], ab_col[:, :], 0.0, None, ALU.is_gt))
            link(dve.tensor_scalar(ab_row[:, :], ab_row[:, :], TINY, None, ALU.max))
            assert n_d[0] == AB_DONE
            dve.wait_ge(s["consts"], N_CONST_EARLY)
            for c in range(2):
                link(dve.tensor_copy(bq_sel[:, c, 0:PARTS:32], bias_qk[:, c:c + 1].broadcast_to([P, 3])))
            assert n_d[0] == BQ_DONE
            dve.wait_ge(s["ctxT_ps"], 1)
            dve.tensor_copy(ctxT, bk6[:, 0:KD * P].rearrange("p (k n) -> p k n", k=KD)).then_inc(s["ctxT_sb"], 1)
            for k in range(KD):
                for b in range(B):
                    src = bk6[:, k * P + b * S2:k * P + (b + 1) * S2]
                    for r in range(2):
                        dve.tensor_copy(ctxD[:, k, b, r * S2:(r + 1) * S2], src).then_inc(s["ctxT_sb"], 1)
            dve.wait_ge(s["gT_ps"], 1)
            dve.tensor_copy(gateT[:, :, :], bk7[:, 0:KD * E].rearrange("p (k e) -> p k e", k=KD)).then_inc(s["gT_sb"], 1)
            dve.wait_ge(s["kT_ps"], 1)
            for c in range(2):
                link(dve.tensor_scalar(kT[:, c, :], bk6[:, 256 + c * P:256 + (c + 1) * P], bias_qk[:, 2 + c:3 + c],
                                       HD ** -0.5, ALU.add, ALU.mult))
                for b in range(B):
                    dve.tensor_tensor(k_blk[c][:, b, :].rearrange("p (h s) -> p h s", h=8),
                                      kT[:, c, None, b * S2:(b + 1) * S2].broadcast_to([P, 8, S2]),
                                      head_mask[:, :, None].broadcast_to([P, 8, S2]), ALU.mult).then_inc(s["kblk"], 1)
            for b in range(B):
                dve.wait_ge(s["v_ps"], b + 1)
                vp = bk7[:, 0:D] if b == 0 else bk7[:, 256:512]
                for r in range(2):
                    rows = slice(r * S2, (r + 1) * S2)
                    dst = v_blk[rows, b, :, r * NOUT:r * NOUT + HD]
                    dve.tensor_scalar(dst, vp[rows, :].rearrange("p (j r d) -> p j r d", j=8, r=2)[:, :, r, :],
                                      ab_mask[rows, b:b + 1], None, ALU.mult).then_inc(s["v_sb"], 1)
                    dve.tensor_copy(v_blk[rows, b, :, r * NOUT + HD:(r + 1) * NOUT],
                                    ab_mask[rows, b:b + 1, None].broadcast_to([S2, 8, 1])).then_inc(s["v_sb"], 1)
            for n in range(8):
                b, c, k = n // 4, n // 2 % 2, n % 2
                dve.wait_ge(s["a_hi_s"], n + 1)
                dve.tensor_tensor(a_lo[b][:, k, c * HS:(c + 1) * HS], a_bank(n), a_hi[b][:, k, c * HS:(c + 1) * HS],
                                  ALU.subtract).then_inc(s["a_lo_s"], 1)

            def three_parts(dst, src, n, signal):
                res = beta_res[0][:, 0:n]
                res2 = beta_res[1][:, 0:n]
                link(dve.tensor_copy(dst, src))
                link(dve.tensor_tensor(res, src, dst, ALU.subtract))
                link(dve.tensor_copy(dst[32:64], res[32:64]))
                link(dve.tensor_copy(dst[64:PARTS], res[64:PARTS]))
                link(dve.tensor_tensor(res2[64:PARTS], res[64:PARTS], dst[64:PARTS], ALU.subtract))
                dve.tensor_copy(dst[64:PARTS], res2[64:PARTS]).then_inc(s[signal], 1)

            for n in range(2 * B):
                b, c = n // 2, n % 2
                dve.wait_ge(s["beta_ps"], n + 1)
                three_parts(beta[:, b, c * HS:(c + 1) * HS], pt_ps2[0:PARTS, c * HS:(c + 1) * HS], HS, "beta_sb")
            dve.wait_ge(s["bo_ps"], 1)
            three_parts(bo_parts[:, :], bk7[0:PARTS, 0:D], D, "bo_sb")
            dve.wait_ge(s["x_loads"], 16 * B)

            def rsqrt(r, v, ve, w, w2, chain, base):
                n = [0]

                def go(ins):
                    n[0] += 1
                    ins.then_inc(s[chain], 1)
                    dve.wait_ge(s[chain], base + n[0])

                go(dve.tensor_scalar(ve, v, LN_EPS, None, ALU.add))
                go(dve.tensor_scalar(r.bitcast(I32), ve.bitcast(I32), -0.5, float(0x5F3759DF), ALU.mult, ALU.add))
                for _ in range(2):
                    go(dve.tensor_tensor(w, r, r, ALU.mult))
                    go(dve.tensor_tensor(w, w, ve, ALU.mult))
                    go(dve.tensor_scalar(w2, w, 0.375, -1.25, ALU.mult, ALU.add))
                    go(dve.tensor_tensor(w2, w2, w, ALU.mult))
                    go(dve.scalar_tensor_tensor(out=r, in0=w2, scalar=1.875, in1=r, op0=ALU.add, op1=ALU.mult))
                assert n[0] == RSQRT_OPS

            def tile(t, tt):
                return xs[:, tt, :] if t is not None else xs[:, bass.ds(tt, 1), :].rearrange("p u d -> p (u d)")

            for t in range(T):
                dve.bn_stats(st_all[:, t, :], xs[:, t, :]).then_inc(s["ln1_stats"], 1)
            dve.wait_ge(s["ln1_stats"], T)
            for t in range(T):
                dve.bn_aggr(mv_all[:, t, :], st_all[:, t, :]).then_inc(s["ln1_mv"], 1)
            dve.wait_ge(s["ln1_mv"], T)
            rsqrt(rs_all[:, :], mv_all[:, :, 1], rsw[:, 0:T], rsw[:, T:2 * T], rsw[:, 2 * T:3 * T], "ln1_rstd", 0)

            def ln1(t, tt, par):
                at = slice(tt, tt + 1) if t is not None else bass.ds(tt, 1)
                dve.tensor_scalar(xn[par][:, :], tile(t, tt), mv_all[:, at, 0], rs_all[:, at], ALU.subtract, ALU.mult)\
                    .then_inc(s["xn_ready"], 1)

            def ln2(x_in, dst, bt):
                carry(dve)
                dve.bn_stats(st2[:, :], x_in).then_inc(s["ln2_stats"], 1)
                dve.wait_ge(s["ln2_stats"], bt + 1)
                carry(dve)
                dve.bn_aggr(mv2[:, :], st2[:, :]).then_inc(s["ln2_mv"], 1)
                dve.wait_ge(s["ln2_mv"], bt + 1)
                rsqrt(rs2[:, :], mv2[:, 1:2], rsw[:, 0:1], rsw[:, 1:2], rsw[:, 2:3], "ln2_rstd", bt * RSQRT_OPS)
                dve.tensor_scalar(dst, x_in, mv2[:, 0:1], rs2[:, 0:1], ALU.subtract, ALU.mult).then_inc(s["xn2_ready"], 1)

            ln1(0, 0, 0)

            def step(u, par, t):
                tt = 2 * u + par
                if here(t, 0):
                    dve.wait_ge(s["xt_hi"], tt + 1)
                    dve.tensor_tensor(xT_lo[par][:, :], bk6[:, 0:KD * P], xT_hi[par][:, :], ALU.subtract)\
                        .then_inc(s["xt_lo"], 1)
                if here(t, 2):
                    bt = tt - 2
                    ov = bk7[:, 0:H * NOUT].rearrange("p (h n) -> p h n", h=H)
                    dve.wait_ge(s["o_ps"], bt + 1)
                    dve.reciprocal(o_inv[:, :], ov[:, :, HD:NOUT].rearrange("p h n -> p (h n)")).then_inc(s["o_recip"], 1)
                    dve.wait_ge(s["o_recip"], bt + 1)
                    dve.tensor_tensor(o_sb[:, :].rearrange("p (h n) -> p h n", h=H), ov[:, :, 0:HD],
                                      o_inv[:, :, None].broadcast_to([P, H, HD]), ALU.mult).then_inc(s["o_norm"], 1)
                if here(t, -1):
                    if t is None or t >= 1:
                        dve.wait_ge(s["xt_ps"], tt)
                    ln1(t, tt + 1, 1 - par)
                if here(t, 3):
                    bt = tt - 3
                    dve.wait_ge(s["logit_ps"], bt + 1)
                    lo = logits[:, bt, :] if t is not None else logits[:, bass.ds(bt, 1), :].rearrange("p u e -> p (u e)")
                    dve.tensor_copy(lo, bk6[:, 256:256 + E]).then_inc(s["logit_sb"], 1)
                if here(t, 0):
                    sv = sc_ps[par][:, :].rearrange("p (h n) -> p h n", h=H)
                    dve.wait_ge(s["s_ps"], tt + 1)
                    dve.tensor_reduce(top[:, :], sv, AX.X, ALU.max).then_inc(s["smax"], 1)
                    dve.wait_ge(s["smax"], tt + 1)
                    if t is None or t >= 2:
                        dve.wait_ge(s["pt_ps"], 2 * (tt - 1))
                    dve.tensor_tensor(prob[par].rearrange("p (h n) -> p h n", h=H), sv,
                                      top[:, :, None].broadcast_to([P, H, S2]), ALU.subtract).then_inc(s["ssub"], 1)
                if here(t, 2):
                    bu, bp = back(u, par, 2)
                    bt = tt - 2
                    dve.wait_ge(s["attn_ps"], bt + 1)
                    xt = tile(t, bt)
                    dve.tensor_tensor(xt, bk7[:, 0:D], xt, ALU.add).then_inc(s["x2_ready"], 1)
                    dve.wait_ge(s["x2_ready"], bt + 1)
                    if t is None or bt >= 2:
                        dve.wait_ge(xn2_st[bp], 16 * bu)
                        dve.wait_ge(s["x2t_ps"], bt - 1)
                    ln2(xt, xn2[bp][:, :], bt)

            attention_steps(dve, step)

            n_r = [0]

            def rlink(ins):
                n_r[0] += 1
                ins.then_inc(s["route"], 1)
                dve.wait_ge(s["route"], n_r[0])

            score, ex, biased, rank, pos, pick = r_small[:6]
            dve.wait_ge(s["logit_sb"], T)
            for b in range(B):
                dve.wait_ge(x2_st[b], 16 * UT)
            dve.wait_ge(s["pt_ps"], 2 * T)
            dve.wait_ge(s["o_ps"], T)
            rlink(dve.tensor_reduce(t_max[:, :], logits[:, :, :], AX.X, ALU.max))
            dve.tensor_tensor(ex, logits[:, :, :], t_max[:, :, None].broadcast_to([P, T, E]), ALU.subtract)\
                .then_inc(s["exp_in"], 1)
            dve.wait_ge(s["exp_out"], 1)
            rlink(dve.tensor_reduce(t_sum[:, :], ex, AX.X, ALU.add))
            rlink(dve.reciprocal(t_sum[:, :], t_sum[:, :]))
            dve.tensor_tensor(score, ex, t_sum[:, :, None].broadcast_to([P, T, E]), ALU.mult).then_inc(s["scores_in"], 1)
            dve.wait_ge(s["scores_in"], 1)
            rlink(dve.tensor_tensor(biased, score, ebias[:, None, :].broadcast_to([P, T, E]), ALU.add))
            s_e = biased[:, :, :, None].broadcast_to([P, T, E, E])
            s_f = biased[:, :, None, :].broadcast_to([P, T, E, E])
            rlink(dve.tensor_tensor(rank_w, s_f, s_e, ALU.is_equal))
            rlink(dve.tensor_tensor(rank_w, rank_w, lower[:, None, :, :].broadcast_to([P, T, E, E]), ALU.mult))
            rlink(dve.tensor_tensor(rank_w2, s_f, s_e, ALU.is_gt))
            rlink(dve.tensor_tensor(rank_w, rank_w, rank_w2, ALU.add))
            rlink(dve.tensor_reduce(rank, rank_w, AX.X, ALU.add))
            dve.tensor_scalar(sel16[:, :, :], rank, float(TOPK), None, ALU.is_lt).then_inc(s["selected"], 1)
            dve.wait_ge(s["prefix_ps"], 1)
            rlink(dve.tensor_tensor(count_w[:, :, :], bk7[:, 0:E, None].broadcast_to([P, E, T]), tile_edge[:, :, :],
                                    ALU.is_gt))
            rlink(dve.tensor_reduce(n_tiles[:, :], count_w[:, :, :], AX.X, ALU.add))
            rlink(dve.tensor_tensor(ee_w[:, :, :], lower[:, :, :], n_tiles[:, None, :].broadcast_to([P, E, E]), ALU.mult))
            rlink(dve.tensor_reduce(first_tile[:, :], ee_w[:, :, :], AX.X, ALU.add))
            rlink(dve.tensor_tensor(last_tile[:, :], first_tile[:, :], n_tiles[:, :], ALU.add))
            rlink(dve.tensor_scalar(first_tile[:, :], first_tile[:, :], float(P), None, ALU.mult))
            rlink(dve.tensor_tensor(pos, bk6[:, 0:T * E].rearrange("p (t e) -> p t e", t=T),
                                    first_tile[:, None, :].broadcast_to([P, T, E]), ALU.add))
            for k in range(TOPK):
                rlink(dve.scalar_tensor_tensor(out=pick.rearrange("p t e -> p (t e)"), in0=rank.rearrange("p t e -> p (t e)"),
                                               scalar=float(k), in1=pos.rearrange("p t e -> p (t e)"),
                                               op0=ALU.is_equal, op1=ALU.mult))
                rlink(dve.tensor_reduce(pos_k[:, :, k:k + 1].rearrange("p t k -> p (t k)"), pick, AX.X, ALU.add))
            rlink(dve.tensor_copy(pos_i[:, :, :], pos_k[:, :, :]))
            rlink(dve.tensor_scalar(pos_i[:, :, :], pos_i[:, :, :], 7, None, ALU.logical_shift_right))
            rlink(dve.tensor_copy(pos_a[:, :, :], pos_i[:, :, :]))
            rlink(dve.tensor_scalar(pos_b[:, :, :], pos_a[:, :, :], -float(P), None, ALU.mult))
            rlink(dve.tensor_tensor(pos_b[:, :, :], pos_b[:, :, :], pos_k[:, :, :], ALU.add))
            NP = T * TOPK
            pa = pos_a[:, :, :].rearrange("p t k -> p (t k)")
            pb = pos_b[:, :, :].rearrange("p t k -> p (t k)")
            rlink(dve.tensor_tensor(oneh_a, iota_p[:, None, 0:J].broadcast_to([P, NP, J]),
                                    pa[:, :, None].broadcast_to([P, NP, J]), ALU.is_equal))
            rlink(dve.tensor_tensor(oneh_b, iota_p[:, None, :].broadcast_to([P, NP, P]),
                                    pb[:, :, None].broadcast_to([P, NP, P]), ALU.is_equal))
            dve.tensor_tensor(val_a[:, :, 0:J].rearrange("p (t k) j -> p t k j", k=TOPK),
                              oneh_a.rearrange("p (t k) j -> p t k j", k=TOPK),
                              tok_id[:, :, None, None].broadcast_to([P, T, TOPK, J]), ALU.mult)\
                .then_inc(s["oneh_ready"], 1)
            rlink(dve.tensor_tensor(tile_cmp[:, :, :], iota_p[:, 0:J, None].broadcast_to([P, J, E]),
                                    last_tile[:, None, :].broadcast_to([P, J, E]), ALU.is_ge))
            rlink(dve.tensor_reduce(tile_exp[:, :], tile_cmp[:, :, :], AX.X, ALU.add))
            rlink(dve.tensor_scalar(tile_exp[:, :], tile_exp[:, :], float(E - 1), None, ALU.min))
            rlink(dve.tensor_tensor(tile_oh[:, :, :], iota_p[:, None, 0:E].broadcast_to([P, J, E]),
                                    tile_exp[:, :, None].broadcast_to([P, J, E]), ALU.is_equal))
            rlink(dve.tensor_copy(tile_off[:, :], tile_exp[:, :]))
            dve.wait_ge(s["slots_ps"], 1)
            rlink(dve.tensor_copy(slot_tok[:, :], bk7[:, 64:64 + J]))
            rlink(dve.tensor_scalar(slot_pad[:, :], slot_tok[:, :], 0.0, None, ALU.is_equal))
            rlink(dve.tensor_scalar(idx_get[:, :], slot_tok[:, :], -1.0, 0.0, ALU.add, ALU.max))
            rlink(dve.tensor_scalar(slot_tmp[:, :], slot_tok[:, :], -1.0, None, ALU.add))
            rlink(dve.tensor_scalar(slot_tok[:, :], slot_pad[:, :], row_id[:, 0:1], None, ALU.mult))
            rlink(dve.scalar_tensor_tensor(out=slot_pad[:, :], in0=slot_pad[:, :], scalar=float(TOK + 1),
                                           in1=slot_tok[:, :], op0=ALU.mult, op1=ALU.add))
            dve.tensor_tensor(idx_put[:, :], slot_tmp[:, :], slot_pad[:, :], ALU.add).then_inc(s["idx_ready"], 1)
            dve.wait_ge(s["idx_ready"], 1)

            def slots(j, par):
                static = isinstance(j, int)
                dve.wait_ge(gathered[par], 16 * ((j - par) // 2 + 1) if static else 8 * (j - par) + 16)
                oh = tile_oh[:, j, :] if static else tile_oh[:, bass.ds(j, 1), :].rearrange("p u e -> p (u e)")
                if not static or j >= 1:
                    dve.wait_ge(s["sc_ready"], j)
                dve.tensor_tensor(score_w[:, :], gx[par][:, D:XR], oh, ALU.mult).then_inc(s["sc_tmp"], 1)
                dve.wait_ge(s["sc_tmp"], j + 1)
                dve.tensor_reduce(slot_score[par][:, :], score_w[:, :], AX.X, ALU.add).then_inc(s["sc_ready"], 1)
                dve.wait_ge(s["gt_hi"], j + 1)
                dve.tensor_tensor(gT_lo[par], bk6[:, 0:KD * P], gT_hi[par], ALU.subtract).then_inc(s["gt_lo"], 1)

            slots(0, 0)

            def step(j, par):
                static = isinstance(j, int)
                if not static or j < J:
                    for c in range(2):
                        dve.wait_ge(s["silu_done"], 2 * j + c + 1)
                        dve.scalar_tensor_tensor(out=hid[par].rearrange("p (c n) -> p c n", c=2)[:, c, :],
                                                 in0=h3_ps[:, c, :], scalar=slot_score[par][:, 0:1],
                                                 in1=sil[par].rearrange("p (c n) -> p c n", c=2)[:, c, :],
                                                 op0=ALU.mult, op1=ALU.mult).then_inc(s["h_ready"], 1)
                    if not static or j + 1 < J:
                        slots(j + 1, 1 - par)
                if not static or j >= 1:
                    q = 1 - par
                    dve.wait_ge(s["y_ps"], j)
                    if not static or j >= 3:
                        dve.wait_ge(s["put_done"], 16 * (j - 2))
                    dve.tensor_copy(y_sb[q], bk7[:, 0:D]).then_inc(s["y_ready"], 1)
                if not static or j < J:
                    dve.wait_ge(s["ht_hi"], j + 1)
                    dve.tensor_tensor(hT_lo[par], hT_ps, hT_hi[par], ALU.subtract).then_inc(s["ht_lo"], 1)

            expert_steps(dve, step)

        @block.tensor
        def _(pe):
            pe.wait_ge(s["consts"], N_CONST_EARLY)
            pe.wait_ge(s["prep_loads"], 16 * PREP_DMAS)
            idt = ident[:, :]
            for k in range(KD):
                ins = pe.transpose(bk6[:, k * P:(k + 1) * P], ctx_n[:, k * P:(k + 1) * P], idt)
            ins.then_inc(s["ctxT_ps"], 1)
            for k in range(KD):
                ins = pe.transpose(bk7[:, k * E:(k + 1) * E], gate_n[:, k * P:(k + 1) * P], ident[0:E, 0:E])
            ins.then_inc(s["gT_ps"], 1)
            for k in range(KD):
                for r in range(4):
                    ins = pe.transpose(sc_ps[0][:, k * 512 + r * P:k * 512 + (r + 1) * P],
                                       prep[:, 2 + r, k * P:(k + 1) * P], idt)
            ins.then_inc(s["wkvT_ps"], 1)
            for k in range(KD):
                for r in range(2):
                    ins = pe.transpose(pt_ps2[:, k * D + r * P:k * D + (r + 1) * P], wo_n[:, r, k * P:(k + 1) * P], idt)
            ins.then_inc(s["woT_ps"], 1)
            pe.wait_ge(s["ctxT_sb"], 9)
            pe.wait_ge(s["wkvT_sb"], 2)
            for c in range(2):
                for k in range(KD):
                    ins = pe.matmul(bk6[:, 256 + c * P:256 + (c + 1) * P], wkvT[:, k, c * P:(c + 1) * P], ctxT[:, k, :],
                                    start=k == 0, stop=k == KD - 1)
            ins.then_inc(s["kT_ps"], 1)
            pe.wait_ge(s["gT_sb"], 1)
            for b in range(B):
                if b:
                    pe.wait_ge(s["v_sb"], 4)
                vp = bk7[:, 0:D] if b == 0 else bk7[:, 256:512]
                for k in range(KD):
                    pe.matmul(vp, ctxD[:, k, b, :], wkvT[:, k, 2 * P:4 * P], start=k == 0, stop=False)
                pe.matmul(vp, ones_row[:, :], bv_row[:, :], start=False, stop=True).then_inc(s["v_ps"], 1)
            pe.wait_ge(s["kblk"], 4)
            for n in range(8):
                b, c, k = n // 4, n // 2 % 2, n % 2
                if n >= 4:
                    pe.wait_ge(s["a_lo_s"], n - 3)
                pe.matmul(a_bank(n), prep[:, c, k * P:(k + 1) * P], k_blk[c][:, b, :], start=True, stop=True)\
                    .then_inc(s["a_ps"], 1)
            pe.wait_ge(s["prep_dve"], BQ_DONE)
            pe.wait_ge(s["prep_act"], 1)
            pe.wait_ge(s["woT_sb"], 1)
            for n in range(2 * B):
                b, c = n // 2, n % 2
                if n >= 2:
                    pe.wait_ge(s["beta_sb"], n - 1)
                o = pt_ps2[0:PARTS, c * HS:(c + 1) * HS]
                pe.matmul(o, bq_sel[:, c, :], k_blk[c][:, b, :], start=True, stop=False)
                pe.matmul(o.rearrange("p (h s) -> p h s", h=8), parts_sel[:, :],
                          ab_row[:, None, b * S2:(b + 1) * S2].broadcast_to([1, 8, S2]), start=False, stop=True)\
                    .then_inc(s["beta_ps"], 1)
            pe.wait_ge(s["v_sb"], 8)
            pe.matmul(bk7[0:PARTS, 0:D], parts_sel[:, :], bo_row[:, :], start=True, stop=True).then_inc(s["bo_ps"], 1)

            def x_transpose(tt, par):
                pe.wait_ge(s["xn_ready"], tt + 1)
                for k in range(KD):
                    ins = pe.transpose(bk6[:, k * P:(k + 1) * P], xn[par][:, k * P:(k + 1) * P], idt)
                ins.then_inc(s["xt_ps"], 1)

            def scores_half(par, c):
                o = sc_ps[par][:, c * HS:(c + 1) * HS]
                cols = slice(c * HS, (c + 1) * HS)
                first = True
                for k in range(KD):
                    kk = slice(k * P, (k + 1) * P)
                    for l, r in ((xT_hi, a_hi), (xT_hi, a_lo), (xT_lo, a_hi)):
                        pe.matmul(o, l[par][:, kk], r[par][:, k, cols], start=first, stop=False)
                        first = False
                return pe.matmul(o, ones16[0:PARTS, :], beta[:, par, cols], start=False, stop=True)

            pe.wait_ge(s["kT_ps"], 1)
            pe.wait_ge(s["kblk"], 4)
            x_transpose(0, 0)

            def step(u, par, t):
                tt = 2 * u + par
                if here(t, 2):
                    bp = par
                    bt = tt - 2
                    pe.wait_ge(s["pt_sb"], 2 * (bt + 1))
                    if t is None or bt >= 1:
                        pe.wait_ge(s["x2_ready"], bt)
                    else:
                        pe.wait_ge(s["bo_sb"], 1)
                    for j in range(8):
                        ins = pe.matmul(bk7[:, j * 2 * NOUT:(j + 1) * 2 * NOUT], probT[bp][:, j * P:(j + 1) * P],
                                        v_blk[:, bp, j, :], start=True, stop=True)
                    ins.then_inc(s["o_ps"], 1)
                if here(t, 0):
                    pe.wait_ge(s["xt_lo"], tt + 1)
                    if t is None or t >= 2:
                        pe.wait_ge(s["ssub"], tt - 1)
                    elif t == 0:
                        pe.wait_ge(s["a_lo_s"], 8)
                        pe.wait_ge(s["beta_sb"], 4)
                    scores_half(par, 0)
                if here(t, 3):
                    bp = 1 - par
                    bt = tt - 3
                    pe.wait_ge(s["xn2_ready"], bt + 1)
                    for k in range(KD):
                        ins = pe.transpose(bk6[:, k * P:(k + 1) * P], xn2[bp][:, k * P:(k + 1) * P], idt)
                    ins.then_inc(s["x2t_ps"], 1)
                if here(t, 2):
                    bt = tt - 2
                    pe.wait_ge(s["o_norm"], bt + 1)
                    for k in range(KD):
                        ins = pe.transpose(bk7[:, k * P:(k + 1) * P], o_sb[:, k * P:(k + 1) * P], idt)
                    ins.then_inc(s["ot_ps"], 1)
                if here(t, 0):
                    scores_half(par, 1).then_inc(s["s_ps"], 1)
                if here(t, 3):
                    bt = tt - 3
                    pe.wait_ge(s["x2t_sb"], bt + 1)
                    for k in range(KD):
                        ins = pe.matmul(bk6[:, 256:256 + E], xn2T[:, k * P:(k + 1) * P], gateT[:, k, :],
                                        start=k == 0, stop=k == KD - 1)
                    ins.then_inc(s["logit_ps"], 1)
                if here(t, 2):
                    bt = tt - 2
                    pe.wait_ge(s["ot_sb"], bt + 1)
                    for k in range(KD):
                        pe.matmul(bk7[:, 0:D], oT[:, k * P:(k + 1) * P], woT[:, k, :], start=k == 0, stop=False)
                    pe.matmul(bk7[:, 0:D], ones16[0:PARTS, :], bo_parts[:, :], start=False, stop=True)\
                        .then_inc(s["attn_ps"], 1)
                if here(t, 1):
                    bu, bp = back(u, par, 1)
                    bt = tt - 1
                    pe.wait_ge(s["p_exp"], bt + 1)
                    for c in range(2):
                        if t is None or bt >= 1:
                            pe.wait_ge(s["pt_sb"], 2 * bt)
                        for q in range(4):
                            j = 4 * c + q
                            ins = pe.transpose(pt_ps2[:, j * P:(j + 1) * P], prob[bp][:, j * P:(j + 1) * P], idt)
                        ins.then_inc(s["pt_ps"], 1)
                if here(t, -1):
                    if t is None or t >= 3:
                        pe.wait_ge(s["logit_sb"], tt - 2)
                    pe.wait_ge(s["xt_lo"], tt + 1)
                    x_transpose(tt + 1, 1 - par)

            attention_steps(pe, step)

            pe.wait_ge(s["selected"], 1)
            def earlier_partitions(start):
                ins = pe.matmul(bk6[:, 0:T * E], before_half[:, :], sel16[:, :, :].rearrange("p t e -> p (t e)"),
                                start=start, stop=not start, skip_group_check=True)
                return ins

            earlier_partitions(True)
            for t in range(T - 1):
                pe.matmul(bk6[:, (t + 1) * E:T * E].rearrange("p (t e) -> p t e", e=E), ones16[:, :],
                          sel16[:, t:t + 1, :].broadcast_to([P, T - 1 - t, E]), start=False, stop=False,
                          skip_group_check=True)
            earlier_partitions(False)
            for t in range(T):
                ins = pe.matmul(bk7[:, 0:E], ones16[:, :], sel16[:, t, :], start=t == 0, stop=t == T - 1)
            ins.then_inc(s["prefix_ps"], 1)
            pe.wait_ge(s["oneh_ready"], 1)
            for n in range(T * TOPK):
                ins = pe.matmul(bk7[:, 64:64 + J], oneh_b[:, n, :], val_a[:, n, 0:J], start=n == 0,
                                stop=n == T * TOPK - 1)
            ins.then_inc(s["slots_ps"], 1)
            pe.wait_ge(s["idx_ready"], 1)
            pe.wait_ge(s["wlo"], T)

            def x_rows(j, par, j1):
                pe.wait_ge(gathered[par], j1)
                if not isinstance(j, int) or j >= 1:
                    pe.wait_ge(s["gt_lo"], j)
                for k in range(KD):
                    ins = pe.transpose(bk6[:, k * P:(k + 1) * P], gx[par][:, k * P:(k + 1) * P], idt)
                ins.then_inc(s["gt_ps"], 1)

            x_rows(0, 0, 16)

            def step(j, par):
                static = isinstance(j, int)
                q = 1 - par
                if not static or j < J:
                    col = slice(j, j + 1) if static else bass.ds(j, 1)
                    e = pe.value_load(tile_off[0:1, col], min_val=0, max_val=E - 1)
                    pe.wait_ge(s["gt_lo"], j + 1)
                    if not static or j >= 1:
                        pe.wait_ge(s["h_ready"], 2 * j)
                    for c in range(2):
                        for ps, half in ((h1_ps, 0), (h3_ps, 1)):
                            for k in range(KD):
                                kk = slice(k * P, (k + 1) * P)
                                cols = bass.ds(e * WE + (half * HALF + k * F + c * FH), FH)
                                pe.matmul(ps[:, c, :], gT_hi[par][:, kk], w_hi[:, cols], start=k == 0, stop=False)
                                pe.matmul(ps[:, c, :], gT_lo[par][:, kk], w_hi[:, cols], start=False, stop=False)
                                ins = pe.matmul(ps[:, c, :], gT_hi[par][:, kk], w_lo[:, cols], start=False,
                                                stop=k == KD - 1)
                        ins.then_inc(s["h_ps"], 1)
                if not static or j + 1 < J:
                    x_rows(j + 1, q, 16 * ((j + 1 - q) // 2 + 1) if static else 8 * (j + 1 - q) + 16)
                if not static or j >= 1:
                    colp = slice(j - 1, j) if static else bass.ds(j - 1, 1)
                    ep = pe.value_load(tile_off[0:1, colp], min_val=0, max_val=E - 1)
                    pe.wait_ge(s["ht_lo"], j)
                    if not static or j >= 2:
                        pe.wait_ge(s["y_ready"], j - 1)
                    for c in range(KF):
                        rows = P if c < KF - 1 else FL
                        off = W13 + c * D if c < KF // 2 else HALF + W13 + (c - KF // 2) * D
                        cc = slice(c * P, (c + 1) * P)
                        cols = bass.ds(ep * WE + off, D)
                        pe.matmul(bk7[:, 0:D], hT_hi[q][0:rows, cc], w_hi[0:rows, cols], start=c == 0, stop=False)
                        pe.matmul(bk7[:, 0:D], hT_lo[q][0:rows, cc], w_hi[0:rows, cols], start=False, stop=False)
                        ins = pe.matmul(bk7[:, 0:D], hT_hi[q][0:rows, cc], w_lo[0:rows, cols], start=False,
                                        stop=c == KF - 1)
                    ins.then_inc(s["y_ps"], 1)
                if not static or j < J:
                    pe.wait_ge(s["h_ready"], 2 * (j + 1))
                    if not static or j >= 1:
                        pe.wait_ge(s["ht_lo"], j)
                    for c in range(KF):
                        rows = P if c < KF - 1 else FL
                        ins = pe.transpose(hT_ps[0:rows, c * P:(c + 1) * P], hid[par][:, c * P:c * P + rows], idt)
                    ins.then_inc(s["ht_ps"], 1)

            expert_steps(pe, step)


N_CONST = 22
N_CONST_EARLY = 14
AB_DONE = 2
RSQRT_OPS = 12
BQ_DONE = 4
PREP_DMAS = 3 + 13

_INS = ["x", "ctx_1024", "fside_BxS2_0", "L0_xattn_in_proj_weight", "L0_xattn_in_proj_bias",
        "L0_xattn_out_proj_weight", "L0_xattn_out_proj_bias", "L0_ffn_gate_w", "L0_ffn_expert_bias",
        "L0_ffn_w1", "L0_ffn_w2", "L0_ffn_w3"]


def kernel(**inputs):
    import numpy as _np
    import concourse.bacc as _bacc
    from concourse import mybir as _mybir
    from concourse.bass_utils import run_bass_kernel_spmd as _run

    nc = _bacc.Bacc("TRN2", target_bir_lowering=False, num_devices=1)
    arrays, args = {}, []
    for name in _INS:
        a = _np.ascontiguousarray(inputs[name])
        arrays[f"in_{name}"] = a
        args.append(nc.dram_tensor(f"in_{name}", a.shape, _mybir.dt.from_np(a.dtype), kind="ExternalInput").ap())
    shape = inputs["x"].shape
    args.append(nc.dram_tensor("out_0", shape, _mybir.dt.float32, kind="ExternalOutput").ap())
    xattn_moe(nc, *args)
    r = _run(nc, [arrays], core_ids=[0])
    return r.results[0]["out_0"]
```

```python
from contextlib import ExitStack

import concourse.bass as bass
from concourse import mybir

ALU = mybir.AluOpType
ACT = mybir.ActivationFunctionType
F32 = mybir.dt.float32
F16 = mybir.dt.float16
I32 = mybir.dt.int32
AX = mybir.AxisListType

P = 128
LN_EPS = 1e-5
TINY = 1.2e-38
PARTS = 96


def xattn_moe(nc, x, ctx_in, abundance, w_in, b_in, w_out, b_out, gate_w, expert_bias, w1, w2, w3, out):
    B, N, D = x.shape
    S2 = ctx_in.shape[1]
    HD = 16
    H = D // HD
    E, _, F = w1.shape
    KD = D // P
    KF = (F + P - 1) // P
    FL = F - (KF - 1) * P
    UT = N // P
    T = B * UT
    TOK = B * N
    SL = H * S2
    HS = SL // 2
    TOPK = 2
    J = (TOK * TOPK + E * (P - 1)) // P
    NOUT = HD + 1
    W13 = KD * F
    W2H = KF // 2 * D
    HALF = W13 + W2H
    WE = 2 * HALF
    FH = F // 2
    XR = D + E
    assert B == 2 and KD == 2 and E == 8 and UT == 8 and KF == 6

    with ExitStack() as stack:
        def sb(name, shape, dt=F32):
            return stack.enter_context(nc.sbuf_tensor(name, shape, dt))

        def sem(name):
            return stack.enter_context(nc.semaphore(name))

        table = nc.dram_tensor("table", [TOK, XR], F32, kind="Internal").ap()
        acc = nc.dram_tensor("acc", [TOK + P, D], F32, kind="Internal").ap()
        table_v = table.rearrange("(b u p) d -> b u p d", b=B, p=P)
        acc_v = acc[0:TOK, :].rearrange("(b u p) d -> b u p d", b=B, p=P)

        w_hi = sb("w_hi", [P, E * WE], F16)
        w_lo = sb("w_lo", [P, E * WE], F16)
        ARENA = T * D + B * KD * SL
        arena = sb("arena", [P, ARENA])
        stage = [sb("stage_w13", [P, W13]), sb("stage_w2", [P, W2H])]

        class Region:

            def __init__(self, base, start=0):
                self.base, self.at = base, start

            def __call__(self, cols, dt=F32):
                words = cols if dt != F16 else (cols + 1) // 2
                assert self.at + words <= self.base.shape[-1], (self.at, words)
                a = self.base[:, self.at:self.at + words]
                self.at += words
                return a if dt == F32 else a.bitcast(dt)

        take = Region(arena)
        xs = take(T * D).rearrange("p (t d) -> p t d", t=T)
        a_hi = [take(KD * SL, F16).rearrange("p (k n) -> p k n", k=KD) for _ in range(B)]
        a_lo = [take(KD * SL, F16).rearrange("p (k n) -> p k n", k=KD) for _ in range(B)]
        take = Region(w_hi[:, (E - 1) * WE:E * WE].bitcast(F32))
        prob = [take(SL) for _ in range(2)]
        take = Region(w_lo[:, (E - 1) * WE:E * WE].bitcast(F32))
        probT = [take(SL) for _ in range(2)]
        xn = [sb(f"xn{i}", [P, D]) for i in range(2)]
        xn2 = [sb(f"xn2{i}", [P, D]) for i in range(2)]

        take = Region(arena)
        oneh_b = take(T * TOPK * P, F16).rearrange("p (n s) -> p n s", s=P)
        oneh_a = take(T * TOPK * J).rearrange("p (n j) -> p n j", j=J)
        val_a = take(T * TOPK * (J + 1), F16).rearrange("p (n j) -> p n j", j=J + 1)
        rank_w = take(T * E * E).rearrange("p (t e f) -> p t e f", t=T, e=E)
        rank_w2 = take(T * E * E).rearrange("p (t e f) -> p t e f", t=T, e=E)
        r_small = [take(T * E).rearrange("p (t e) -> p t e", t=T) for _ in range(7)]
        tile_oh = take(J * E).rearrange("p (j e) -> p j e", j=J)
        tile_cmp = take(J * E).rearrange("p (j e) -> p j e", j=J)
        count_w = take(E * T).rearrange("p (e t) -> p e t", e=E)
        ee_w = take(E * E).rearrange("p (e f) -> p e f", e=E)
        n_tiles, first_tile, last_tile = take(E), take(E), take(E)
        tile_exp, slot_tok, slot_pad, slot_tmp = take(J), take(J), take(J), take(J)
        tile_off, idx_get, idx_put = (take(J).bitcast(I32) for _ in range(3))
        pos_k, pos_b, pos_a = (take(T * TOPK).rearrange("p (t k) -> p t k", k=TOPK) for _ in range(3))
        t_max, t_sum = take(T), take(T)
        pos_i = take(T * TOPK).bitcast(I32).rearrange("p (t k) -> p t k", k=TOPK)

        take = Region(arena)
        hid = [take(F) for _ in range(2)]
        sil = [take(F) for _ in range(2)]
        hT_hi = [take(KF * P, F16) for _ in range(2)]
        hT_lo = [take(KF * P, F16) for _ in range(2)]
        y_sb = [take(D) for _ in range(2)]
        gx = [take(XR) for _ in range(2)]
        gT_hi = [take(KD * P, F16) for _ in range(2)]
        gT_lo = [take(KD * P, F16) for _ in range(2)]
        assert take.at <= 5984
        score_w = sb("score_w", [P, E])
        slot_score = [sb(f"slot_score{i}", [P, 1]) for i in range(2)]
        get_now = [sb(f"get_now{i}", [P, 1], I32) for i in range(2)]
        put_now = [sb(f"put_now{i}", [P, 1], I32) for i in range(2)]

        ident = sb("ident", [P, P])
        ones16 = sb("ones16", [P, P], F16)
        before_half = sb("before_half", [P, P], F16)
        iota_p = sb("iota_p", [P, P])
        tok_id = sb("tok_id", [P, T])
        row_id = sb("row_id", [P, 1])
        lower = sb("lower", [P, E, E])
        tile_edge = sb("tile_edge", [P, E, T])

        gateT = sb("gateT", [P, KD, E])
        woT = sb("woT", [P, KD, D])
        v_blk = sb("v_blk", [P, B, 8, 2 * NOUT])
        beta = sb("beta", [PARTS, B, SL], F16)
        bo_parts = sb("bo_parts", [PARTS, D], F16)
        ebias = sb("ebias", [P, E])

        take = Region(w_hi[:, 3 * WE:(E - 1) * WE].bitcast(F32))
        prep = take(6 * D).rearrange("p (r d) -> p r d", r=6)
        wo_n = take(2 * D).rearrange("p (r d) -> p r d", r=2)
        ctx_n = take(D)
        wkvT = take(KD * 4 * P).rearrange("p (k n) -> p k n", k=KD)
        k_blk = [take(B * HS).rearrange("p (b n) -> p b n", b=B) for _ in range(2)]
        ctxT = take(KD * P).rearrange("p (k n) -> p k n", k=KD)
        ctxD = take(KD * B * P).rearrange("p (k b n) -> p k b n", k=KD, b=B)
        kT = take(2 * P).rearrange("p (c n) -> p c n", c=2)
        gate_n = take(D)[0:E]
        bias_qk = take(4)
        bq_sel = take(2 * PARTS).rearrange("p (c n) -> p c n", c=2)
        bv_row = take(D)[0:1]
        take = Region(w_lo[:, 3 * WE:(E - 1) * WE].bitcast(F32))
        bo_row = take(D)[0:1]
        ab_row = take(B * S2)[0:1]
        ab_col = take(B)
        ab_mask = take(B)
        beta_res = [take(HS)[0:PARTS] for i in range(2)]
        ones_row = take(P)[0:1]
        parts_sel = take(PARTS)[0:1]
        head_mask = take(8)
        zero_rows = take(D)

        st_all = take(T * 6).rearrange("p (t n) -> p t n", t=T)
        mv_all = sb("mv_all", [P, T, 2])
        rs_all = sb("rs_all", [P, T])
        rsw = sb("rsw", [P, 3 * T])
        st2 = sb("st2", [P, 6])
        mv2 = sb("mv2", [P, 2])
        rs2 = sb("rs2", [P, 1])
        rsw2 = sb("rsw2", [P, 3])
        xT_hi = [sb(f"xThi{i}", [P, KD * P], F16) for i in range(2)]
        xT_lo = [sb(f"xTlo{i}", [P, KD * P], F16) for i in range(2)]
        top = sb("top", [P, H])
        o_inv = sb("o_inv", [P, H])
        o_sb = sb("o_sb", [P, D])
        oT = sb("oT", [P, KD * P])
        xn2T = sb("xn2T", [P, KD * P])
        logits = sb("logits", [P, T, E])
        sel16 = sb("sel16", [P, T, E], F16)

        bank = [stack.enter_context(nc.psum_tensor(f"bank{i}", [P, 512], F32)) for i in range(2)]
        sc_ps = [stack.enter_context(nc.psum_tensor(f"sc{i}", [P, 1024], F32)) for i in range(2)]
        pt_ps2 = stack.enter_context(nc.psum_tensor("ptps", [P, 1024], F32))
        bk6, bk7 = bank
        LG = 288
        h1_ps = sc_ps[0][:, :].rearrange("p (c n) -> p c n", c=2)[:, :, 0:FH]
        h3_ps = sc_ps[1][:, :].rearrange("p (c n) -> p c n", c=2)[:, :, 0:FH]
        hT_ps = pt_ps2[:, 0:KF * P]

        names = """consts prep_loads x_loads w_loads0 w_loads1 xn2_st0 xn2_st1 x2_st0 x2_st1 score_st zero_st
            ctxT_ps ctxT_sb wkvT_ps wkvT_sb woT_ps woT_sb gT_ps gT_sb kT_ps kT_sb kblk v_ps v_sb a_ps a_hi_s a_lo_s
            beta_ps beta_sb bo_ps bo_sb prep_dve prep_act
            ln1_stats ln1_mv ln1_rstd xn_ready xt_ps xt_hi xt_lo s_ps smax ssub p_exp pt_ps pt_sb
            o_ps o_recip o_norm ot_ps ot_sb attn_ps x2_ready ln2_stats ln2_mv ln2_rstd xn2_ready
            x2t_ps x2t_sb logit_ps logit_sb whi wlo
            route exp_in exp_out scores_in selected prefix_ps oneh_ready slots_ps idx_ready
            get_idx gat0 gat1 put_idx put_done sc_tmp sc_ready gt_ps gt_hi gt_lo h_ps silu_done h_ready ht_ps ht_hi ht_lo
            y_ps y_ready copied carried_dve carried_pool""".split()
        s = {n: sem(n) for n in names}
        w_loads = [s["w_loads0"], s["w_loads1"]]
        xn2_st = [s["xn2_st0"], s["xn2_st1"]]
        x2_st = [s["x2_st0"], s["x2_st1"]]
        gathered = [s["gat0"], s["gat1"]]
        LOADS = 12

        def back(u, par, k):
            return u + (par - k) // 2, (par - k) % 2

        def attention_steps(eng, step):
            for t in range(6):
                step(t // 2, t % 2, t)
            with eng.Fori(3, UT - 1) as u:
                step(u, 0, None)
                step(u, 1, None)
            for t in range(T - 2, T + 4):
                step(t // 2, t % 2, t)

        HALVES = [(e, g) for e in range(3) for g in range(2)] + [(3, 1), (4, 1), (5, 1)] \
            + [(e, 0) for e in range(3, 7)] + [(6, 1), (7, 0), (7, 1)]
        PIECES = 2 * len(HALVES)
        AHEAD = PIECES - 4 - T

        def piece_columns(n, u=None):
            kind = n % 2
            width = (W13, W2H)[kind]
            if u is not None:
                return bass.ds(u * WE + kind * W13, width)
            e, g = HALVES[n // 2]
            at = e * WE + g * HALF + kind * W13
            return slice(at, at + width)

        def piece_at(u, par, t):
            return par, piece_columns(par, u) if t is None else piece_columns(AHEAD + t)

        def here(t, lag):
            return t is None or 0 <= t - lag < T

        def expert_steps(eng, step):
            for j in range(3):
                step(j, j % 2)
            with eng.Fori(1, (J - 3) // 2) as v:
                step(2 * v + 1, 1)
                step(2 * v + 2, 0)
            for j in range(J - 2, J + 1):
                step(j, j % 2)

        def carry(eng):
            eng.sem_inc(s["carried_dve" if eng.engine == nc.vector.engine else "carried_pool"], 1)

        def rsqrt(eng, r, v, ve, w, w2, chain, base):
            n = [0]

            def go(ins):
                n[0] += 1
                ins.then_inc(s[chain], 1)
                eng.wait_ge(s[chain], base + n[0])

            def scalar_op(*operands):
                if not isinstance(base, int):
                    carry(eng)
                go(eng.tensor_scalar(*operands))

            scalar_op(ve, v, LN_EPS, None, ALU.add)
            scalar_op(r.bitcast(I32), ve.bitcast(I32), -0.5, float(0x5F3759DF), ALU.mult, ALU.add)
            for _ in range(2):
                go(eng.tensor_tensor(w, r, r, ALU.mult))
                go(eng.tensor_tensor(w, w, ve, ALU.mult))
                scalar_op(w2, w, 0.375, -1.25, ALU.mult, ALU.add)
                go(eng.tensor_tensor(w2, w2, w, ALU.mult))
                scalar_op(w2, w2, 1.875, None, ALU.add)
                go(eng.tensor_tensor(r, r, w2, ALU.mult))
            assert n[0] == RSQRT_OPS

        def a_bank(n):
            return sc_ps[n // 2 % 2][:, n % 2 * 512:n % 2 * 512 + HS]

        assert J % 2 == 1
        block = stack.enter_context(nc.Block())

        @block.sync
        def _(sp):
            sp.dma_start(ctx_n, ctx_in.rearrange("b s d -> (b s) d")).then_inc(s["prep_loads"], 16)
            sp.dma_start(prep, w_in.rearrange("(r p) d -> p r d", p=P)).then_inc(s["prep_loads"], 16)
            sp.dma_start(wo_n, w_out.rearrange("(r p) d -> p r d", p=P)).then_inc(s["prep_loads"], 16)
            sp.wait_ge(s["prep_loads"], 16 * PREP_DMAS)
            for b in range(B):
                sp.dma_start(xs[:, b:T:2, :], x[b].rearrange("(u p) d -> p u d", p=P)).then_inc(s["x_loads"], 16)

            def load(n, count, u=None):
                kind = n % 2
                e, g = HALVES[n // 2]
                if u is not None:
                    e, g = bass.ds(u, 1), 0
                if u is not None or n >= 2:
                    sp.wait_ge(s["whi"], count - 1)
                    sp.wait_ge(s["wlo"], count - 1)
                dst = stage[kind]
                if kind == 0:
                    src = (w1, w3)[g][e]
                    src = src.rearrange("(k p) f -> p k f", p=P) if u is None else src.rearrange("e (k p) f -> p (e k) f", p=P)
                    sp.dma_start(dst.rearrange("p (k f) -> p k f", k=KD), src).then_inc(w_loads[0], 16)
                    return
                src = w2[e] if u is None else w2[e].rearrange("e f d -> (e f) d")
                c0 = g * KF // 2 * P
                full = KF // 2 - 1
                rows = P if g == 0 else FL
                sp.dma_start(dst[:, 0:full * D].rearrange("p (c d) -> p c d", c=full),
                             src[c0:c0 + full * P, :].rearrange("(c p) d -> p c d", p=P)).then_inc(w_loads[1], 16)
                c0 += full * P
                sp.dma_start(dst[0:rows, full * D:W2H], src[c0:c0 + rows, :]).then_inc(w_loads[1], 16)

            for n in range(2):
                load(n, n)
            sp.wait_ge(s["consts"], N_CONST_EARLY)
            sp.dma_start(acc[TOK:TOK + P, :], zero_rows).then_inc(s["zero_st"], 16)
            for n in range(2, AHEAD + 1):
                load(n, n)

            def step(u, par, t):
                if t is None:
                    n = AHEAD + 2 * u + par + 1
                    load(1 - par, n, u + par)
                elif t < T:
                    load(AHEAD + t + 1, AHEAD + t + 1)
                if here(t, 2):
                    bu, bt = u - 1, 2 * u + par - 2
                    if t is None:
                        acc_d = acc_v[par, bass.ds(bu, 1)].rearrange("u p d -> p (u d)")
                        x_s = xs[:, bass.ds(bt, 1), :].rearrange("p u d -> p (u d)")
                    else:
                        acc_d, x_s = acc_v[par, bu], xs[:, bt, :]
                    sp.wait_ge(s["x2_ready"], bt + 1)
                    sp.dma_start(acc_d, x_s).then_inc(x2_st[par], 16)
                if here(t, 3):
                    bu, bp = back(u, par, 3)
                    bt = 2 * bu + bp
                    if t is None:
                        tab_d = table_v[bp, bass.ds(bu, 1), :, 0:D].rearrange("u p d -> p (u d)")
                    else:
                        tab_d = table_v[bp, bu, :, 0:D]
                    sp.wait_ge(s["xn2_ready"], bt + 1)
                    sp.dma_start(tab_d, xn2[bp][:, :]).then_inc(xn2_st[bp], 16)

            attention_steps(sp, step)
            for n in range(AHEAD + T + 1, PIECES):
                load(n, n)
            sp.wait_ge(s["scores_in"], 1)
            for b in range(B):
                sp.dma_start(table_v[b, :, :, D:XR].rearrange("u p e -> p u e"),
                             r_small[0][:, b:T:2, :]).then_inc(s["score_st"], 16)
            sp.wait_ge(s["put_done"], 16 * J)
            sp.dma_start(out.rearrange("b n d -> (b n) d"), acc[0:TOK, :]).then_inc(s["copied"], 16)
            sp.wait_ge(s["copied"], 16)

        @block.gpsimd
        def _(pool):
            n_c = [0]

            def const(ins):
                n_c[0] += 1
                ins.then_inc(s["consts"], 1)
                pool.wait_ge(s["consts"], n_c[0])

            const(pool.memset(ident[:, :], 0.0))
            const(pool.affine_select(out=ident[:, :], in_=ident[:, :], compare_op=ALU.not_equal, fill=1.0, base=0,
                                     pattern=[[-1, P]], channel_multiplier=1))
            const(pool.memset(ones_row[:, :], 1.0))
            const(pool.memset(ones16[:, :], 1.0))
            const(pool.memset(before_half[:, :], 0.5))
            const(pool.affine_select(out=before_half[:, :], in_=before_half[:, :], compare_op=ALU.is_gt, fill=0.0, base=0,
                                     pattern=[[1, P]], channel_multiplier=-1))
            const(pool.memset(head_mask[:, :], 1.0))
            const(pool.affine_select(out=head_mask[:, :], in_=head_mask[:, :], compare_op=ALU.is_ge, fill=0.0,
                                     base=0, pattern=[[-HD, 8]], channel_multiplier=1))
            const(pool.affine_select(out=head_mask[:, :], in_=head_mask[:, :], compare_op=ALU.is_ge, fill=0.0,
                                     base=HD - 1, pattern=[[HD, 8]], channel_multiplier=-1))
            const(pool.memset(bq_sel[:, :, :], 0.0))
            const(pool.memset(parts_sel[:, :], 0.0))
            const(pool.memset(parts_sel[:, 0:PARTS:32], 1.0))
            const(pool.memset(v_blk[:, :, :, :], 0.0))
            const(pool.memset(zero_rows[:, :], 0.0))
            const(pool.iota(iota_p[:, :], pattern=[[1, P]], base=0, channel_multiplier=0,
                            allow_small_or_imprecise_dtypes=True))
            const(pool.iota(row_id[:, :], pattern=[[0, 1]], base=0, channel_multiplier=1,
                            allow_small_or_imprecise_dtypes=True))
            for b in range(B):
                const(pool.iota(tok_id[:, b:T:2], pattern=[[P, UT]], base=b * N + 1, channel_multiplier=1,
                                allow_small_or_imprecise_dtypes=True))
            const(pool.memset(lower[:, :, :], 1.0))
            const(pool.affine_select(out=lower[:, :, :], in_=lower[:, :, :], compare_op=ALU.is_gt, fill=0.0, base=0,
                                     pattern=[[1, E], [-1, E]], channel_multiplier=0))
            const(pool.iota(tile_edge[:, :, :], pattern=[[0, E], [P, T]], base=0, channel_multiplier=0,
                            allow_small_or_imprecise_dtypes=True))
            assert n_c[0] == N_CONST

            def weights_low(n, kind, cols):
                pool.wait_ge(s["whi"], n + 1)
                pool.tensor_tensor(w_lo[:, cols], stage[kind][:, :], w_hi[:, cols], ALU.subtract).then_inc(s["wlo"], 1)

            for n in range(AHEAD):
                weights_low(n, n % 2, piece_columns(n))

            def step(u, par, t):
                tt = 2 * u + par
                if here(t, 3):
                    bt = tt - 3
                    pool.wait_ge(s["ln2_mv"], bt + 1)
                    rsqrt(pool, rs2[:, :], mv2[:, 1:2], rsw2[:, 0:1], rsw2[:, 1:2], rsw2[:, 2:3], "ln2_rstd",
                          bt * RSQRT_OPS)
                if here(t, 0):
                    weights_low(AHEAD + tt, *piece_at(u, par, t))

            attention_steps(pool, step)
            pool.wait_ge(s["o_ps"], T)
            for n in range(AHEAD + T, PIECES):
                weights_low(n, n % 2, piece_columns(n))
            pool.wait_ge(s["zero_st"], 16)
            for b in range(2):
                pool.wait_ge(x2_st[b], 16 * UT)
                pool.wait_ge(xn2_st[b], 16 * UT)
            pool.wait_ge(s["score_st"], 16 * B)
            pool.wait_ge(s["idx_ready"], 1)

            def gather(j, par, dyn):
                col = bass.ds(j, 1) if dyn else slice(j, j + 1)
                pool.tensor_copy(get_now[par][:, :], idx_get[:, col]).then_inc(s["get_idx"], 1)
                pool.wait_ge(s["get_idx"], j + 1)
                carry(pool)
                pool.indirect_dma_start(out=gx[par], out_offset=None, in_=table[:, :],
                                        in_offset=bass.IndirectOffsetOnAxis(ap=get_now[par][:, 0:1], axis=0))\
                    .then_inc(gathered[par], 16)

            gather(0, 0, False)
            gather(1, 1, False)

            def step(j, par):
                static = isinstance(j, int)
                if not static or j + 2 < J:
                    pool.wait_ge(s["gt_ps"], j + 1)
                    pool.wait_ge(s["sc_tmp"], j + 1)
                    gather(j + 2, par, not static)
                if not static or j >= 1:
                    q = 1 - par
                    col = slice(j - 1, j) if static else bass.ds(j - 1, 1)
                    pool.tensor_copy(put_now[q][:, :], idx_put[:, col]).then_inc(s["put_idx"], 1)
                    pool.wait_ge(s["put_idx"], j)
                    pool.wait_ge(s["y_ready"], j)
                    if not static or j >= 2:
                        pool.wait_ge(s["put_done"], 16 * (j - 1))
                    carry(pool)
                    pool.indirect_dma_start(out=acc[:, :],
                                            out_offset=bass.IndirectOffsetOnAxis(ap=put_now[q][:, 0:1], axis=0),
                                            in_=y_sb[q], in_offset=None, compute_op=ALU.add)\
                        .then_inc(s["put_done"], 16)

            expert_steps(pool, step)

        @block.scalar
        def _(act):
            with nc.allow_non_contiguous_dma(reason="columns of biases"):
                for c in range(4):
                    act.dma_start(bias_qk[:, c:c + 1], b_in[c * P:(c + 1) * P].rearrange("(p a) -> p a", a=1))\
                        .then_inc(s["prep_loads"], 16)
                for b in range(B):
                    for r in range(2):
                        act.dma_start(ab_col[r * S2:(r + 1) * S2, b:b + 1],
                                      abundance[b].rearrange("(p a) -> p a", a=1)).then_inc(s["prep_loads"], 16)
            act.dma_start(gate_n[:, :], gate_w).then_inc(s["prep_loads"], 16)
            act.dma_start(bv_row[:, :], b_in[2 * D:3 * D].rearrange("(a n) -> a n", a=1)).then_inc(s["prep_loads"], 16)
            act.dma_start(bo_row[:, :], b_out.rearrange("(a n) -> a n", a=1)).then_inc(s["prep_loads"], 16)
            act.dma_start(ab_row[:, :], abundance.rearrange("(a b) s -> a (b s)", a=1)).then_inc(s["prep_loads"], 16)
            act.dma_start(ebias[:, :], expert_bias.rearrange("(a n) -> a n", a=1).broadcast_to([P, E]))\
                .then_inc(s["prep_loads"], 16)
            def weights_high(n, kind, cols, rank):
                act.wait_ge(w_loads[kind], (16, 32)[kind] * (rank + 1))
                act.activation(w_hi[:, cols], stage[kind][:, :], ACT.Copy).then_inc(s["whi"], 1)

            act.wait_ge(s["prep_dve"], AB_DONE)
            act.activation(ab_row[:, :], ab_row[:, :], ACT.Ln).then_inc(s["prep_act"], 1)
            act.wait_ge(s["wkvT_ps"], 1)
            act.activation(wkvT[:, 0, :], sc_ps[0][:, 0:4 * P], ACT.Copy).then_inc(s["wkvT_sb"], 1)
            act.activation(wkvT[:, 1, :], sc_ps[0][:, 512:512 + 4 * P], ACT.Copy).then_inc(s["wkvT_sb"], 1)
            act.wait_ge(s["woT_ps"], 1)
            act.activation(woT[:, :, :], pt_ps2[:, 0:2 * D].rearrange("p (k n) -> p k n", k=2), ACT.Copy)\
                .then_inc(s["woT_sb"], 1)
            for n in range(8):
                b, c, k = n // 4, n // 2 % 2, n % 2
                act.wait_ge(s["a_ps"], n + 1)
                act.activation(a_hi[b][:, k, c * HS:(c + 1) * HS], a_bank(n), ACT.Copy).then_inc(s["a_hi_s"], 1)

            def tokens_high(tt, par, static):
                act.wait_ge(s["xt_ps"], tt + 1)
                if not static or tt >= 2:
                    act.wait_ge(s["s_ps"], 2 * (tt - 1))
                act.activation(xT_hi[par][:, :], bk6[:, 0:KD * P], ACT.Copy).then_inc(s["xt_hi"], 1)

            for n in range(AHEAD):
                weights_high(n, n % 2, piece_columns(n), n // 2)
            tokens_high(0, 0, True)

            def step(u, par, t):
                tt = 2 * u + par
                if here(t, 1):
                    act.wait_ge(s["ssub"], tt)
                    act.activation(prob[1 - par], prob[1 - par], ACT.Exp).then_inc(s["p_exp"], 1)
                if here(t, -1):
                    tokens_high(tt + 1, 1 - par, t is not None)
                if here(t, 4):
                    bt = tt - 4
                    act.wait_ge(s["x2t_ps"], bt + 1)
                    if t is None or bt >= 1:
                        act.wait_ge(s["logit_ps"], bt)
                    act.activation(xn2T[:, :], pt_ps2[:, 0:KD * P], ACT.Copy).then_inc(s["x2t_sb"], 1)
                if here(t, 0):
                    weights_high(AHEAD + tt, *piece_at(u, par, t), AHEAD // 2 + u)
                if here(t, 2):
                    bt = tt - 2
                    act.wait_ge(s["ot_ps"], bt + 1)
                    if t is None or bt >= 1:
                        act.wait_ge(s["attn_ps"], bt)
                    act.activation(oT[:, :], bk6[:, KD * P:2 * KD * P], ACT.Copy).then_inc(s["ot_sb"], 1)
                if here(t, 1):
                    bt = tt - 1
                    for c in range(2):
                        act.wait_ge(s["pt_ps"], 2 * bt + c + 1)
                        act.activation(probT[1 - par][:, c * HS:(c + 1) * HS], pt_ps2[:, c * HS:(c + 1) * HS], ACT.Copy)\
                            .then_inc(s["pt_sb"], 1)

            attention_steps(act, step)
            act.wait_ge(s["pt_ps"], 2 * T)
            for n in range(AHEAD + T, PIECES):
                weights_high(n, n % 2, piece_columns(n), n // 2)
            act.wait_ge(s["exp_in"], 1)
            act.activation(r_small[1], r_small[1], ACT.Exp).then_inc(s["exp_out"], 1)

            def rows_high(j, par):
                act.wait_ge(s["gt_ps"], j + 1)
                if not isinstance(j, int) or j >= 2:
                    act.wait_ge(s["h_ps"], 2 * (j - 1))
                act.activation(gT_hi[par], bk6[:, 0:KD * P], ACT.Copy).then_inc(s["gt_hi"], 1)

            rows_high(0, 0)

            def step(j, par):
                static = isinstance(j, int)
                if not static or j < J:
                    act.wait_ge(s["sc_ready"], j + 1)
                    for c in range(2):
                        act.wait_ge(s["h_ps"], 2 * j + c + 1)
                        act.activation(sil[par].rearrange("p (c n) -> p c n", c=2)[:, c, :], h1_ps[:, c, :], ACT.Silu,
                                       scale=slot_score[par][:, 0:1]).then_inc(s["silu_done"], 1)
                    if not static or j + 1 < J:
                        rows_high(j + 1, 1 - par)
                    act.wait_ge(s["ht_ps"], j + 1)
                    if not static or j >= 2:
                        act.wait_ge(s["y_ps"], j - 1)
                    act.activation(hT_hi[par], hT_ps, ACT.Copy).then_inc(s["ht_hi"], 1)

            expert_steps(act, step)

        @block.vector
        def _(dve):
            def link(ins):
                n_d[0] += 1
                ins.then_inc(s["prep_dve"], 1)
                dve.wait_ge(s["prep_dve"], n_d[0])

            n_d = [0]
            dve.wait_ge(s["prep_loads"], 16 * PREP_DMAS)
            link(dve.tensor_scalar(ab_mask[:, :], ab_col[:, :], 0.0, None, ALU.is_gt))
            link(dve.tensor_scalar(ab_row[:, :], ab_row[:, :], TINY, None, ALU.max))
            assert n_d[0] == AB_DONE
            dve.wait_ge(s["consts"], N_CONST_EARLY)
            for c in range(2):
                link(dve.tensor_copy(bq_sel[:, c, 0:PARTS:32], bias_qk[:, c:c + 1].broadcast_to([P, 3])))
            assert n_d[0] == BQ_DONE
            dve.wait_ge(s["ctxT_ps"], 1)
            dve.tensor_copy(ctxT, bk6[:, 0:KD * P].rearrange("p (k n) -> p k n", k=KD)).then_inc(s["ctxT_sb"], 1)
            for k in range(KD):
                for b in range(B):
                    src = bk6[:, k * P + b * S2:k * P + (b + 1) * S2]
                    for r in range(2):
                        dve.tensor_copy(ctxD[:, k, b, r * S2:(r + 1) * S2], src).then_inc(s["ctxT_sb"], 1)
            dve.wait_ge(s["gT_ps"], 1)
            dve.tensor_copy(gateT[:, :, :], bk7[:, 0:KD * E].rearrange("p (k e) -> p k e", k=KD)).then_inc(s["gT_sb"], 1)
            dve.wait_ge(s["kT_ps"], 1)
            for c in range(2):
                link(dve.tensor_scalar(kT[:, c, :], bk6[:, 256 + c * P:256 + (c + 1) * P], bias_qk[:, 2 + c:3 + c],
                                       HD ** -0.5, ALU.add, ALU.mult))
                for b in range(B):
                    dve.tensor_tensor(k_blk[c][:, b, :].rearrange("p (h s) -> p h s", h=8),
                                      kT[:, c, None, b * S2:(b + 1) * S2].broadcast_to([P, 8, S2]),
                                      head_mask[:, :, None].broadcast_to([P, 8, S2]), ALU.mult).then_inc(s["kblk"], 1)
            for b in range(B):
                dve.wait_ge(s["v_ps"], b + 1)
                vp = bk7[:, 0:D] if b == 0 else bk7[:, 256:512]
                for r in range(2):
                    rows = slice(r * S2, (r + 1) * S2)
                    dst = v_blk[rows, b, :, r * NOUT:r * NOUT + HD]
                    dve.tensor_scalar(dst, vp[rows, :].rearrange("p (j r d) -> p j r d", j=8, r=2)[:, :, r, :],
                                      ab_mask[rows, b:b + 1], None, ALU.mult).then_inc(s["v_sb"], 1)
                    dve.tensor_copy(v_blk[rows, b, :, r * NOUT + HD:(r + 1) * NOUT],
                                    ab_mask[rows, b:b + 1, None].broadcast_to([S2, 8, 1])).then_inc(s["v_sb"], 1)
            for n in range(8):
                b, c, k = n // 4, n // 2 % 2, n % 2
                dve.wait_ge(s["a_hi_s"], n + 1)
                dve.tensor_tensor(a_lo[b][:, k, c * HS:(c + 1) * HS], a_bank(n), a_hi[b][:, k, c * HS:(c + 1) * HS],
                                  ALU.subtract).then_inc(s["a_lo_s"], 1)

            def three_parts(dst, src, n, signal):
                res = beta_res[0][:, 0:n]
                res2 = beta_res[1][:, 0:n]
                link(dve.tensor_copy(dst, src))
                link(dve.tensor_tensor(res, src, dst, ALU.subtract))
                link(dve.tensor_copy(dst[32:64], res[32:64]))
                link(dve.tensor_copy(dst[64:PARTS], res[64:PARTS]))
                link(dve.tensor_tensor(res2[64:PARTS], res[64:PARTS], dst[64:PARTS], ALU.subtract))
                dve.tensor_copy(dst[64:PARTS], res2[64:PARTS]).then_inc(s[signal], 1)

            for n in range(2 * B):
                b, c = n // 2, n % 2
                dve.wait_ge(s["beta_ps"], n + 1)
                three_parts(beta[:, b, c * HS:(c + 1) * HS], pt_ps2[0:PARTS, c * HS:(c + 1) * HS], HS, "beta_sb")
            dve.wait_ge(s["bo_ps"], 1)
            three_parts(bo_parts[:, :], bk7[0:PARTS, 0:D], D, "bo_sb")
            dve.wait_ge(s["x_loads"], 16 * B)

            def tile(t, tt):
                return xs[:, tt, :] if t is not None else xs[:, bass.ds(tt, 1), :].rearrange("p u d -> p (u d)")

            for t in range(T):
                dve.bn_stats(st_all[:, t, :], xs[:, t, :]).then_inc(s["ln1_stats"], 1)
            dve.wait_ge(s["ln1_stats"], T)
            for t in range(T):
                dve.bn_aggr(mv_all[:, t, :], st_all[:, t, :]).then_inc(s["ln1_mv"], 1)
            dve.wait_ge(s["ln1_mv"], T)
            rsqrt(dve, rs_all[:, :], mv_all[:, :, 1], rsw[:, 0:T], rsw[:, T:2 * T], rsw[:, 2 * T:3 * T], "ln1_rstd", 0)

            def ln1(t, tt, par):
                at = slice(tt, tt + 1) if t is not None else bass.ds(tt, 1)
                dve.tensor_scalar(xn[par][:, :], tile(t, tt), mv_all[:, at, 0], rs_all[:, at], ALU.subtract, ALU.mult)\
                    .then_inc(s["xn_ready"], 1)

            ln1(0, 0, 0)
            ln1(1, 1, 1)

            def tokens_low(tt, par):
                dve.wait_ge(s["xt_hi"], tt + 1)
                dve.tensor_tensor(xT_lo[par][:, :], bk6[:, 0:KD * P], xT_hi[par][:, :], ALU.subtract)\
                    .then_inc(s["xt_lo"], 1)

            tokens_low(0, 0)

            def step(u, par, t):
                tt = 2 * u + par
                sv = sc_ps[par][:, :].rearrange("p (h n) -> p h n", h=H)
                ov = bk7[:, 0:H * NOUT].rearrange("p (h n) -> p h n", h=H)

                def maxima(c):
                    dve.wait_ge(s["s_ps"], 2 * tt + c + 1)
                    hh = slice(c * H // 2, (c + 1) * H // 2)
                    dve.tensor_reduce(top[:, hh], sv[:, hh, :], AX.X, ALU.max).then_inc(s["smax"], 1)

                if here(t, 3):
                    dve.wait_ge(s["ln2_stats"], tt - 2)
                    carry(dve)
                    dve.bn_aggr(mv2[:, :], st2[:, :]).then_inc(s["ln2_mv"], 1)
                if here(t, 0):
                    if t is None or t >= 1:
                        dve.wait_ge(s["ssub"], tt)
                    maxima(0)
                if here(t, 2):
                    dve.wait_ge(s["o_ps"], tt - 1)
                    dve.reciprocal(o_inv[:, :], ov[:, :, HD:NOUT].rearrange("p h n -> p (h n)")).then_inc(s["o_recip"], 1)
                if here(t, -2):
                    dve.wait_ge(s["xt_ps"], tt + 1)
                    ln1(t, tt + 2, par)
                if here(t, 2):
                    bt = tt - 2
                    dve.wait_ge(s["o_recip"], bt + 1)
                    if t is None or bt >= 1:
                        dve.wait_ge(s["ot_ps"], bt)
                    dve.tensor_tensor(o_sb[:, :].rearrange("p (h n) -> p h n", h=H), ov[:, :, 0:HD],
                                      o_inv[:, :, None].broadcast_to([P, H, HD]), ALU.mult).then_inc(s["o_norm"], 1)
                if here(t, -1):
                    tokens_low(tt + 1, 1 - par)
                if here(t, 0):
                    maxima(1)
                    dve.wait_ge(s["smax"], 2 * (tt + 1))
                    if t is None or t >= 2:
                        dve.wait_ge(s["pt_ps"], 2 * (tt - 1))
                    dve.tensor_tensor(prob[par].rearrange("p (h n) -> p h n", h=H), sv,
                                      top[:, :, None].broadcast_to([P, H, S2]), ALU.subtract).then_inc(s["ssub"], 1)
                if here(t, 3):
                    bu, bp = back(u, par, 3)
                    bt = tt - 3
                    dve.wait_ge(s["ln2_rstd"], (bt + 1) * RSQRT_OPS)
                    if t is None or bt >= 2:
                        dve.wait_ge(xn2_st[bp], 16 * bu)
                        dve.wait_ge(s["x2t_ps"], bt - 1)
                    dve.tensor_scalar(xn2[bp][:, :], tile(t, bt), mv2[:, 0:1], rs2[:, 0:1], ALU.subtract, ALU.mult)\
                        .then_inc(s["xn2_ready"], 1)
                if here(t, 4):
                    bt = tt - 4
                    dve.wait_ge(s["logit_ps"], bt + 1)
                    lo = logits[:, bt, :] if t is not None else logits[:, bass.ds(bt, 1), :].rearrange("p u e -> p (u e)")
                    dve.tensor_copy(lo, bk7[:, LG:LG + E]).then_inc(s["logit_sb"], 1)
                if here(t, 2):
                    bt = tt - 2
                    dve.wait_ge(s["attn_ps"], bt + 1)
                    xt = tile(t, bt)
                    dve.tensor_tensor(xt, bk6[:, KD * P:2 * KD * P], xt, ALU.add).then_inc(s["x2_ready"], 1)
                    dve.wait_ge(s["x2_ready"], bt + 1)
                    if t is None or bt >= 1:
                        dve.wait_ge(s["ln2_mv"], bt)
                    carry(dve)
                    dve.bn_stats(st2[:, :], xt).then_inc(s["ln2_stats"], 1)

            attention_steps(dve, step)

            n_r = [0]

            def rlink(ins):
                n_r[0] += 1
                ins.then_inc(s["route"], 1)
                dve.wait_ge(s["route"], n_r[0])

            score, ex, biased, rank, pos, pick = r_small[:6]
            dve.wait_ge(s["logit_sb"], T)
            for b in range(B):
                dve.wait_ge(x2_st[b], 16 * UT)
            dve.wait_ge(s["pt_ps"], 2 * T)
            dve.wait_ge(s["o_ps"], T)
            rlink(dve.tensor_reduce(t_max[:, :], logits[:, :, :], AX.X, ALU.max))
            dve.tensor_tensor(ex, logits[:, :, :], t_max[:, :, None].broadcast_to([P, T, E]), ALU.subtract)\
                .then_inc(s["exp_in"], 1)
            dve.wait_ge(s["exp_out"], 1)
            rlink(dve.tensor_reduce(t_sum[:, :], ex, AX.X, ALU.add))
            rlink(dve.reciprocal(t_sum[:, :], t_sum[:, :]))
            dve.tensor_tensor(score, ex, t_sum[:, :, None].broadcast_to([P, T, E]), ALU.mult).then_inc(s["scores_in"], 1)
            dve.wait_ge(s["scores_in"], 1)
            rlink(dve.tensor_tensor(biased, score, ebias[:, None, :].broadcast_to([P, T, E]), ALU.add))
            s_e = biased[:, :, :, None].broadcast_to([P, T, E, E])
            s_f = biased[:, :, None, :].broadcast_to([P, T, E, E])
            rlink(dve.tensor_tensor(rank_w, s_f, s_e, ALU.is_equal))
            rlink(dve.tensor_tensor(rank_w, rank_w, lower[:, None, :, :].broadcast_to([P, T, E, E]), ALU.mult))
            rlink(dve.tensor_tensor(rank_w2, s_f, s_e, ALU.is_gt))
            rlink(dve.tensor_tensor(rank_w, rank_w, rank_w2, ALU.add))
            rlink(dve.tensor_reduce(rank, rank_w, AX.X, ALU.add))
            dve.tensor_scalar(sel16[:, :, :], rank, float(TOPK), None, ALU.is_lt).then_inc(s["selected"], 1)
            dve.wait_ge(s["prefix_ps"], 1)
            rlink(dve.tensor_tensor(count_w[:, :, :], bk7[:, 0:E, None].broadcast_to([P, E, T]), tile_edge[:, :, :],
                                    ALU.is_gt))
            rlink(dve.tensor_reduce(n_tiles[:, :], count_w[:, :, :], AX.X, ALU.add))
            rlink(dve.tensor_tensor(ee_w[:, :, :], lower[:, :, :], n_tiles[:, None, :].broadcast_to([P, E, E]), ALU.mult))
            rlink(dve.tensor_reduce(first_tile[:, :], ee_w[:, :, :], AX.X, ALU.add))
            rlink(dve.tensor_tensor(last_tile[:, :], first_tile[:, :], n_tiles[:, :], ALU.add))
            rlink(dve.tensor_scalar(first_tile[:, :], first_tile[:, :], float(P), None, ALU.mult))
            rlink(dve.tensor_tensor(pos, bk6[:, 0:T * E].rearrange("p (t e) -> p t e", t=T),
                                    first_tile[:, None, :].broadcast_to([P, T, E]), ALU.add))
            for k in range(TOPK):
                rlink(dve.scalar_tensor_tensor(out=pick.rearrange("p t e -> p (t e)"), in0=rank.rearrange("p t e -> p (t e)"),
                                               scalar=float(k), in1=pos.rearrange("p t e -> p (t e)"),
                                               op0=ALU.is_equal, op1=ALU.mult))
                rlink(dve.tensor_reduce(pos_k[:, :, k:k + 1].rearrange("p t k -> p (t k)"), pick, AX.X, ALU.add))
            rlink(dve.tensor_copy(pos_i[:, :, :], pos_k[:, :, :]))
            rlink(dve.tensor_scalar(pos_i[:, :, :], pos_i[:, :, :], 7, None, ALU.logical_shift_right))
            rlink(dve.tensor_copy(pos_a[:, :, :], pos_i[:, :, :]))
            rlink(dve.tensor_scalar(pos_b[:, :, :], pos_a[:, :, :], -float(P), None, ALU.mult))
            rlink(dve.tensor_tensor(pos_b[:, :, :], pos_b[:, :, :], pos_k[:, :, :], ALU.add))
            NP = T * TOPK
            pa = pos_a[:, :, :].rearrange("p t k -> p (t k)")
            pb = pos_b[:, :, :].rearrange("p t k -> p (t k)")
            rlink(dve.tensor_tensor(oneh_a, iota_p[:, None, 0:J].broadcast_to([P, NP, J]),
                                    pa[:, :, None].broadcast_to([P, NP, J]), ALU.is_equal))
            rlink(dve.tensor_tensor(oneh_b, iota_p[:, None, :].broadcast_to([P, NP, P]),
                                    pb[:, :, None].broadcast_to([P, NP, P]), ALU.is_equal))
            dve.tensor_tensor(val_a[:, :, 0:J].rearrange("p (t k) j -> p t k j", k=TOPK),
                              oneh_a.rearrange("p (t k) j -> p t k j", k=TOPK),
                              tok_id[:, :, None, None].broadcast_to([P, T, TOPK, J]), ALU.mult)\
                .then_inc(s["oneh_ready"], 1)
            rlink(dve.tensor_tensor(tile_cmp[:, :, :], iota_p[:, 0:J, None].broadcast_to([P, J, E]),
                                    last_tile[:, None, :].broadcast_to([P, J, E]), ALU.is_ge))
            rlink(dve.tensor_reduce(tile_exp[:, :], tile_cmp[:, :, :], AX.X, ALU.add))
            rlink(dve.tensor_scalar(tile_exp[:, :], tile_exp[:, :], float(E - 1), None, ALU.min))
            rlink(dve.tensor_tensor(tile_oh[:, :, :], iota_p[:, None, 0:E].broadcast_to([P, J, E]),
                                    tile_exp[:, :, None].broadcast_to([P, J, E]), ALU.is_equal))
            rlink(dve.tensor_copy(tile_off[:, :], tile_exp[:, :]))
            dve.wait_ge(s["slots_ps"], 1)
            rlink(dve.tensor_copy(slot_tok[:, :], bk7[:, 64:64 + J]))
            rlink(dve.tensor_scalar(slot_pad[:, :], slot_tok[:, :], 0.0, None, ALU.is_equal))
            rlink(dve.tensor_scalar(idx_get[:, :], slot_tok[:, :], -1.0, 0.0, ALU.add, ALU.max))
            rlink(dve.tensor_scalar(slot_tmp[:, :], slot_tok[:, :], -1.0, None, ALU.add))
            rlink(dve.tensor_scalar(slot_tok[:, :], slot_pad[:, :], row_id[:, 0:1], None, ALU.mult))
            rlink(dve.scalar_tensor_tensor(out=slot_pad[:, :], in0=slot_pad[:, :], scalar=float(TOK + 1),
                                           in1=slot_tok[:, :], op0=ALU.mult, op1=ALU.add))
            dve.tensor_tensor(idx_put[:, :], slot_tmp[:, :], slot_pad[:, :], ALU.add).then_inc(s["idx_ready"], 1)
            dve.wait_ge(s["idx_ready"], 1)

            def slots(j, par):
                static = isinstance(j, int)
                dve.wait_ge(gathered[par], 16 * ((j - par) // 2 + 1) if static else 8 * (j - par) + 16)
                oh = tile_oh[:, j, :] if static else tile_oh[:, bass.ds(j, 1), :].rearrange("p u e -> p (u e)")
                if not static or j >= 1:
                    dve.wait_ge(s["sc_ready"], j)
                dve.tensor_tensor(score_w[:, :], gx[par][:, D:XR], oh, ALU.mult).then_inc(s["sc_tmp"], 1)
                dve.wait_ge(s["sc_tmp"], j + 1)
                dve.tensor_reduce(slot_score[par][:, :], score_w[:, :], AX.X, ALU.add).then_inc(s["sc_ready"], 1)
                dve.wait_ge(s["gt_hi"], j + 1)
                dve.tensor_tensor(gT_lo[par], bk6[:, 0:KD * P], gT_hi[par], ALU.subtract).then_inc(s["gt_lo"], 1)

            slots(0, 0)

            def step(j, par):
                static = isinstance(j, int)
                if not static or j < J:
                    for c in range(2):
                        dve.wait_ge(s["silu_done"], 2 * j + c + 1)
                        dve.scalar_tensor_tensor(out=hid[par].rearrange("p (c n) -> p c n", c=2)[:, c, :],
                                                 in0=h3_ps[:, c, :], scalar=slot_score[par][:, 0:1],
                                                 in1=sil[par].rearrange("p (c n) -> p c n", c=2)[:, c, :],
                                                 op0=ALU.mult, op1=ALU.mult).then_inc(s["h_ready"], 1)
                    if not static or j + 1 < J:
                        slots(j + 1, 1 - par)
                if not static or j >= 1:
                    q = 1 - par
                    dve.wait_ge(s["y_ps"], j)
                    if not static or j >= 3:
                        dve.wait_ge(s["put_done"], 16 * (j - 2))
                    dve.tensor_copy(y_sb[q], bk7[:, 0:D]).then_inc(s["y_ready"], 1)
                if not static or j < J:
                    dve.wait_ge(s["ht_hi"], j + 1)
                    dve.tensor_tensor(hT_lo[par], hT_ps, hT_hi[par], ALU.subtract).then_inc(s["ht_lo"], 1)

            expert_steps(dve, step)

        @block.tensor
        def _(pe):
            pe.wait_ge(s["consts"], N_CONST_EARLY)
            pe.wait_ge(s["prep_loads"], 16 * PREP_DMAS)
            idt = ident[:, :]
            for k in range(KD):
                ins = pe.transpose(bk6[:, k * P:(k + 1) * P], ctx_n[:, k * P:(k + 1) * P], idt)
            ins.then_inc(s["ctxT_ps"], 1)
            for k in range(KD):
                ins = pe.transpose(bk7[:, k * E:(k + 1) * E], gate_n[:, k * P:(k + 1) * P], ident[0:E, 0:E])
            ins.then_inc(s["gT_ps"], 1)
            for k in range(KD):
                for r in range(4):
                    ins = pe.transpose(sc_ps[0][:, k * 512 + r * P:k * 512 + (r + 1) * P],
                                       prep[:, 2 + r, k * P:(k + 1) * P], idt)
            ins.then_inc(s["wkvT_ps"], 1)
            for k in range(KD):
                for r in range(2):
                    ins = pe.transpose(pt_ps2[:, k * D + r * P:k * D + (r + 1) * P], wo_n[:, r, k * P:(k + 1) * P], idt)
            ins.then_inc(s["woT_ps"], 1)
            pe.wait_ge(s["ctxT_sb"], 9)
            pe.wait_ge(s["wkvT_sb"], 2)
            for c in range(2):
                for k in range(KD):
                    ins = pe.matmul(bk6[:, 256 + c * P:256 + (c + 1) * P], wkvT[:, k, c * P:(c + 1) * P], ctxT[:, k, :],
                                    start=k == 0, stop=k == KD - 1)
            ins.then_inc(s["kT_ps"], 1)
            pe.wait_ge(s["gT_sb"], 1)
            for b in range(B):
                if b:
                    pe.wait_ge(s["v_sb"], 4)
                vp = bk7[:, 0:D] if b == 0 else bk7[:, 256:512]
                for k in range(KD):
                    pe.matmul(vp, ctxD[:, k, b, :], wkvT[:, k, 2 * P:4 * P], start=k == 0, stop=False)
                pe.matmul(vp, ones_row[:, :], bv_row[:, :], start=False, stop=True).then_inc(s["v_ps"], 1)
            pe.wait_ge(s["kblk"], 4)
            for n in range(8):
                b, c, k = n // 4, n // 2 % 2, n % 2
                if n >= 4:
                    pe.wait_ge(s["a_lo_s"], n - 3)
                pe.matmul(a_bank(n), prep[:, c, k * P:(k + 1) * P], k_blk[c][:, b, :], start=True, stop=True)\
                    .then_inc(s["a_ps"], 1)
            pe.wait_ge(s["prep_dve"], BQ_DONE)
            pe.wait_ge(s["prep_act"], 1)
            pe.wait_ge(s["woT_sb"], 1)
            for n in range(2 * B):
                b, c = n // 2, n % 2
                if n >= 2:
                    pe.wait_ge(s["beta_sb"], n - 1)
                o = pt_ps2[0:PARTS, c * HS:(c + 1) * HS]
                pe.matmul(o, bq_sel[:, c, :], k_blk[c][:, b, :], start=True, stop=False)
                pe.matmul(o.rearrange("p (h s) -> p h s", h=8), parts_sel[:, :],
                          ab_row[:, None, b * S2:(b + 1) * S2].broadcast_to([1, 8, S2]), start=False, stop=True)\
                    .then_inc(s["beta_ps"], 1)
            pe.wait_ge(s["v_sb"], 8)
            pe.matmul(bk7[0:PARTS, 0:D], parts_sel[:, :], bo_row[:, :], start=True, stop=True).then_inc(s["bo_ps"], 1)

            def x_transpose(tt, par):
                pe.wait_ge(s["xn_ready"], tt + 1)
                if not isinstance(tt, int) or tt >= 1:
                    pe.wait_ge(s["xt_lo"], tt)
                for k in range(KD):
                    ins = pe.transpose(bk6[:, k * P:(k + 1) * P], xn[par][:, k * P:(k + 1) * P], idt)
                ins.then_inc(s["xt_ps"], 1)

            def scores_half(par, c):
                o = sc_ps[par][:, c * HS:(c + 1) * HS]
                cols = slice(c * HS, (c + 1) * HS)
                first = True
                for k in range(KD):
                    kk = slice(k * P, (k + 1) * P)
                    for l, r in ((xT_hi, a_hi), (xT_hi, a_lo), (xT_lo, a_hi)):
                        pe.matmul(o, l[par][:, kk], r[par][:, k, cols], start=first, stop=False)
                        first = False
                return pe.matmul(o, ones16[0:PARTS, :], beta[:, par, cols], start=False, stop=True)

            pe.wait_ge(s["kT_ps"], 1)
            pe.wait_ge(s["kblk"], 4)
            x_transpose(0, 0)

            def step(u, par, t):
                tt = 2 * u + par
                if here(t, 0):
                    pe.wait_ge(s["xt_lo"], tt + 1)
                    if t is None or t >= 2:
                        pe.wait_ge(s["ssub"], tt - 1)
                    elif t == 0:
                        pe.wait_ge(s["a_lo_s"], 8)
                        pe.wait_ge(s["beta_sb"], 4)
                    scores_half(par, 0).then_inc(s["s_ps"], 1)
                if here(t, 2):
                    bt = tt - 2
                    pe.wait_ge(s["pt_sb"], 2 * (bt + 1))
                    if t is None or bt >= 1:
                        pe.wait_ge(s["o_norm"], bt)
                    else:
                        pe.wait_ge(s["bo_sb"], 1)
                    if t is None or t >= 5:
                        pe.wait_ge(s["logit_sb"], tt - 4)
                    for j in range(8):
                        ins = pe.matmul(bk7[:, j * 2 * NOUT:(j + 1) * 2 * NOUT], probT[par][:, j * P:(j + 1) * P],
                                        v_blk[:, par, j, :], start=True, stop=True)
                    ins.then_inc(s["o_ps"], 1)
                if here(t, -1):
                    if t is None or t >= 3:
                        pe.wait_ge(s["x2_ready"], tt - 2)
                    x_transpose(tt + 1, 1 - par)
                if here(t, 4):
                    bt = tt - 4
                    pe.wait_ge(s["xn2_ready"], bt + 1)
                    if t is None or bt >= 1:
                        pe.wait_ge(s["x2t_sb"], bt)
                    for k in range(KD):
                        ins = pe.transpose(pt_ps2[:, k * P:(k + 1) * P], xn2[par][:, k * P:(k + 1) * P], idt)
                    ins.then_inc(s["x2t_ps"], 1)
                if here(t, 0):
                    scores_half(par, 1).then_inc(s["s_ps"], 1)
                if here(t, 2):
                    bt = tt - 2
                    pe.wait_ge(s["o_norm"], bt + 1)
                    if t is None or bt >= 1:
                        pe.wait_ge(s["x2_ready"], bt)
                    if here(t, -1):
                        pe.wait_ge(s["xt_lo"], tt + 2)
                    for k in range(KD):
                        ins = pe.transpose(bk6[:, (KD + k) * P:(KD + k + 1) * P], o_sb[:, k * P:(k + 1) * P], idt)
                    ins.then_inc(s["ot_ps"], 1)
                if here(t, 1):
                    bt = tt - 1
                    pe.wait_ge(s["p_exp"], bt + 1)
                    for c in range(2):
                        if t is None or bt >= 1:
                            pe.wait_ge(s["pt_sb"], 2 * bt)
                        if c == 0 and (t is None or bt >= 3):
                            pe.wait_ge(s["x2t_sb"], bt - 2)
                        for q in range(4):
                            j = 4 * c + q
                            ins = pe.transpose(pt_ps2[:, j * P:(j + 1) * P], prob[1 - par][:, j * P:(j + 1) * P], idt)
                        ins.then_inc(s["pt_ps"], 1)
                if here(t, 2):
                    bt = tt - 2
                    pe.wait_ge(s["ot_sb"], bt + 1)
                    o = bk6[:, KD * P:2 * KD * P]
                    for k in range(KD):
                        pe.matmul(o, oT[:, k * P:(k + 1) * P], woT[:, k, :], start=k == 0, stop=False)
                    pe.matmul(o, ones16[0:PARTS, :], bo_parts[:, :], start=False, stop=True).then_inc(s["attn_ps"], 1)
                if here(t, 4):
                    bt = tt - 4
                    pe.wait_ge(s["x2t_sb"], bt + 1)
                    if t is None or bt >= 1:
                        pe.wait_ge(s["logit_sb"], bt)
                    for k in range(KD):
                        ins = pe.matmul(bk7[:, LG:LG + E], xn2T[:, k * P:(k + 1) * P], gateT[:, k, :],
                                        start=k == 0, stop=k == KD - 1)
                    ins.then_inc(s["logit_ps"], 1)

            attention_steps(pe, step)

            pe.wait_ge(s["selected"], 1)
            def earlier_partitions(start):
                ins = pe.matmul(bk6[:, 0:T * E], before_half[:, :], sel16[:, :, :].rearrange("p t e -> p (t e)"),
                                start=start, stop=not start, skip_group_check=True)
                return ins

            earlier_partitions(True)
            for t in range(T - 1):
                pe.matmul(bk6[:, (t + 1) * E:T * E].rearrange("p (t e) -> p t e", e=E), ones16[:, :],
                          sel16[:, t:t + 1, :].broadcast_to([P, T - 1 - t, E]), start=False, stop=False,
                          skip_group_check=True)
            earlier_partitions(False)
            for t in range(T):
                ins = pe.matmul(bk7[:, 0:E], ones16[:, :], sel16[:, t, :], start=t == 0, stop=t == T - 1)
            ins.then_inc(s["prefix_ps"], 1)
            pe.wait_ge(s["oneh_ready"], 1)
            for n in range(T * TOPK):
                ins = pe.matmul(bk7[:, 64:64 + J], oneh_b[:, n, :], val_a[:, n, 0:J], start=n == 0,
                                stop=n == T * TOPK - 1)
            ins.then_inc(s["slots_ps"], 1)
            pe.wait_ge(s["idx_ready"], 1)
            pe.wait_ge(s["wlo"], PIECES)

            def x_rows(j, par, j1):
                pe.wait_ge(gathered[par], j1)
                if not isinstance(j, int) or j >= 1:
                    pe.wait_ge(s["gt_lo"], j)
                for k in range(KD):
                    ins = pe.transpose(bk6[:, k * P:(k + 1) * P], gx[par][:, k * P:(k + 1) * P], idt)
                ins.then_inc(s["gt_ps"], 1)

            x_rows(0, 0, 16)

            def step(j, par):
                static = isinstance(j, int)
                q = 1 - par
                if not static or j < J:
                    col = slice(j, j + 1) if static else bass.ds(j, 1)
                    e = pe.value_load(tile_off[0:1, col], min_val=0, max_val=E - 1)
                    pe.wait_ge(s["gt_lo"], j + 1)
                    if not static or j >= 1:
                        pe.wait_ge(s["h_ready"], 2 * j)
                    for c in range(2):
                        for ps, half in ((h1_ps, 0), (h3_ps, 1)):
                            for k in range(KD):
                                kk = slice(k * P, (k + 1) * P)
                                cols = bass.ds(e * WE + (half * HALF + k * F + c * FH), FH)
                                pe.matmul(ps[:, c, :], gT_hi[par][:, kk], w_hi[:, cols], start=k == 0, stop=False)
                                pe.matmul(ps[:, c, :], gT_lo[par][:, kk], w_hi[:, cols], start=False, stop=False)
                                ins = pe.matmul(ps[:, c, :], gT_hi[par][:, kk], w_lo[:, cols], start=False,
                                                stop=k == KD - 1)
                        ins.then_inc(s["h_ps"], 1)
                if not static or j + 1 < J:
                    x_rows(j + 1, q, 16 * ((j + 1 - q) // 2 + 1) if static else 8 * (j + 1 - q) + 16)
                if not static or j >= 1:
                    colp = slice(j - 1, j) if static else bass.ds(j - 1, 1)
                    ep = pe.value_load(tile_off[0:1, colp], min_val=0, max_val=E - 1)
                    pe.wait_ge(s["ht_lo"], j)
                    if not static or j >= 2:
                        pe.wait_ge(s["y_ready"], j - 1)
                    for c in range(KF):
                        rows = P if c < KF - 1 else FL
                        off = W13 + c * D if c < KF // 2 else HALF + W13 + (c - KF // 2) * D
                        cc = slice(c * P, (c + 1) * P)
                        cols = bass.ds(ep * WE + off, D)
                        pe.matmul(bk7[:, 0:D], hT_hi[q][0:rows, cc], w_hi[0:rows, cols], start=c == 0, stop=False)
                        pe.matmul(bk7[:, 0:D], hT_lo[q][0:rows, cc], w_hi[0:rows, cols], start=False, stop=False)
                        ins = pe.matmul(bk7[:, 0:D], hT_hi[q][0:rows, cc], w_lo[0:rows, cols], start=False,
                                        stop=c == KF - 1)
                    ins.then_inc(s["y_ps"], 1)
                if not static or j < J:
                    pe.wait_ge(s["h_ready"], 2 * (j + 1))
                    if not static or j >= 1:
                        pe.wait_ge(s["ht_lo"], j)
                    for c in range(KF):
                        rows = P if c < KF - 1 else FL
                        ins = pe.transpose(hT_ps[0:rows, c * P:(c + 1) * P], hid[par][:, c * P:c * P + rows], idt)
                    ins.then_inc(s["ht_ps"], 1)

            expert_steps(pe, step)


N_CONST = 21
N_CONST_EARLY = 14
AB_DONE = 2
RSQRT_OPS = 14
BQ_DONE = 4
PREP_DMAS = 3 + 13

_INS = ["x", "ctx_1024", "fside_BxS2_0", "L0_xattn_in_proj_weight", "L0_xattn_in_proj_bias",
        "L0_xattn_out_proj_weight", "L0_xattn_out_proj_bias", "L0_ffn_gate_w", "L0_ffn_expert_bias",
        "L0_ffn_w1", "L0_ffn_w2", "L0_ffn_w3"]


def kernel(**inputs):
    import numpy as _np
    import concourse.bacc as _bacc
    from concourse import mybir as _mybir
    from concourse.bass_utils import run_bass_kernel_spmd as _run

    nc = _bacc.Bacc("TRN2", target_bir_lowering=False, num_devices=1)
    arrays, args = {}, []
    for name in _INS:
        a = _np.ascontiguousarray(inputs[name])
        arrays[f"in_{name}"] = a
        args.append(nc.dram_tensor(f"in_{name}", a.shape, _mybir.dt.from_np(a.dtype), kind="ExternalInput").ap())
    shape = inputs["x"].shape
    args.append(nc.dram_tensor("out_0", shape, _mybir.dt.float32, kind="ExternalOutput").ap())
    xattn_moe(nc, *args)
    r = _run(nc, [arrays], core_ids=[0])
    return r.results[0]["out_0"]
```

```python
from contextlib import ExitStack

import concourse.bass as bass
from concourse import mybir

ALU = mybir.AluOpType
ACT = mybir.ActivationFunctionType
F32 = mybir.dt.float32
F16 = mybir.dt.float16
I32 = mybir.dt.int32
AX = mybir.AxisListType

P = 128
LN_EPS = 1e-5
TINY = 1.2e-38


def xattn_moe(nc, x, ctx_in, abundance, w_in, b_in, w_out, b_out, gate_w, expert_bias, w1, w2, w3, out):
    B, N, D = x.shape
    S2 = ctx_in.shape[1]
    HD = 16
    H = D // HD
    E, _, F = w1.shape
    KD = D // P
    KF = (F + P - 1) // P
    FL = F - (KF - 1) * P
    UT = N // P
    T = B * UT
    TOK = B * N
    SL = H * S2
    HS = SL // 2
    TOPK = 2
    J = (TOK * TOPK + E * (P - 1)) // P
    NOUT = HD + 1
    W13 = KD * F
    W2H = KF // 2 * D
    HALF = W13 + W2H
    WE = 2 * HALF
    FH = F // 2
    XR = D + E
    assert B == 2 and KD == 2 and E == 8 and UT == 8 and KF == 6 and FL == P // 2

    with ExitStack() as stack:
        def sb(name, shape, dt=F32):
            return stack.enter_context(nc.sbuf_tensor(name, shape, dt))

        def sem(name):
            return stack.enter_context(nc.semaphore(name))

        table = nc.dram_tensor("table", [TOK, XR], F32, kind="Internal").ap()
        acc = nc.dram_tensor("acc", [TOK + P, D], F32, kind="Internal").ap()
        table_v = table.rearrange("(b u p) d -> b u p d", b=B, p=P)
        acc_v = acc[0:TOK, :].rearrange("(b u p) d -> b u p d", b=B, p=P)

        w_hi = sb("w_hi", [P, E * WE], F16)
        w_lo = sb("w_lo", [P, E * WE], F16)
        ARENA = T * D + B * KD * SL
        arena = sb("arena", [P, ARENA])
        stage = [[sb(f"stage_w13_{i}", [P, W13]) for i in range(2)], [sb(f"stage_w2_{i}", [P, W2H]) for i in range(2)]]

        class Region:

            def __init__(self, base, start=0):
                self.base, self.at = base, start

            def __call__(self, cols, dt=F32):
                words = cols if dt != F16 else (cols + 1) // 2
                assert self.at + words <= self.base.shape[-1], (self.at, words)
                a = self.base[:, self.at:self.at + words]
                self.at += words
                return a if dt == F32 else a.bitcast(dt)

        take = Region(arena)
        xs = take(T * D).rearrange("p (t d) -> p t d", t=T)
        kb_hi, kb_lo = (take(2 * B * HS, F16).rearrange("p (c b n) -> p c b n", c=2, b=B) for _ in range(2))
        wq_hi, wq_lo = (take(KD * D, F16).rearrange("p (k n) -> p k n", k=KD) for _ in range(2))
        xT_hi, xT_lo = take(KD * P, F16), take(KD * P, F16)
        qT_hi, qT_lo = ([take(2 * P, F16) for _ in range(2)] for _ in range(2))
        take = Region(w_hi[:, (E - 1) * WE:E * WE].bitcast(F32))
        prob = [take(SL) for _ in range(2)]
        take = Region(w_lo[:, (E - 1) * WE:E * WE].bitcast(F32))
        probT = [take(SL) for _ in range(2)]
        xn = [sb(f"xn{i}", [P, D]) for i in range(2)]
        xn2 = [sb(f"xn2{i}", [P, D]) for i in range(2)]

        take = Region(arena)
        oneh_b = take(T * TOPK * P, F16).rearrange("p (n s) -> p n s", s=P)
        oneh_a = take(T * TOPK * J).rearrange("p (n j) -> p n j", j=J)
        val_a = take(T * TOPK * (J + 1), F16).rearrange("p (n j) -> p n j", j=J + 1)
        count_w = take(E * T).rearrange("p (e t) -> p e t", e=E)
        assert take.at <= T * D
        take = Region(arena, T * D)
        rank_w = take(T * E * E).rearrange("p (t e f) -> p t e f", t=T, e=E)
        pick = take(T * TOPK * E).rearrange("p (t k e) -> p t k e", t=T, k=TOPK)
        chosen = take(T * TOPK * E).rearrange("p (t k e) -> p t k e", t=T, k=TOPK)
        tile_cmp = take(J * E).rearrange("p (j e) -> p j e", j=J)
        r_small = [take(T * E).rearrange("p (t e) -> p t e", t=T) for _ in range(5)]
        tile_oh = take(J * E).rearrange("p (j e) -> p j e", j=J)
        ee_w = take(E * E).rearrange("p (e f) -> p e f", e=E)
        n_tiles, first_tile, last_tile = take(E), take(E), take(E)
        tile_exp, slot_tok, slot_pad = take(J), take(J), take(J)
        tile_off, idx_get, idx_put = (take(J).bitcast(I32) for _ in range(3))
        pos_k, pos_b, pos_a = (take(T * TOPK).rearrange("p (t k) -> p t k", k=TOPK) for _ in range(3))
        t_max, t_sum = take(T), take(T)
        pos_i = take(T * TOPK).bitcast(I32).rearrange("p (t k) -> p t k", k=TOPK)
        silu_warm = take(1)
        EARLY = T - 4

        take = Region(arena)
        LC = (KF - 1) * P
        hid = [take(KF * P) for _ in range(2)]
        sil = [take(F) for _ in range(2)]
        hT_hi = [take(KF * P, F16) for _ in range(2)]
        hT_lo = [take(LC, F16) for _ in range(2)]
        y_sb = [take(D) for _ in range(2)]
        gx = [take(XR) for _ in range(2)]
        gT_hi = [take(KD * P, F16) for _ in range(2)]
        gT_lo = [take(KD * P, F16) for _ in range(2)]
        assert take.at <= T * D + T * E * E + 2 * T * TOPK * E + J * E
        score_w = sb("score_w", [P, E])
        slot_score = [sb(f"slot_score{i}", [P, 1]) for i in range(2)]
        get_now = [sb(f"get_now{i}", [P, 1], I32) for i in range(2)]
        put_now = [sb(f"put_now{i}", [P, 1], I32) for i in range(2)]

        ident = sb("ident", [P, P])
        ones16 = sb("ones16", [P, P], F16)
        shares16 = sb("shares16", [P, P], F16)
        key_diag = sb("key_diag", [P, S2], F16)
        low_rows = sb("low_rows", [P, 1])
        before_half = sb("before_half", [P, P], F16)
        iota_p = sb("iota_p", [P, P])
        tok_id = sb("tok_id", [P, T])
        pad_row = sb("pad_row", [P, 1])
        tie = sb("tie", [P, E, E])
        lower = sb("lower", [P, E, E])
        tile_edge = sb("tile_edge", [P, E, T])

        gateT = sb("gateT", [P, KD, E])
        woT = sb("woT", [P, KD, D])
        v_blk = sb("v_blk", [P, B, 8, 2 * NOUT])
        beta = sb("beta", [P, B, SL], F16)
        bo16 = sb("bo16", [P, D], F16)
        ebias = sb("ebias", [P, E])

        take = Region(w_hi[:, 3 * WE:(E - 1) * WE].bitcast(F32))
        prep = take(6 * D).rearrange("p (r d) -> p r d", r=6)
        wo_n = take(2 * D).rearrange("p (r d) -> p r d", r=2)
        ctx_n = take(D)
        wkT = take(KD * D).rearrange("p (k n) -> p k n", k=KD)
        wvT = take(KD * D).rearrange("p (k n) -> p k n", k=KD)
        kT_hi, kT_lo = (take(2 * B * S2, F16).rearrange("p (c b s) -> p c b s", c=2, b=B) for _ in range(2))
        ctxD = take(KD * B * P).rearrange("p (k b r s) -> p k b r s", k=KD, b=B, r=2)
        kT = take(2 * B * P).rearrange("p (c b r s) -> p c b r s", c=2, b=B, r=2)
        gate_n = take(D)[0:E]
        rows6 = take(P)[0:6]
        cols6 = take(6)
        bias_qk, ab_col = cols6[:, 0:4], cols6[:, 4:6]
        bq_blk = take(2 * 8).rearrange("p (c h) -> p c h", c=2)
        bv_row = take(D)[0:1]
        take = Region(w_lo[:, 3 * WE:(E - 1) * WE].bitcast(F32))
        bo_all = take(D)
        ab_log = take(B)
        ab_mask = take(B)
        bias_sum = take(B * H)
        bias_rest = take(B * H)
        bo_rest = take(D)
        bias16 = take(B * H, F16)
        ones_row = take(P)[0:1]
        head_mask = take(8)
        zero_rows = take(D)

        FIRST = 4
        REST = T - FIRST
        st_all = take(T * 6).rearrange("p (t n) -> p t n", t=T)
        mv_all = sb("mv_all", [P, T, 2])
        rs_all = sb("rs_all", [P, T])
        rsw = sb("rsw", [P, 3 * FIRST])
        rsw1 = sb("rsw1", [P, 3 * (T - FIRST)])
        st2 = sb("st2", [P, 6])
        mv2 = sb("mv2", [P, 2])
        rs2 = sb("rs2", [P, 1])
        rsw2 = sb("rsw2", [P, 3])
        top = sb("top", [P, H])
        o_inv = sb("o_inv", [P, H])
        o_sb = sb("o_sb", [P, D])
        oT = sb("oT", [P, KD * P])
        xn2T = sb("xn2T", [P, KD * P])
        logits = sb("logits", [P, T, E])
        sel16 = sb("sel16", [P, T, E], F16)

        bank = [stack.enter_context(nc.psum_tensor(f"bank{i}", [P, 512], F32)) for i in range(2)]
        sc_ps = [stack.enter_context(nc.psum_tensor(f"sc{i}", [P, 1024], F32)) for i in range(2)]
        pt_ps2 = stack.enter_context(nc.psum_tensor("ptps", [P, 1024], F32))
        bk6, bk7 = bank
        h1_ps = sc_ps[0][:, :].rearrange("p (c n) -> p c n", c=2)[:, :, 0:FH]
        h3_ps = sc_ps[1][:, :].rearrange("p (c n) -> p c n", c=2)[:, :, 0:FH]
        hT_ps = pt_ps2[:, 0:KF * P]

        names = """consts ctx_load wkv_load wq_load wo_load row_loads bo_load eb_load x_load0 x_load1 w_loads00 w_loads01 w_loads10 w_loads11 xn2_st0 xn2_st1 x2_st0 x2_st1 score_st zero_st
            cols_ps cols_sb ctxT_ps ctx_sb wkT_ps wkT_sb wvT_ps wvT_sb woT_ps woT_sb gT_ps gT_sb kT_ps kT_sb kT16 kb_dve kb_pool wqT_ps wq_hi_s wq_lo_s
            v_ps v_sb ab_floor ab_mask_s ab_log_s bq_s bias_ps prep_dve bias_parts beta_s bo_s
            ln1_stats ln1_mv ln1_rstd ln1_rstd_b xn_ready xt_ps xt_hi xt_lo q_ps q_hi_s q_lo_s s_ps smax ssub p_exp pt_ps pt_sb
            o_ps o_recip o_norm ot_ps ot_sb attn_ps x2_ready ln2_stats ln2_mv ln2_rstd xn2_ready
            x2t_ps x2t_sb logit_ps logit_sb whi wlo
            route exp_in exp_out silu_table scores_in selected prefix_ps oneh_ready slots_ps get_ready put_ready experts_ready
            get_idx gat0 gat1 put_idx put_done sc_tmp sc_ready gt_ps gt_hi gt_lo h_ps silu_done h_ready ht_ps ht_hi ht_lo
            y_ps y_ready copied carried_dve carried_pool""".split()
        s = {n: sem(n) for n in names}
        w_loads = [[s["w_loads00"], s["w_loads01"]], [s["w_loads10"], s["w_loads11"]]]
        xn2_st = [s["xn2_st0"], s["xn2_st1"]]
        x2_st = [s["x2_st0"], s["x2_st1"]]
        gathered = [s["gat0"], s["gat1"]]

        def back(u, par, k):
            return u + (par - k) // 2, (par - k) % 2

        def attention_steps(eng, step):
            for t in range(6):
                step(t // 2, t % 2, t)
            with eng.Fori(3, UT - 1) as u:
                step(u, 0, None)
                step(u, 1, None)
            for t in range(T - 2, T + 4):
                step(t // 2, t % 2, t)

        STEPS = T + 4
        STEP_HALVES = [(1, 0), (1, 1), (2, 1)] + [(e, 0) for e in range(2, 7)] + [(3, 1), (4, 1)]
        BESIDE = {4: (5, 1), 14: (6, 1)}
        PIECES = [(0, g, kind, g) for g in range(2) for kind in range(2)]
        AHEAD = len(PIECES)
        at_step = []
        for t in range(STEPS):
            at_step.append([len(PIECES)])
            PIECES.append((*STEP_HALVES[t // 2], t % 2, 0))
            if t - t % 2 in BESIDE:
                at_step[t].append(len(PIECES))
                PIECES.append((*BESIDE[t - t % 2], t % 2, 1))
        LATE = len(PIECES)
        PIECES += [(E - 1, g, kind, 1 - g) for g in range(2) for kind in range(2)]
        assert len({p[:3] for p in PIECES}) == len(PIECES) == 4 * E

        def loop_piece(u, par):
            return 2 * u + par + (at_step[6][0] - 6)

        def rank(n):
            same = [m for m in range(n) if PIECES[m][2:] == PIECES[n][2:]]
            return len(same), same[-1] if same else None

        def piece_columns(n):
            e, g, kind, _ = PIECES[n]
            at = e * WE + g * HALF + kind * W13
            return slice(at, at + (W13, W2H)[kind])

        def loop_columns(u, par):
            return bass.ds((u - 1) * WE + par * W13, (W13, W2H)[par])

        def here(t, lag):
            return t is None or 0 <= t - lag < T

        def expert_steps(eng, step):
            for j in range(3):
                step(j, j % 2)
            with eng.Fori(1, (J - 3) // 2) as v:
                step(2 * v + 1, 1)
                step(2 * v + 2, 0)
            for j in range(J - 2, J + 1):
                step(j, j % 2)

        def carry(eng):
            eng.sem_inc(s["carried_dve" if eng.engine == nc.vector.engine else "carried_pool"], 1)

        def rsqrt(eng, r, v, ve, w, w2, chain, base):
            n = [0]

            def go(ins):
                n[0] += 1
                ins.then_inc(s[chain], 1)
                eng.wait_ge(s[chain], base + n[0])

            def scalar_op(*operands):
                if not isinstance(base, int):
                    carry(eng)
                go(eng.tensor_scalar(*operands))

            scalar_op(ve, v, LN_EPS, None, ALU.add)
            scalar_op(r.bitcast(I32), ve.bitcast(I32), -0.5, float(0x5F3759DF), ALU.mult, ALU.add)
            go(eng.tensor_tensor(w, r, r, ALU.mult))
            go(eng.tensor_tensor(w, w, ve, ALU.mult))
            scalar_op(w2, w, 0.375, -1.25, ALU.mult, ALU.add)
            go(eng.tensor_tensor(w2, w2, w, ALU.mult))
            scalar_op(w2, w2, 1.875, None, ALU.add)
            go(eng.tensor_tensor(r, r, w2, ALU.mult))
            go(eng.tensor_tensor(w, r, r, ALU.mult))
            go(eng.tensor_tensor(w, w, ve, ALU.mult))
            scalar_op(w2, w, -0.5, 1.5, ALU.mult, ALU.add)
            go(eng.tensor_tensor(r, r, w2, ALU.mult))
            assert n[0] == RSQRT_OPS

        def v_bank(b):
            return bk7[:, 0:D] if b == 0 else pt_ps2[:, 512:512 + D]

        assert J % 2 == 1
        block = stack.enter_context(nc.Block())

        @block.sync
        def _(sp):
            sp.dma_start(ctx_n, ctx_in.rearrange("b s d -> (b s) d")).then_inc(s["ctx_load"], 16)
            w_in_v = w_in.rearrange("(r p) d -> p r d", p=P)
            sp.dma_start(prep[:, 2:6, :], w_in_v[:, 2:6, :]).then_inc(s["wkv_load"], 16)
            sp.dma_start(prep[:, 0:2, :], w_in_v[:, 0:2, :]).then_inc(s["wq_load"], 16)
            sp.dma_start(wo_n, w_out.rearrange("(r p) d -> p r d", p=P)).then_inc(s["wo_load"], 16)
            sp.wait_ge(s["wkv_load"], 16)
            for b in range(B):
                sp.dma_start(xs[:, b:T:2, :], x[b].rearrange("(u p) d -> p u d", p=P)).then_inc(s[f"x_load{b}"], 16)

            def load(n, kind=None, expert=None):
                if kind is None:
                    e, g, kind, buf = PIECES[n]
                    if rank(n)[0]:
                        sp.wait_ge(s["whi"], rank(n)[1] + 1)
                        sp.wait_ge(s["wlo"], rank(n)[1] + 1)
                else:
                    e, g, buf = bass.ds(expert, 1), 0, 0
                    sp.wait_ge(s["whi"], n - 1)
                    sp.wait_ge(s["wlo"], n - 1)
                dst, loaded = stage[kind][buf], w_loads[kind][buf]
                if kind == 0:
                    src = (w1, w3)[g][e]
                    src = src.rearrange("(k p) f -> p k f", p=P) if expert is None else src.rearrange("e (k p) f -> p (e k) f", p=P)
                    sp.dma_start(dst.rearrange("p (k f) -> p k f", k=KD), src).then_inc(loaded, 16)
                    return
                src = w2[e] if expert is None else w2[e].rearrange("e f d -> (e f) d")
                c0 = g * KF // 2 * P
                full = KF // 2 - 1
                sp.dma_start(dst[:, 0:full * D].rearrange("p (c d) -> p c d", c=full),
                             src[c0:c0 + full * P, :].rearrange("(c p) d -> p c d", p=P)).then_inc(loaded, 16)
                c0 += full * P
                for r in range(2):
                    rows = c0 + r * FL if g == 0 else c0
                    sp.dma_start(dst[r * FL:(r + 1) * FL, full * D:W2H], src[rows:rows + FL, :]).then_inc(loaded, 16)

            for n in range(AHEAD):
                load(n)
            sp.wait_ge(s["consts"], N_CONST_EARLY)
            sp.dma_start(acc[TOK:TOK + P, :], zero_rows).then_inc(s["zero_st"], 16)
            load(AHEAD)

            def step(u, par, t):
                if t is None:
                    load(loop_piece(u, par) + 1, 1 - par, u + par - 1)
                if t == T - 2:
                    load(at_step[t][1])
                if t is not None and t + 1 < STEPS:
                    for n in at_step[t + 1]:
                        load(n)
                if t == T:
                    for n in (LATE, LATE + 1):
                        load(n)
                if here(t, 2):
                    bu, bt = u - 1, 2 * u + par - 2
                    if t is None:
                        acc_d = acc_v[par, bass.ds(bu, 1)].rearrange("u p d -> p (u d)")
                        x_s = xs[:, bass.ds(bt, 1), :].rearrange("p u d -> p (u d)")
                    else:
                        acc_d, x_s = acc_v[par, bu], xs[:, bt, :]
                    sp.wait_ge(s["x2_ready"], bt + 1)
                    sp.dma_start(acc_d, x_s).then_inc(x2_st[par], 16)
                if here(t, 3):
                    bu, bp = back(u, par, 3)
                    bt = 2 * bu + bp
                    if t is None:
                        tab_d = table_v[bp, bass.ds(bu, 1), :, 0:D].rearrange("u p d -> p (u d)")
                    else:
                        tab_d = table_v[bp, bu, :, 0:D]
                    sp.wait_ge(s["xn2_ready"], bt + 1)
                    sp.dma_start(tab_d, xn2[bp][:, :]).then_inc(xn2_st[bp], 16)

            attention_steps(sp, step)
            for n in range(LATE + 2, len(PIECES)):
                load(n)
            sp.wait_ge(s["scores_in"], 2)
            for b in range(B):
                sp.dma_start(table_v[b, :, :, D:XR].rearrange("u p e -> p u e"),
                             r_small[0][:, b:T:2, :]).then_inc(s["score_st"], 16)
            sp.wait_ge(s["put_done"], 16 * J)
            sp.dma_start(out.rearrange("b n d -> (b n) d"), acc[0:TOK, :]).then_inc(s["copied"], 16)
            sp.wait_ge(s["copied"], 16)

        @block.gpsimd
        def _(pool):
            n_c = [0]

            def const(ins):
                n_c[0] += 1
                ins.then_inc(s["consts"], 1)
                pool.wait_ge(s["consts"], n_c[0])

            const(pool.memset(ident[:, :], 0.0))
            const(pool.affine_select(out=ident[:, :], in_=ident[:, :], compare_op=ALU.not_equal, fill=1.0, base=0,
                                     pattern=[[-1, P]], channel_multiplier=1))
            const(pool.memset(ones_row[:, :], 1.0))
            const(pool.memset(ones16[:, :], 1.0))
            const(pool.memset(before_half[:, :], 0.5))
            const(pool.affine_select(out=before_half[:, :], in_=before_half[:, :], compare_op=ALU.is_gt, fill=0.0, base=0,
                                     pattern=[[1, P]], channel_multiplier=-1))
            const(pool.memset(head_mask[:, :], 1.0))
            const(pool.affine_select(out=head_mask[:, :], in_=head_mask[:, :], compare_op=ALU.is_ge, fill=0.0,
                                     base=0, pattern=[[-HD, 8]], channel_multiplier=1))
            const(pool.affine_select(out=head_mask[:, :], in_=head_mask[:, :], compare_op=ALU.is_ge, fill=0.0,
                                     base=HD - 1, pattern=[[HD, 8]], channel_multiplier=-1))
            const(pool.memset(key_diag[:, :], 0.0))
            for half in range(2):
                const(pool.affine_select(out=key_diag[:, :], in_=key_diag[:, :], compare_op=ALU.not_equal, fill=1.0,
                                         base=-half * S2, pattern=[[-1, S2]], channel_multiplier=1))
            const(pool.memset(low_rows[:, :], -1.0))
            const(pool.memset(low_rows[0:S2, :], 0.0))
            const(pool.memset(shares16[:, :], 2.0 / P))
            const(pool.memset(v_blk[:, :, :, :], 0.0))
            const(pool.memset(zero_rows[:, :], 0.0))
            assert n_c[0] == N_CONST_EARLY

            pool.wait_ge(s["kT16"], 2)
            for c in range(2):
                for dst, src in ((kb_hi, kT_hi), (kb_lo, kT_lo)):
                    pool.tensor_tensor(dst[:, c, 1, :].rearrange("p (h s) -> p h s", h=8),
                                       src[:, c, 1:2, :].broadcast_to([P, 8, S2]),
                                       head_mask[:, :, None].broadcast_to([P, 8, S2]), ALU.mult).then_inc(s["kb_pool"], 1)

            const(pool.iota(iota_p[:, :], pattern=[[1, P]], base=0, channel_multiplier=0,
                            allow_small_or_imprecise_dtypes=True))
            const(pool.iota(pad_row[:, :], pattern=[[0, 1]], base=TOK + 1, channel_multiplier=1,
                            allow_small_or_imprecise_dtypes=True))
            for b in range(B):
                const(pool.iota(tok_id[:, b:T:2], pattern=[[P, UT]], base=b * N + 1, channel_multiplier=1,
                                allow_small_or_imprecise_dtypes=True))
            const(pool.memset(lower[:, :, :], 1.0))
            const(pool.affine_select(out=lower[:, :, :], in_=lower[:, :, :], compare_op=ALU.is_gt, fill=0.0, base=0,
                                     pattern=[[1, E], [-1, E]], channel_multiplier=0))
            const(pool.memset(tie[:, :, :], -TINY))
            const(pool.affine_select(out=tie[:, :, :], in_=tie[:, :, :], compare_op=ALU.is_gt, fill=0.0, base=0,
                                     pattern=[[1, E], [-1, E]], channel_multiplier=0))
            const(pool.iota(tile_edge[:, :, :], pattern=[[0, E], [P, T]], base=0, channel_multiplier=0,
                            allow_small_or_imprecise_dtypes=True))
            assert n_c[0] == N_CONST

            pool.wait_ge(s["bias_parts"], 1)
            for b in range(B):
                pool.tensor_tensor(beta[:, b, :].rearrange("p (h s) -> p h s", h=H),
                                   bias16[:, b * H:(b + 1) * H, None].broadcast_to([P, H, S2]),
                                   key_diag[:, None, :].broadcast_to([P, H, S2]), ALU.mult).then_inc(s["beta_s"], 1)

            def weights_low(number, staged, cols):
                pool.wait_ge(s["whi"], number + 1)
                pool.tensor_tensor(w_lo[:, cols], staged[:, :], w_hi[:, cols], ALU.subtract).then_inc(s["wlo"], 1)

            def piece_low(n):
                kind, buf = PIECES[n][2:]
                weights_low(n, stage[kind][buf], piece_columns(n))

            for n in range(AHEAD):
                piece_low(n)

            def step(u, par, t):
                tt = 2 * u + par
                if t == 1:
                    pool.wait_ge(s["ln1_mv"], T)
                    rsqrt(pool, rs_all[:, FIRST:T], mv_all[:, FIRST:T, 1], rsw1[:, 0:REST],
                          rsw1[:, REST:2 * REST], rsw1[:, 2 * REST:3 * REST], "ln1_rstd_b", 0)
                if here(t, 3):
                    bt = tt - 3
                    pool.wait_ge(s["ln2_mv"], bt + 1)
                    rsqrt(pool, rs2[:, :], mv2[:, 1:2], rsw2[:, 0:1], rsw2[:, 1:2], rsw2[:, 2:3], "ln2_rstd",
                          bt * RSQRT_OPS)
                if t is None:
                    weights_low(loop_piece(u, par), stage[par][0], loop_columns(u, par))
                else:
                    for n in at_step[t]:
                        piece_low(n)

            attention_steps(pool, step)
            pool.wait_ge(s["o_ps"], T)
            for n in range(LATE, len(PIECES)):
                piece_low(n)
            pool.wait_ge(s["zero_st"], 16)
            for b in range(2):
                pool.wait_ge(x2_st[b], 16 * UT)
                pool.wait_ge(xn2_st[b], 16 * UT)
            pool.wait_ge(s["score_st"], 16 * B)
            pool.wait_ge(s["get_ready"], 1)

            def gather(j, par, dyn):
                col = bass.ds(j, 1) if dyn else slice(j, j + 1)
                pool.tensor_copy(get_now[par][:, :], idx_get[:, col]).then_inc(s["get_idx"], 1)
                pool.wait_ge(s["get_idx"], j + 1)
                carry(pool)
                pool.indirect_dma_start(out=gx[par], out_offset=None, in_=table[:, :],
                                        in_offset=bass.IndirectOffsetOnAxis(ap=get_now[par][:, 0:1], axis=0))\
                    .then_inc(gathered[par], 16)

            gather(0, 0, False)
            gather(1, 1, False)
            pool.wait_ge(s["put_ready"], 1)

            def step(j, par):
                static = isinstance(j, int)
                if not static or j + 2 < J:
                    pool.wait_ge(s["gt_ps"], j + 1)
                    pool.wait_ge(s["sc_tmp"], j + 1)
                    gather(j + 2, par, not static)
                if not static or j >= 1:
                    q = 1 - par
                    col = slice(j - 1, j) if static else bass.ds(j - 1, 1)
                    pool.tensor_copy(put_now[q][:, :], idx_put[:, col]).then_inc(s["put_idx"], 1)
                    pool.wait_ge(s["put_idx"], j)
                    pool.wait_ge(s["y_ready"], j)
                    if not static or j >= 2:
                        pool.wait_ge(s["put_done"], 16 * (j - 1))
                    carry(pool)
                    pool.indirect_dma_start(out=acc[:, :],
                                            out_offset=bass.IndirectOffsetOnAxis(ap=put_now[q][:, 0:1], axis=0),
                                            in_=y_sb[q], in_offset=None, compute_op=ALU.add)\
                        .then_inc(s["put_done"], 16)

            expert_steps(pool, step)

        @block.scalar
        def _(act):
            act.dma_start(rows6[0:4, :], b_in[0:4 * P].rearrange("(r p) -> r p", p=P)).then_inc(s["row_loads"], 16)
            for r in range(2):
                act.dma_start(rows6[4:6, r * S2:(r + 1) * S2], abundance).then_inc(s["row_loads"], 16)
            act.dma_start(gate_n[:, :], gate_w).then_inc(s["row_loads"], 16)
            act.dma_start(bv_row[:, :], b_in[2 * D:3 * D].rearrange("(a n) -> a n", a=1)).then_inc(s["row_loads"], 16)
            act.dma_start(bo_all[:, :], b_out.rearrange("(a n) -> a n", a=1).broadcast_to([P, D]))\
                .then_inc(s["bo_load"], 16)
            act.dma_start(ebias[:, :], expert_bias.rearrange("(a n) -> a n", a=1).broadcast_to([P, E]))\
                .then_inc(s["eb_load"], 16)

            def weights_high(cols, count, kind, buf):
                loads = 16 if kind == 0 else 48
                act.wait_ge(w_loads[kind][buf], loads * (count + 1))
                act.activation(w_hi[:, cols], stage[kind][buf][:, :], ACT.Copy).then_inc(s["whi"], 1)

            def piece_high(n):
                weights_high(piece_columns(n), rank(n)[0], *PIECES[n][2:])

            act.wait_ge(s["ab_floor"], 1)
            act.activation(ab_log[:, :], ab_log[:, :], ACT.Ln).then_inc(s["ab_log_s"], 1)
            act.wait_ge(s["wkT_ps"], 1)
            act.activation(wkT, sc_ps[0][:, 0:KD * D].rearrange("p (k n) -> p k n", k=KD), ACT.Copy).then_inc(s["wkT_sb"], 1)
            act.wait_ge(s["wvT_ps"], 1)
            act.activation(wvT, sc_ps[0][:, 512:512 + KD * D].rearrange("p (k n) -> p k n", k=KD), ACT.Copy)\
                .then_inc(s["wvT_sb"], 1)
            act.wait_ge(s["wqT_ps"], 1)
            act.activation(wq_hi, sc_ps[0][:, 0:KD * D].rearrange("p (k n) -> p k n", k=KD), ACT.Copy)\
                .then_inc(s["wq_hi_s"], 1)
            act.wait_ge(s["woT_ps"], 1)
            act.activation(woT[:, :, :], pt_ps2[:, 0:2 * D].rearrange("p (k n) -> p k n", k=2), ACT.Copy)\
                .then_inc(s["woT_sb"], 1)
            for b in range(B):
                act.wait_ge(s["v_ps"], b + 1)
                act.wait_ge(s["ab_mask_s"], 1)
                for r in range(2):
                    rows = slice(r * S2, (r + 1) * S2)
                    act.activation(v_blk[rows, b, :, r * NOUT:r * NOUT + HD],
                                   v_bank(b)[rows, :].rearrange("p (j r d) -> p j r d", j=8, r=2)[:, :, r, :], ACT.Identity,
                                   scale=ab_mask[rows, b:b + 1]).then_inc(s["v_sb"], 1)
                    act.activation(v_blk[rows, b, :, r * NOUT + HD:(r + 1) * NOUT],
                                   ab_mask[rows, b:b + 1, None].broadcast_to([S2, 8, 1]), ACT.Copy).then_inc(s["v_sb"], 1)

            def tokens_high(tt):
                act.wait_ge(s["xt_ps"], tt + 1)
                if not isinstance(tt, int) or tt >= 1:
                    act.wait_ge(s["q_ps"], tt)
                act.activation(xT_hi, bk6[:, 0:KD * P], ACT.Copy).then_inc(s["xt_hi"], 1)

            def queries_high(tt, par):
                act.wait_ge(s["q_ps"], tt + 1)
                if not isinstance(tt, int) or tt >= 2:
                    act.wait_ge(s["s_ps"], 2 * (tt - 1))
                act.activation(qT_hi[par], bk7[:, 0:2 * P], ACT.Copy).then_inc(s["q_hi_s"], 1)

            for n in range(2):
                piece_high(n)
            tokens_high(0)
            queries_high(0, 0)

            def step(u, par, t):
                tt = 2 * u + par
                if t == T + 2:
                    act.wait_ge(s["exp_in"], 1)
                    act.activation(r_small[1][:, 0:EARLY, :], r_small[1][:, 0:EARLY, :], ACT.Exp).then_inc(s["exp_out"], 1)
                if here(t, 1):
                    act.wait_ge(s["ssub"], tt)
                    act.activation(prob[1 - par], prob[1 - par], ACT.Exp).then_inc(s["p_exp"], 1)
                if t == 0:
                    for n in range(2, 4):
                        piece_high(n)
                if here(t, -1):
                    tokens_high(tt + 1)
                if here(t, 4):
                    bt = tt - 4
                    act.wait_ge(s["x2t_ps"], bt + 1)
                    if t is None or bt >= 1:
                        act.wait_ge(s["logit_ps"], bt)
                    act.activation(xn2T[:, :], pt_ps2[:, 0:KD * P], ACT.Copy).then_inc(s["x2t_sb"], 1)
                if t is None:
                    weights_high(loop_columns(u, par), rank(at_step[6][0])[0] + u - 3, par, 0)
                elif t < T:
                    piece_high(at_step[t][0])
                if here(t, 2):
                    bt = tt - 2
                    act.wait_ge(s["ot_ps"], bt + 1)
                    if t is None or bt >= 1:
                        act.wait_ge(s["attn_ps"], bt)
                    act.activation(oT[:, :], bk6[:, KD * P:2 * KD * P], ACT.Copy).then_inc(s["ot_sb"], 1)
                if here(t, -1):
                    queries_high(tt + 1, 1 - par)
                if here(t, 1):
                    bt = tt - 1
                    for c in range(2):
                        act.wait_ge(s["pt_ps"], 2 * bt + c + 1)
                        act.activation(probT[1 - par][:, c * HS:(c + 1) * HS], pt_ps2[:, c * HS:(c + 1) * HS], ACT.Copy)\
                            .then_inc(s["pt_sb"], 1)
                if t is not None:
                    for n in at_step[t][t < T:]:
                        piece_high(n)

            attention_steps(act, step)
            act.wait_ge(s["pt_ps"], 2 * T)
            piece_high(LATE)
            act.wait_ge(s["exp_in"], 2)
            act.activation(r_small[1][:, EARLY:T, :], r_small[1][:, EARLY:T, :], ACT.Exp).then_inc(s["exp_out"], 1)
            for n in range(LATE + 1, len(PIECES)):
                piece_high(n)
            act.activation(silu_warm, ident[:, 0:1], ACT.Silu).then_inc(s["silu_table"], 1)

            def rows_high(j, par):
                act.wait_ge(s["gt_ps"], j + 1)
                if not isinstance(j, int) or j >= 2:
                    act.wait_ge(s["h_ps"], 2 * (j - 1))
                act.activation(gT_hi[par], bk6[:, 0:KD * P], ACT.Copy).then_inc(s["gt_hi"], 1)

            rows_high(0, 0)

            def step(j, par):
                static = isinstance(j, int)
                if not static or j < J:
                    act.wait_ge(s["sc_ready"], j + 1)
                    for c in range(2):
                        act.wait_ge(s["h_ps"], 2 * j + c + 1)
                        act.activation(sil[par].rearrange("p (c n) -> p c n", c=2)[:, c, :], h1_ps[:, c, :], ACT.Silu,
                                       scale=slot_score[par][:, 0:1]).then_inc(s["silu_done"], 1)
                    if not static or j + 1 < J:
                        rows_high(j + 1, 1 - par)
                    act.wait_ge(s["ht_ps"], j + 1)
                    if not static or j >= 2:
                        act.wait_ge(s["y_ps"], j - 1)
                    act.activation(hT_hi[par], hT_ps, ACT.Copy).then_inc(s["ht_hi"], 1)

            expert_steps(act, step)

        @block.vector
        def _(dve):
            def link(ins):
                n_d[0] += 1
                ins.then_inc(s["prep_dve"], 1)
                dve.wait_ge(s["prep_dve"], n_d[0])

            n_d = [0]
            dve.wait_ge(s["cols_ps"], 1)
            dve.tensor_copy(cols6, pt_ps2[:, 0:6]).then_inc(s["cols_sb"], 1)
            dve.wait_ge(s["cols_sb"], 1)
            dve.tensor_scalar(ab_log[:, :], ab_col, TINY, None, ALU.max).then_inc(s["ab_floor"], 1)
            dve.tensor_scalar(ab_mask[:, :], ab_col, 0.0, None, ALU.is_gt).then_inc(s["ab_mask_s"], 1)
            dve.wait_ge(s["consts"], N_CONST_EARLY)
            for c in range(2):
                dve.tensor_scalar(bq_blk[:, c, :], head_mask[:, :], bias_qk[:, c:c + 1], None, ALU.mult)\
                    .then_inc(s["bq_s"], 1)
            dve.wait_ge(s["ctxT_ps"], 1)
            for k in range(KD):
                dve.tensor_copy(ctxD[:, k],
                                bk6[:, k * P:(k + 1) * P].rearrange("p (b s) -> p b s", b=B)[:, :, None, :]
                                .broadcast_to([P, B, 2, S2])).then_inc(s["ctx_sb"], 1)
            dve.wait_ge(s["gT_ps"], 1)
            dve.tensor_copy(gateT[:, :, :], bk7[:, 0:KD * E].rearrange("p (k e) -> p k e", k=KD)).then_inc(s["gT_sb"], 1)
            for c in range(2):
                dve.wait_ge(s["kT_ps"], c + 1)
                dve.tensor_scalar(kT[:, c].rearrange("p b r s -> p (b r s)"), sc_ps[1][:, c * 512:c * 512 + B * P],
                                  bias_qk[:, 2 + c:3 + c], HD ** -0.5, ALU.add, ALU.mult).then_inc(s["kT_sb"], 1)
            dve.wait_ge(s["kT_sb"], 2)
            dve.tensor_copy(kT_hi, kT[:, :, :, 0, :]).then_inc(s["kT16"], 1)
            dve.wait_ge(s["kT16"], 1)
            dve.tensor_tensor(kT_lo, kT[:, :, :, 0, :], kT_hi, ALU.subtract).then_inc(s["kT16"], 1)
            dve.wait_ge(s["kT16"], 2)
            for c in range(2):
                for dst, src in ((kb_hi, kT_hi), (kb_lo, kT_lo)):
                    dve.tensor_tensor(dst[:, c, 0, :].rearrange("p (h s) -> p h s", h=8),
                                      src[:, c, 0:1, :].broadcast_to([P, 8, S2]),
                                      head_mask[:, :, None].broadcast_to([P, 8, S2]), ALU.mult).then_inc(s["kb_dve"], 1)
            dve.wait_ge(s["wq_hi_s"], 1)
            dve.tensor_tensor(wq_lo, sc_ps[0][:, 0:KD * D].rearrange("p (k n) -> p k n", k=KD), wq_hi, ALU.subtract)\
                .then_inc(s["wq_lo_s"], 1)

            dve.wait_ge(s["bias_ps"], 1)
            dve.wait_ge(s["ab_log_s"], 1)
            link(dve.tensor_tensor(bias_sum.rearrange("p (b n) -> p b n", b=B),
                                   bk6[:, 0:B * H].rearrange("p (b n) -> p b n", b=B),
                                   ab_log[:, :, None].broadcast_to([P, B, H]), ALU.add))
            link(dve.tensor_copy(bias16, bias_sum))
            link(dve.scalar_tensor_tensor(out=bias_rest, in0=bias16, scalar=low_rows[:, 0:1], in1=bias_sum,
                                          op0=ALU.mult, op1=ALU.add))
            dve.tensor_copy(bias16, bias_rest).then_inc(s["bias_parts"], 1)

            def first_stats(tt):
                if tt < B:
                    dve.wait_ge(s[f"x_load{tt}"], 16)
                dve.bn_stats(st_all[:, tt, :], xs[:, tt, :]).then_inc(s["ln1_stats"], 1)

            def first_moments(a, b):
                dve.wait_ge(s["ln1_stats"], b)
                for tt in range(a, b):
                    dve.bn_aggr(mv_all[:, tt, :], st_all[:, tt, :]).then_inc(s["ln1_mv"], 1)

            for tt in range(FIRST):
                first_stats(tt)

            def tile(t, tt):
                return xs[:, tt, :] if t is not None else xs[:, bass.ds(tt, 1), :].rearrange("p u d -> p (u d)")

            first_moments(0, FIRST)
            dve.wait_ge(s["ln1_mv"], FIRST)
            rsqrt(dve, rs_all[:, 0:FIRST], mv_all[:, 0:FIRST, 1], rsw[:, 0:FIRST], rsw[:, FIRST:2 * FIRST],
                  rsw[:, 2 * FIRST:3 * FIRST], "ln1_rstd", 0)

            def ln1(t, tt, par):
                at = slice(tt, tt + 1) if t is not None else bass.ds(tt, 1)
                dve.tensor_scalar(xn[par][:, :], tile(t, tt), mv_all[:, at, 0], rs_all[:, at], ALU.subtract, ALU.mult)\
                    .then_inc(s["xn_ready"], 1)

            ln1(0, 0, 0)
            ln1(1, 1, 1)

            def queries_low(tt, par):
                dve.wait_ge(s["q_hi_s"], tt + 1)
                dve.tensor_tensor(qT_lo[par], bk7[:, 0:2 * P], qT_hi[par], ALU.subtract)\
                    .then_inc(s["q_lo_s"], 1)

            def tokens_low(tt):
                dve.wait_ge(s["xt_hi"], tt + 1)
                dve.tensor_tensor(xT_lo, bk6[:, 0:KD * P], xT_hi, ALU.subtract)\
                    .then_inc(s["xt_lo"], 1)

            tokens_low(0)
            queries_low(0, 0)
            for tt in range(FIRST, FIRST + 4):
                first_stats(tt)

            n_r = [0]

            def rlink(ins):
                n_r[0] += 1
                ins.then_inc(s["route"], 1)
                dve.wait_ge(s["route"], n_r[0])

            score, ex, biased, rank_e, pos = r_small

            def gate_shift(a, b):
                dve.wait_ge(s["logit_sb"], b)
                rlink(dve.tensor_reduce(t_max[:, a:b], logits[:, a:b, :], AX.X, ALU.max))
                dve.tensor_tensor(ex[:, a:b, :], logits[:, a:b, :], t_max[:, a:b, None].broadcast_to([P, b - a, E]),
                                  ALU.subtract).then_inc(s["exp_in"], 1)

            def gate_scores(a, b, group):
                dve.wait_ge(s["exp_out"], group)
                rlink(dve.tensor_reduce(t_sum[:, a:b], ex[:, a:b, :], AX.X, ALU.add))
                rlink(dve.reciprocal(t_sum[:, a:b], t_sum[:, a:b]))
                dve.tensor_tensor(score[:, a:b, :], ex[:, a:b, :], t_sum[:, a:b, None].broadcast_to([P, b - a, E]),
                                  ALU.mult).then_inc(s["scores_in"], 1)
                dve.wait_ge(s["scores_in"], group)
                dve.wait_ge(s["eb_load"], 16)
                rlink(dve.tensor_tensor(biased[:, a:b, :], score[:, a:b, :], ebias[:, None, :].broadcast_to([P, b - a, E]),
                                        ALU.add))

            def beaten(a, b):
                shape = [P, b - a, E, E]
                rlink(dve.tensor_tensor(rank_w[:, a:b], biased[:, a:b, None, :].broadcast_to(shape),
                                        biased[:, a:b, :, None].broadcast_to(shape), ALU.subtract))
                rlink(dve.tensor_tensor(rank_w[:, a:b], rank_w[:, a:b], tie[:, None, :, :].broadcast_to(shape),
                                        ALU.is_gt))

            def ranks(a, b):
                rlink(dve.tensor_reduce(rank_e[:, a:b, :], rank_w[:, a:b], AX.X, ALU.add))
                dve.tensor_scalar(sel16[:, a:b, :], rank_e[:, a:b, :], float(TOPK), None, ALU.is_lt)\
                    .then_inc(s["selected"], 1)

            def step(u, par, t):
                tt = 2 * u + par
                sv = sc_ps[par][:, :].rearrange("p (h n) -> p h n", h=H)
                ov = bk7[:, 0:H * NOUT].rearrange("p (h n) -> p h n", h=H)

                def maxima(c):
                    dve.wait_ge(s["s_ps"], 2 * tt + c + 1)
                    hh = slice(c * H // 2, (c + 1) * H // 2)
                    dve.tensor_reduce(top[:, hh], sv[:, hh, :], AX.X, ALU.max).then_inc(s["smax"], 1)

                if here(t, 3):
                    dve.wait_ge(s["ln2_stats"], tt - 2)
                    carry(dve)
                    dve.bn_aggr(mv2[:, :], st2[:, :]).then_inc(s["ln2_mv"], 1)
                if t == T + 2:
                    gate_scores(0, EARLY, 1)
                    beaten(0, EARLY)
                if here(t, 0):
                    if t is None or t >= 1:
                        dve.wait_ge(s["ssub"], tt)
                    maxima(0)
                if here(t, 2):
                    dve.wait_ge(s["o_ps"], tt - 1)
                    dve.reciprocal(o_inv[:, :], ov[:, :, HD:NOUT].rearrange("p h n -> p (h n)")).then_inc(s["o_recip"], 1)
                if t in (0, 1):
                    for n in range(8 + 4 * t, 12 + 4 * t):
                        first_stats(n)
                if t == 1:
                    first_moments(FIRST, T)
                if here(t, 2):
                    bt = tt - 2
                    dve.wait_ge(s["o_recip"], bt + 1)
                    if t is None or bt >= 1:
                        dve.wait_ge(s["ot_ps"], bt)
                    dve.tensor_tensor(o_sb[:, :].rearrange("p (h n) -> p h n", h=H), ov[:, :, 0:HD],
                                      o_inv[:, :, None].broadcast_to([P, H, HD]), ALU.mult).then_inc(s["o_norm"], 1)
                if here(t, -1):
                    tokens_low(tt + 1)
                if t == 1:
                    dve.wait_ge(s["bo_load"], 16)
                    link(dve.tensor_copy(bo16[:, :], bo_all))
                    link(dve.scalar_tensor_tensor(out=bo_rest, in0=bo16[:, :], scalar=low_rows[:, 0:1], in1=bo_all,
                                                  op0=ALU.mult, op1=ALU.add))
                    dve.tensor_copy(bo16[:, :], bo_rest).then_inc(s["bo_s"], 1)
                if here(t, 0):
                    maxima(1)
                    dve.wait_ge(s["smax"], 2 * (tt + 1))
                    if t is None or t >= 2:
                        dve.wait_ge(s["pt_ps"], 2 * (tt - 1))
                    dve.tensor_tensor(prob[par].rearrange("p (h n) -> p h n", h=H), sv,
                                      top[:, :, None].broadcast_to([P, H, S2]), ALU.subtract).then_inc(s["ssub"], 1)
                if here(t, -1):
                    queries_low(tt + 1, 1 - par)
                if t == 2:
                    dve.wait_ge(s["ln1_rstd_b"], RSQRT_OPS)
                if here(t, -2):
                    dve.wait_ge(s["xt_ps"], tt + 1)
                    ln1(t, tt + 2, par)
                if here(t, 3):
                    bu, bp = back(u, par, 3)
                    bt = tt - 3
                    dve.wait_ge(s["ln2_rstd"], (bt + 1) * RSQRT_OPS)
                    if t is None or bt >= 2:
                        dve.wait_ge(xn2_st[bp], 16 * bu)
                        dve.wait_ge(s["x2t_ps"], bt - 1)
                    dve.tensor_scalar(xn2[bp][:, :], tile(t, bt), mv2[:, 0:1], rs2[:, 0:1], ALU.subtract, ALU.mult)\
                        .then_inc(s["xn2_ready"], 1)
                if t == T + 3:
                    ranks(0, EARLY)
                if here(t, 4):
                    bt = tt - 4
                    dve.wait_ge(s["logit_ps"], bt + 1)
                    if here(t, 2):
                        dve.wait_ge(s["attn_ps"], tt - 1)
                    lo = logits[:, bt, :] if t is not None else logits[:, bass.ds(bt, 1), :].rearrange("p u e -> p (u e)")
                    dve.tensor_copy(lo, bk6[:, 0:E]).then_inc(s["logit_sb"], 1)
                if t == T + 1:
                    gate_shift(0, EARLY)
                if here(t, 2):
                    bt = tt - 2
                    dve.wait_ge(s["attn_ps"], bt + 1)
                    xt = tile(t, bt)
                    dve.tensor_tensor(xt, bk6[:, KD * P:2 * KD * P], xt, ALU.add).then_inc(s["x2_ready"], 1)
                    dve.wait_ge(s["x2_ready"], bt + 1)
                    if t is None or bt >= 1:
                        dve.wait_ge(s["ln2_mv"], bt)
                    carry(dve)
                    dve.bn_stats(st2[:, :], xt).then_inc(s["ln2_stats"], 1)

            attention_steps(dve, step)

            gate_shift(EARLY, T)
            gate_scores(EARLY, T, 2)
            beaten(EARLY, T)
            ranks(EARLY, T)
            dve.wait_ge(x2_st[0], 16 * UT)
            dve.wait_ge(x2_st[1], 16 * UT)
            for k in range(TOPK):
                rlink(dve.tensor_scalar(chosen[:, :, k, :], rank_e, float(k), None, ALU.is_equal))
            dve.wait_ge(s["prefix_ps"], 1)
            rlink(dve.tensor_tensor(count_w[:, :, :], bk7[:, 0:E, None].broadcast_to([P, E, T]), tile_edge[:, :, :],
                                    ALU.is_gt))
            rlink(dve.tensor_reduce(n_tiles[:, :], count_w[:, :, :], AX.X, ALU.add))
            rlink(dve.tensor_tensor(ee_w[:, :, :], lower[:, :, :], n_tiles[:, None, :].broadcast_to([P, E, E]), ALU.mult))
            rlink(dve.tensor_reduce(first_tile[:, :], ee_w[:, :, :], AX.X, ALU.add))
            rlink(dve.tensor_tensor(last_tile[:, :], first_tile[:, :], n_tiles[:, :], ALU.add))
            rlink(dve.tensor_scalar(first_tile[:, :], first_tile[:, :], float(P), None, ALU.mult))
            rlink(dve.tensor_tensor(pos, bk6[:, 0:T * E].rearrange("p (t e) -> p t e", t=T),
                                    first_tile[:, None, :].broadcast_to([P, T, E]), ALU.add))
            rlink(dve.tensor_tensor(pick, chosen, pos[:, :, None, :].broadcast_to([P, T, TOPK, E]), ALU.mult))
            rlink(dve.tensor_reduce(pos_k[:, :, :], pick, AX.X, ALU.add))
            rlink(dve.tensor_copy(pos_i[:, :, :], pos_k[:, :, :]))
            rlink(dve.tensor_scalar(pos_i[:, :, :], pos_i[:, :, :], 7, None, ALU.logical_shift_right))
            rlink(dve.tensor_copy(pos_a[:, :, :], pos_i[:, :, :]))
            rlink(dve.scalar_tensor_tensor(out=pos_b[:, :, :], in0=pos_a[:, :, :], scalar=-float(P), in1=pos_k[:, :, :],
                                           op0=ALU.mult, op1=ALU.add))
            NP = T * TOPK
            pa = pos_a[:, :, :].rearrange("p t k -> p (t k)")
            pb = pos_b[:, :, :].rearrange("p t k -> p (t k)")

            def one_hot_b(i):
                nn = slice(i * NP // 2, (i + 1) * NP // 2)
                dve.tensor_tensor(oneh_b[:, nn, :], iota_p[:, None, :].broadcast_to([P, NP // 2, P]),
                                  pb[:, nn, None].broadcast_to([P, NP // 2, P]), ALU.is_equal).then_inc(s["oneh_ready"], 1)

            rlink(dve.tensor_tensor(oneh_a, iota_p[:, None, 0:J].broadcast_to([P, NP, J]),
                                    pa[:, :, None].broadcast_to([P, NP, J]), ALU.is_equal))
            dve.tensor_tensor(val_a[:, :, 0:J].rearrange("p (t k) j -> p t k j", k=TOPK),
                              oneh_a.rearrange("p (t k) j -> p t k j", k=TOPK),
                              tok_id[:, :, None, None].broadcast_to([P, T, TOPK, J]), ALU.mult)\
                .then_inc(s["oneh_ready"], 1)
            one_hot_b(0)
            one_hot_b(1)
            rlink(dve.tensor_tensor(tile_cmp[:, :, :], iota_p[:, 0:J, None].broadcast_to([P, J, E]),
                                    last_tile[:, None, :].broadcast_to([P, J, E]), ALU.is_ge))
            rlink(dve.tensor_reduce(tile_exp[:, :], tile_cmp[:, :, :], AX.X, ALU.add))
            dve.wait_ge(s["slots_ps"], 1)
            rlink(dve.tensor_copy(slot_tok[:, :], bk7[:, 64:64 + J]))
            dve.tensor_scalar(idx_get[:, :], slot_tok[:, :], -1.0, 0.0, ALU.add, ALU.max).then_inc(s["get_ready"], 1)
            rlink(dve.tensor_scalar(slot_pad[:, :], slot_tok[:, :], 0.0, pad_row[:, 0:1], ALU.is_equal, ALU.mult))
            dve.scalar_tensor_tensor(out=idx_put[:, :], in0=slot_tok[:, :], scalar=-1.0, in1=slot_pad[:, :],
                                     op0=ALU.add, op1=ALU.add).then_inc(s["put_ready"], 1)
            rlink(dve.tensor_scalar(tile_exp[:, :], tile_exp[:, :], float(E - 1), None, ALU.min))
            rlink(dve.tensor_tensor(tile_oh[:, :, :], iota_p[:, None, 0:E].broadcast_to([P, J, E]),
                                    tile_exp[:, :, None].broadcast_to([P, J, E]), ALU.is_equal))
            dve.tensor_scalar(tile_off[:, :], tile_exp[:, :], float(WE), None, ALU.mult).then_inc(s["experts_ready"], 1)
            dve.wait_ge(s["put_ready"], 1)
            dve.wait_ge(s["experts_ready"], 1)

            def slots(j, par):
                static = isinstance(j, int)
                dve.wait_ge(gathered[par], 16 * ((j - par) // 2 + 1) if static else 8 * (j - par) + 16)
                oh = tile_oh[:, j, :] if static else tile_oh[:, bass.ds(j, 1), :].rearrange("p u e -> p (u e)")
                if not static or j >= 1:
                    dve.wait_ge(s["sc_ready"], j)
                dve.tensor_tensor(score_w[:, :], gx[par][:, D:XR], oh, ALU.mult).then_inc(s["sc_tmp"], 1)
                dve.wait_ge(s["sc_tmp"], j + 1)
                dve.tensor_reduce(slot_score[par][:, :], score_w[:, :], AX.X, ALU.add).then_inc(s["sc_ready"], 1)
                dve.wait_ge(s["gt_hi"], j + 1)
                dve.tensor_tensor(gT_lo[par], bk6[:, 0:KD * P], gT_hi[par], ALU.subtract).then_inc(s["gt_lo"], 1)

            slots(0, 0)

            def step(j, par):
                static = isinstance(j, int)
                if not static or j < J:
                    for a, b, at in ((0, FH, 0), (FH, F, FH), (LC, F, F)):
                        c = a // FH
                        dve.wait_ge(s["silu_done"], 2 * j + c + 1)
                        dve.scalar_tensor_tensor(out=hid[par][:, at:at + b - a], in0=h3_ps[:, c, a - c * FH:b - c * FH],
                                                 scalar=slot_score[par][:, 0:1], in1=sil[par][:, a:b],
                                                 op0=ALU.mult, op1=ALU.mult).then_inc(s["h_ready"], 1)
                    if not static or j + 1 < J:
                        slots(j + 1, 1 - par)
                if not static or j >= 1:
                    q = 1 - par
                    dve.wait_ge(s["y_ps"], j)
                    if not static or j >= 3:
                        dve.wait_ge(s["put_done"], 16 * (j - 2))
                    dve.tensor_copy(y_sb[q], bk7[:, 0:D]).then_inc(s["y_ready"], 1)
                if not static or j < J:
                    dve.wait_ge(s["ht_hi"], j + 1)
                    dve.tensor_tensor(hT_lo[par], hT_ps[:, 0:LC], hT_hi[par][:, 0:LC], ALU.subtract).then_inc(s["ht_lo"], 1)
                    dve.tensor_tensor(hT_hi[par][FL:P, LC:KF * P], hT_ps[FL:P, LC:KF * P], hT_hi[par][FL:P, LC:KF * P],
                                      ALU.subtract).then_inc(s["ht_lo"], 1)

            expert_steps(dve, step)

        @block.tensor
        def _(pe):
            pe.wait_ge(s["consts"], N_CONST_EARLY)
            idt = ident[:, :]
            pe.wait_ge(s["row_loads"], 16 * ROW_DMAS)
            pe.transpose(pt_ps2[:, 0:6], rows6, ident[0:6, 0:6]).then_inc(s["cols_ps"], 1)
            pe.wait_ge(s["ctx_load"], 16)
            for k in range(KD):
                ins = pe.transpose(bk6[:, k * P:(k + 1) * P], ctx_n[:, k * P:(k + 1) * P], idt)
            ins.then_inc(s["ctxT_ps"], 1)
            pe.wait_ge(s["wkv_load"], 16)
            for i, done in enumerate(("wkT_ps", "wvT_ps")):
                for k in range(KD):
                    for r in range(2):
                        ins = pe.transpose(sc_ps[0][:, i * 512 + k * D + r * P:i * 512 + k * D + (r + 1) * P],
                                           prep[:, 2 + 2 * i + r, k * P:(k + 1) * P], idt)
                ins.then_inc(s[done], 1)
            for k in range(KD):
                ins = pe.transpose(bk7[:, k * E:(k + 1) * E], gate_n[:, k * P:(k + 1) * P], ident[0:E, 0:E])
            ins.then_inc(s["gT_ps"], 1)
            pe.wait_ge(s["ctx_sb"], KD)
            pe.wait_ge(s["wkT_sb"], 1)
            for c in range(2):
                for k in range(KD):
                    ins = pe.matmul(sc_ps[1][:, c * 512:c * 512 + B * P], wkT[:, k, c * P:(c + 1) * P],
                                    ctxD[:, k].rearrange("p b r s -> p (b r s)"), start=k == 0, stop=k == KD - 1)
                ins.then_inc(s["kT_ps"], 1)
            pe.wait_ge(s["wq_load"], 16)
            for k in range(KD):
                for r in range(2):
                    ins = pe.transpose(sc_ps[0][:, k * D + r * P:k * D + (r + 1) * P], prep[:, r, k * P:(k + 1) * P], idt)
            ins.then_inc(s["wqT_ps"], 1)
            pe.wait_ge(s["wo_load"], 16)
            pe.wait_ge(s["cols_sb"], 1)
            for k in range(KD):
                for r in range(2):
                    ins = pe.transpose(pt_ps2[:, k * D + r * P:k * D + (r + 1) * P], wo_n[:, r, k * P:(k + 1) * P], idt)
            ins.then_inc(s["woT_ps"], 1)
            pe.wait_ge(s["gT_sb"], 1)
            pe.wait_ge(s["wvT_sb"], 1)
            for b in range(B):
                for k in range(KD):
                    pe.matmul(v_bank(b), ctxD[:, k, b].rearrange("p r s -> p (r s)"), wvT[:, k, :], start=k == 0,
                              stop=False)
                pe.matmul(v_bank(b), ones_row[:, :], bv_row[:, :], start=False, stop=True).then_inc(s["v_ps"], 1)
            pe.wait_ge(s["kT_sb"], 2)
            pe.wait_ge(s["bq_s"], 2)
            for b in range(B):
                for c in range(2):
                    ins = pe.matmul(bk6[:, b * H + c * 8:b * H + (c + 1) * 8], kT[:, c, b].rearrange("p r s -> p (r s)"),
                                    bq_blk[:, c, :], start=True, stop=True)
            ins.then_inc(s["bias_ps"], 1)

            def x_transpose(tt, par):
                pe.wait_ge(s["xn_ready"], tt + 1)
                if not isinstance(tt, int) or tt >= 1:
                    pe.wait_ge(s["xt_lo"], tt)
                for k in range(KD):
                    ins = pe.transpose(bk6[:, k * P:(k + 1) * P], xn[par][:, k * P:(k + 1) * P], idt)
                ins.then_inc(s["xt_ps"], 1)

            def queries(tt):
                pe.wait_ge(s["xt_lo"], tt + 1)
                for c in range(2):
                    o = bk7[:, c * P:(c + 1) * P]
                    cc = slice(c * P, (c + 1) * P)
                    for k in range(KD):
                        kk = slice(k * P, (k + 1) * P)
                        pe.matmul(o, wq_hi[:, k, cc], xT_hi[:, kk], start=k == 0, stop=False)
                        pe.matmul(o, wq_hi[:, k, cc], xT_lo[:, kk], start=False, stop=False)
                        ins = pe.matmul(o, wq_lo[:, k, cc], xT_hi[:, kk], start=False, stop=k == KD - 1)
                ins.then_inc(s["q_ps"], 1)

            def scores_half(par, c):
                o = sc_ps[par][:, c * HS:(c + 1) * HS]
                cc = slice(c * P, (c + 1) * P)
                pe.matmul(o, qT_hi[par][:, cc], kb_hi[:, c, par, :], start=True, stop=False)
                pe.matmul(o, qT_hi[par][:, cc], kb_lo[:, c, par, :], start=False, stop=False)
                pe.matmul(o, qT_lo[par][:, cc], kb_hi[:, c, par, :], start=False, stop=False)
                return pe.matmul(o, ones16[:, :], beta[:, par, c * HS:(c + 1) * HS], start=False, stop=True)

            pe.wait_ge(s["bias_parts"], 1)
            x_transpose(0, 0)
            pe.wait_ge(s["wq_lo_s"], 1)
            pe.wait_ge(s["v_sb"], 2 * B)
            queries(0)

            def step(u, par, t):
                tt = 2 * u + par
                if here(t, 0):
                    pe.wait_ge(s["q_lo_s"], tt + 1)
                    if t is None or t >= 2:
                        pe.wait_ge(s["ssub"], tt - 1)
                    elif t == 0:
                        pe.wait_ge(s["kb_dve"], 4)
                        pe.wait_ge(s["beta_s"], 1)
                    elif t == 1:
                        pe.wait_ge(s["kb_pool"], 4)
                        pe.wait_ge(s["beta_s"], 2)
                    scores_half(par, 0).then_inc(s["s_ps"], 1)
                if here(t, 2):
                    bt = tt - 2
                    pe.wait_ge(s["pt_sb"], 2 * (bt + 1))
                    if t is None or bt >= 1:
                        pe.wait_ge(s["o_norm"], bt)
                    else:
                        pe.wait_ge(s["v_sb"], 4 * B)
                    if here(t, 0):
                        pe.wait_ge(s["q_lo_s"], tt + 1)
                    for j in range(8):
                        ins = pe.matmul(bk7[:, j * 2 * NOUT:(j + 1) * 2 * NOUT], probT[par][:, j * P:(j + 1) * P],
                                        v_blk[:, par, j, :], start=True, stop=True)
                    ins.then_inc(s["o_ps"], 1)
                if here(t, -1):
                    if t is None or t >= 3:
                        pe.wait_ge(s["x2_ready"], tt - 2)
                    if t is None or t >= 5:
                        pe.wait_ge(s["logit_sb"], tt - 4)
                    x_transpose(tt + 1, 1 - par)
                if here(t, 4):
                    bt = tt - 4
                    pe.wait_ge(s["xn2_ready"], bt + 1)
                    if t is None or bt >= 1:
                        pe.wait_ge(s["x2t_sb"], bt)
                    for k in range(KD):
                        ins = pe.transpose(pt_ps2[:, k * P:(k + 1) * P], xn2[par][:, k * P:(k + 1) * P], idt)
                    ins.then_inc(s["x2t_ps"], 1)
                if here(t, 0):
                    scores_half(par, 1).then_inc(s["s_ps"], 1)
                if here(t, 2):
                    bt = tt - 2
                    pe.wait_ge(s["o_norm"], bt + 1)
                    if t is None or bt >= 1:
                        pe.wait_ge(s["x2_ready"], bt)
                    if here(t, -1):
                        pe.wait_ge(s["xt_lo"], tt + 2)
                    for k in range(KD):
                        ins = pe.transpose(bk6[:, (KD + k) * P:(KD + k + 1) * P], o_sb[:, k * P:(k + 1) * P], idt)
                    ins.then_inc(s["ot_ps"], 1)
                if here(t, -1):
                    queries(tt + 1)
                if here(t, 1):
                    bt = tt - 1
                    pe.wait_ge(s["p_exp"], bt + 1)
                    for c in range(2):
                        if t is None or bt >= 1:
                            pe.wait_ge(s["pt_sb"], 2 * bt)
                        if c == 0 and (t is None or bt >= 3):
                            pe.wait_ge(s["x2t_sb"], bt - 2)
                        for q in range(4):
                            j = 4 * c + q
                            ins = pe.transpose(pt_ps2[:, j * P:(j + 1) * P], prob[1 - par][:, j * P:(j + 1) * P], idt)
                        ins.then_inc(s["pt_ps"], 1)
                if here(t, 4):
                    bt = tt - 4
                    pe.wait_ge(s["x2t_sb"], bt + 1)
                    if here(t, 2):
                        pe.wait_ge(s["ot_sb"], tt - 1)
                    else:
                        pe.wait_ge(s["x2_ready"], T)
                    if t is None or bt >= 1:
                        pe.wait_ge(s["logit_sb"], bt)
                    for k in range(KD):
                        ins = pe.matmul(bk6[:, 0:E], xn2T[:, k * P:(k + 1) * P], gateT[:, k, :],
                                        start=k == 0, stop=k == KD - 1)
                    ins.then_inc(s["logit_ps"], 1)
                if here(t, 2):
                    bt = tt - 2
                    pe.wait_ge(s["ot_sb"], bt + 1)
                    if t == 2:
                        pe.wait_ge(s["bo_s"], 1)
                    o = bk6[:, KD * P:2 * KD * P]
                    for k in range(KD):
                        pe.matmul(o, oT[:, k * P:(k + 1) * P], woT[:, k, :], start=k == 0, stop=False)
                    pe.matmul(o, shares16[:, :], bo16[:, :], start=False, stop=True).then_inc(s["attn_ps"], 1)

            attention_steps(pe, step)

            pe.wait_ge(s["selected"], 2)
            def earlier_partitions(start):
                ins = pe.matmul(bk6[:, 0:T * E], before_half[:, :], sel16[:, :, :].rearrange("p t e -> p (t e)"),
                                start=start, stop=not start, skip_group_check=True)
                return ins

            earlier_partitions(True)
            for t in range(T - 1):
                pe.matmul(bk6[:, (t + 1) * E:T * E].rearrange("p (t e) -> p t e", e=E), ones16[:, :],
                          sel16[:, t:t + 1, :].broadcast_to([P, T - 1 - t, E]), start=False, stop=False,
                          skip_group_check=True)
            earlier_partitions(False)
            for t in range(T):
                ins = pe.matmul(bk7[:, 0:E], ones16[:, :], sel16[:, t, :], start=t == 0, stop=t == T - 1)
            ins.then_inc(s["prefix_ps"], 1)
            for n in range(T * TOPK):
                if n % T == 0:
                    pe.wait_ge(s["oneh_ready"], 2 + n // T)
                ins = pe.matmul(bk7[:, 64:64 + J], oneh_b[:, n, :], val_a[:, n, 0:J], start=n == 0,
                                stop=n == T * TOPK - 1)
            ins.then_inc(s["slots_ps"], 1)
            pe.wait_ge(s["experts_ready"], 1)
            pe.wait_ge(s["wlo"], len(PIECES))

            def x_rows(j, par, j1):
                pe.wait_ge(gathered[par], j1)
                if not isinstance(j, int) or j >= 1:
                    pe.wait_ge(s["gt_lo"], j)
                for k in range(KD):
                    ins = pe.transpose(bk6[:, k * P:(k + 1) * P], gx[par][:, k * P:(k + 1) * P], idt)
                ins.then_inc(s["gt_ps"], 1)

            x_rows(0, 0, 16)

            def step(j, par):
                static = isinstance(j, int)
                q = 1 - par
                if not static or j < J:
                    col = slice(j, j + 1) if static else bass.ds(j, 1)
                    w_at = pe.value_load(tile_off[0:1, col], min_val=0, max_val=(E - 1) * WE)
                if not static or j >= 1:
                    pe.wait_ge(s["h_ready"], 3 * j)
                    if not static or j >= 2:
                        pe.wait_ge(s["ht_lo"], 2 * (j - 1))
                    for c in range(KF):
                        ins = pe.transpose(hT_ps[:, c * P:(c + 1) * P], hid[q][:, c * P:(c + 1) * P], idt)
                    ins.then_inc(s["ht_ps"], 1)
                if not static or j < J:
                    pe.wait_ge(s["gt_lo"], j + 1)
                    for c in range(2):
                        for ps, half in ((h1_ps, 0), (h3_ps, 1)):
                            for k in range(KD):
                                kk = slice(k * P, (k + 1) * P)
                                cols = bass.ds(w_at + (half * HALF + k * F + c * FH), FH)
                                pe.matmul(ps[:, c, :], gT_hi[par][:, kk], w_hi[:, cols], start=k == 0, stop=False)
                                pe.matmul(ps[:, c, :], gT_lo[par][:, kk], w_hi[:, cols], start=False, stop=False)
                                ins = pe.matmul(ps[:, c, :], gT_hi[par][:, kk], w_lo[:, cols], start=False,
                                                stop=k == KD - 1)
                        ins.then_inc(s["h_ps"], 1)
                if not static or j + 1 < J:
                    x_rows(j + 1, q, 16 * ((j + 1 - q) // 2 + 1) if static else 8 * (j + 1 - q) + 16)
                if not static or j >= 1:
                    colp = slice(j - 1, j) if static else bass.ds(j - 1, 1)
                    w_before = pe.value_load(tile_off[0:1, colp], min_val=0, max_val=(E - 1) * WE)
                    pe.wait_ge(s["ht_lo"], 2 * j)
                    if not static or j >= 2:
                        pe.wait_ge(s["y_ready"], j - 1)
                    for c in range(KF):
                        off = W13 + c * D if c < KF // 2 else HALF + W13 + (c - KF // 2) * D
                        cc = slice(c * P, (c + 1) * P)
                        cols = bass.ds(w_before + off, D)
                        pe.matmul(bk7[:, 0:D], hT_hi[q][:, cc], w_hi[:, cols], start=c == 0, stop=False)
                        if c < KF - 1:
                            pe.matmul(bk7[:, 0:D], hT_lo[q][:, cc], w_hi[:, cols], start=False, stop=False)
                        rows = P if c < KF - 1 else FL
                        ins = pe.matmul(bk7[:, 0:D], hT_hi[q][0:rows, cc], w_lo[0:rows, cols], start=False,
                                        stop=c == KF - 1)
                    ins.then_inc(s["y_ps"], 1)

            expert_steps(pe, step)


N_CONST = 26
N_CONST_EARLY = 17
RSQRT_OPS = 12
ROW_DMAS = 5

_INS = ["x", "ctx_1024", "fside_BxS2_0", "L0_xattn_in_proj_weight", "L0_xattn_in_proj_bias",
        "L0_xattn_out_proj_weight", "L0_xattn_out_proj_bias", "L0_ffn_gate_w", "L0_ffn_expert_bias",
        "L0_ffn_w1", "L0_ffn_w2", "L0_ffn_w3"]


def kernel(**inputs):
    import numpy as _np
    import concourse.bacc as _bacc
    from concourse import mybir as _mybir
    from concourse.bass_utils import run_bass_kernel_spmd as _run

    nc = _bacc.Bacc("TRN2", target_bir_lowering=False, num_devices=1)
    arrays, args = {}, []
    for name in _INS:
        a = _np.ascontiguousarray(inputs[name])
        arrays[f"in_{name}"] = a
        args.append(nc.dram_tensor(f"in_{name}", a.shape, _mybir.dt.from_np(a.dtype), kind="ExternalInput").ap())
    shape = inputs["x"].shape
    args.append(nc.dram_tensor("out_0", shape, _mybir.dt.float32, kind="ExternalOutput").ap())
    xattn_moe(nc, *args)
    r = _run(nc, [arrays], core_ids=[0])
    return r.results[0]["out_0"]
```
